# Optimizing a Trainium2 kernel written in Bass

```python
import numpy as np
import jax
import jax.numpy as jnp

def _softmax(x, axis=-1):
    return jax.nn.softmax(x, axis=axis)

def _gelu(x):
    return jax.nn.gelu(x, approximate=True)

def _silu(x):
    return jax.nn.silu(x)

def _sigmoid(x):
    return jax.nn.sigmoid(x)

def _layernorm(x, axis=-1, eps=1e-05):
    m = jnp.mean(x, axis=axis, keepdims=True)
    v = jnp.var(x, axis=axis, keepdims=True)
    return (x - m) / jnp.sqrt(v + eps)

def _scatter_add(tgt, idx, src, axis=0):
    return tgt.at[idx].add(src)

def _segment_sum(src, seg, n):
    return jax.ops.segment_sum(src, seg, n)
kernel_name = 'mk_seq_preln_d2_jaxref_r8_bd11f4'

def setup_inputs(seed: int=0):
    np.random.seed(seed)
    _w = jnp.asarray

    def _L0_attn_setup():
        import jax, jax.numpy as jnp
        import numpy as np
        B, S, D = (2, 256, 256)
        H, G = (16, 4)
        HD = D // H
        KV = HD * G
        key = jax.random.key(seed)
        ks = jax.random.split(key, 5)
        scale = 1.0 / np.sqrt(D)
        return {'x': jax.random.normal(ks[0], (B, S, D), dtype=jnp.float32), 'Wqkv': jax.random.normal(ks[1], (D, D + 2 * KV), dtype=jnp.float32) * scale, 'bqkv': jax.random.normal(ks[2], (D + 2 * KV,), dtype=jnp.float32) * 0.01, 'Wout': jax.random.normal(ks[3], (D, D), dtype=jnp.float32) * scale, 'bout': jax.random.normal(ks[4], (D,), dtype=jnp.float32) * 0.01}
    _L0_attn_in = _L0_attn_setup()

    def _L0_ffn_setup():
        import jax, jax.numpy as jnp
        import numpy as np
        HIDDEN = 256
        NUM_EXPERTS = 32
        TOP_K = 4
        MOE_INTER = 96
        GROUP = 2
        NUM_CHUNK = NUM_EXPERTS // GROUP
        CHUNK_INTER = 128
        SMALL_SCALE = 0.05

        def _routing(x2d, gate_w):
            logits = x2d @ gate_w.T
            rw = jax.nn.softmax(logits.astype(jnp.float32), axis=-1)
            scores = jax.nn.sigmoid(logits.astype(jnp.float32))
            _, sel = jax.lax.top_k(scores, TOP_K)
            w = jnp.take_along_axis(rw, sel, axis=-1)
            w = w / w.sum(axis=-1, keepdims=True)
            return (w.astype(x2d.dtype), sel)

        def _moe(x2d, Wg, Wu, Wd, cw):
            g = jnp.einsum('th,ehi->eti', x2d, Wg)
            u = jnp.einsum('th,ehi->eti', x2d, Wu)
            a = jax.nn.silu(g) * u * cw.T[:, :, None]
            return jnp.einsum('eti,eih->th', a, Wd)
        key = jax.random.key(seed)
        ks = jax.random.split(key, 8)
        s = 0.02
        B, S = (2, 256)
        return {'hidden_states': jax.random.normal(ks[0], (B, S, HIDDEN), jnp.float32), 'gate_w': jax.random.normal(ks[1], (NUM_EXPERTS, HIDDEN), jnp.float32) * s, 'Wg': jax.random.normal(ks[2], (NUM_EXPERTS, HIDDEN, MOE_INTER), jnp.float32) * s, 'Wu': jax.random.normal(ks[3], (NUM_EXPERTS, HIDDEN, MOE_INTER), jnp.float32) * s, 'Wd': jax.random.normal(ks[4], (NUM_EXPERTS, MOE_INTER, HIDDEN), jnp.float32) * s, 'cWg': jax.random.normal(ks[5], (NUM_CHUNK, HIDDEN, CHUNK_INTER), jnp.float32) * s, 'cWu': jax.random.normal(ks[6], (NUM_CHUNK, HIDDEN, CHUNK_INTER), jnp.float32) * s, 'cWd': jax.random.normal(ks[7], (NUM_CHUNK, CHUNK_INTER, HIDDEN), jnp.float32) * s}
    _L0_ffn_in = _L0_ffn_setup()

    def _L1_attn_setup():
        import jax, jax.numpy as jnp
        import numpy as np
        B, L, FUSED, DIM = (4, 72, 256, 256)
        DI, DS, DCONV, DTR = (2 * DIM, 16, 4, 128)

        def _mamba_params(key, prefix):
            ks = jax.random.split(key, 6)
            s_in = 1.0 / np.sqrt(DIM)
            s_di = 1.0 / np.sqrt(DI)
            s_dt = 1.0 / np.sqrt(DTR)
            A_log = jnp.log(jnp.broadcast_to(jnp.arange(1, DS + 1, dtype=jnp.float32), (DI, DS)))
            return {prefix + '_in_w': jax.random.normal(ks[0], (2 * DI, DIM), jnp.float32) * s_in, prefix + '_conv_w': jax.random.normal(ks[1], (DI, DCONV), jnp.float32) * 0.5, prefix + '_conv_b': jnp.zeros((DI,), jnp.float32), prefix + '_xproj_w': jax.random.normal(ks[2], (DTR + 2 * DS, DI), jnp.float32) * s_di, prefix + '_dt_w': jax.random.normal(ks[3], (DI, DTR), jnp.float32) * s_dt, prefix + '_dt_b': jax.random.normal(ks[4], (DI,), jnp.float32) * 0.1 - 4.0, prefix + '_A_log': A_log, prefix + '_D': jnp.ones((DI,), jnp.float32), prefix + '_out_w': jax.random.normal(ks[5], (DIM, DI), jnp.float32) * s_di}

        def _dw_conv(x, w, b):
            xt = jnp.transpose(x, (0, 2, 1))
            xp = jnp.pad(xt, ((0, 0), (0, 0), (DCONV - 1, 0)))
            Ln = xt.shape[-1]
            y = b[None, :, None]
            for kk in range(DCONV):
                y = y + w[:, kk][None, :, None] * xp[:, :, kk:kk + Ln]
            return jnp.transpose(y, (0, 2, 1))

        def _selective_scan(xi, dt, Bm, Cm, A, D):

            def step(h, inp):
                dt_t, B_t, C_t, x_t = inp
                dA = jnp.exp(dt_t[..., None] * A)
                h = dA * h + (dt_t * x_t)[..., None] * B_t[:, None, :]
                y = jnp.einsum('bds,bs->bd', h, C_t)
                return (h, y)
            h0 = jnp.zeros((xi.shape[0], DI, DS), xi.dtype)
            inps = (jnp.swapaxes(dt, 0, 1), jnp.swapaxes(Bm, 0, 1), jnp.swapaxes(Cm, 0, 1), jnp.swapaxes(xi, 0, 1))
            _, ys = jax.lax.scan(step, h0, inps)
            return jnp.swapaxes(ys, 0, 1) + xi * D

        def _mamba(x, in_w, conv_w, conv_b, xproj_w, dt_w, dt_b, A_log, D, out_w):
            xz = jnp.einsum('bld,ed->ble', x, in_w)
            xi, z = jnp.split(xz, 2, axis=-1)
            xi = jax.nn.silu(_dw_conv(xi, conv_w, conv_b))
            xdb = jnp.einsum('bld,ed->ble', xi, xproj_w)
            dtr, Bm, Cm = (xdb[..., :DTR], xdb[..., DTR:DTR + DS], xdb[..., DTR + DS:])
            dt = jax.nn.softplus(jnp.einsum('blr,dr->bld', dtr, dt_w) + dt_b)
            y = _selective_scan(xi, dt, Bm, Cm, -jnp.exp(A_log), D)
            y = y * jax.nn.silu(z)
            return jnp.einsum('bld,ed->ble', y, out_w)

        def _layernorm(x, g, b, eps=1e-05):
            mu = jnp.mean(x, -1, keepdims=True)
            var = jnp.mean(jnp.square(x - mu), -1, keepdims=True)
            return (x - mu) * jax.lax.rsqrt(var + eps) * g + b
        key = jax.random.key(seed)
        k = jax.random.split(key, 8)
        inp = {'img_patches': jax.random.normal(k[0], (B, L, FUSED), jnp.float32), 'w_in': jax.random.normal(k[1], (DIM, FUSED), jnp.float32) / np.sqrt(FUSED), 'b_in': jnp.zeros((DIM,), jnp.float32), 'ln_g': jnp.ones((DIM,), jnp.float32), 'ln_b': jnp.zeros((DIM,), jnp.float32), 'w_out': jax.random.normal(k[2], (DIM, DIM), jnp.float32) / np.sqrt(DIM), 'b_out': jnp.zeros((DIM,), jnp.float32)}
        inp.update(_mamba_params(k[3], 'fm'))
        inp.update(_mamba_params(k[4], 'bm'))
        return inp
    _L1_attn_in = _L1_attn_setup()

    def _L1_ffn_setup():
        import jax, jax.numpy as jnp
        import numpy as np
        HIDDEN = 256
        INTER = 688
        LUT_SIZE = 16

        def _ghost_linear(x, idx, lut):
            w = lut[idx]
            return jnp.einsum('bsh,oh->bso', x, w)
        key = jax.random.key(seed)
        k_x, k_lut, k_g, k_u, k_d = jax.random.split(key, 5)
        x = jax.random.normal(k_x, (2, 512, HIDDEN), dtype=jnp.float32)
        lut = jax.random.normal(k_lut, (LUT_SIZE,), dtype=jnp.float32) * 0.02
        gate_idx = jax.random.randint(k_g, (INTER, HIDDEN), 0, LUT_SIZE, dtype=jnp.int32)
        up_idx = jax.random.randint(k_u, (INTER, HIDDEN), 0, LUT_SIZE, dtype=jnp.int32)
        down_idx = jax.random.randint(k_d, (HIDDEN, INTER), 0, LUT_SIZE, dtype=jnp.int32)
        return {'x': x, 'lut': lut, 'gate_idx': gate_idx, 'up_idx': up_idx, 'down_idx': down_idx}
    _L1_ffn_in = _L1_ffn_setup()
    _d = {'L0_attn_x': _L0_attn_in['x'], 'L0_attn_Wqkv': _L0_attn_in['Wqkv'], 'L0_attn_bqkv': _L0_attn_in['bqkv'], 'L0_attn_Wout': _L0_attn_in['Wout'], 'L0_attn_bout': _L0_attn_in['bout'], 'L0_ffn_gate_w': _L0_ffn_in['gate_w'], 'L0_ffn_Wg': _L0_ffn_in['Wg'], 'L0_ffn_Wu': _L0_ffn_in['Wu'], 'L0_ffn_Wd': _L0_ffn_in['Wd'], 'L0_ffn_cWg': _L0_ffn_in['cWg'], 'L0_ffn_cWu': _L0_ffn_in['cWu'], 'L0_ffn_cWd': _L0_ffn_in['cWd'], 'L1_attn_w_in': _L1_attn_in['w_in'], 'L1_attn_b_in': _L1_attn_in['b_in'], 'L1_attn_fm_in_w': _L1_attn_in['fm_in_w'], 'L1_attn_fm_conv_w': _L1_attn_in['fm_conv_w'], 'L1_attn_fm_conv_b': _L1_attn_in['fm_conv_b'], 'L1_attn_fm_xproj_w': _L1_attn_in['fm_xproj_w'], 'L1_attn_fm_dt_w': _L1_attn_in['fm_dt_w'], 'L1_attn_fm_dt_b': _L1_attn_in['fm_dt_b'], 'L1_attn_fm_A_log': _L1_attn_in['fm_A_log'], 'L1_attn_fm_D': _L1_attn_in['fm_D'], 'L1_attn_fm_out_w': _L1_attn_in['fm_out_w'], 'L1_attn_bm_in_w': _L1_attn_in['bm_in_w'], 'L1_attn_bm_conv_w': _L1_attn_in['bm_conv_w'], 'L1_attn_bm_conv_b': _L1_attn_in['bm_conv_b'], 'L1_attn_bm_xproj_w': _L1_attn_in['bm_xproj_w'], 'L1_attn_bm_dt_w': _L1_attn_in['bm_dt_w'], 'L1_attn_bm_dt_b': _L1_attn_in['bm_dt_b'], 'L1_attn_bm_A_log': _L1_attn_in['bm_A_log'], 'L1_attn_bm_D': _L1_attn_in['bm_D'], 'L1_attn_bm_out_w': _L1_attn_in['bm_out_w'], 'L1_attn_ln_g': _L1_attn_in['ln_g'], 'L1_attn_ln_b': _L1_attn_in['ln_b'], 'L1_attn_w_out': _L1_attn_in['w_out'], 'L1_attn_b_out': _L1_attn_in['b_out'], 'L1_ffn_lut': _L1_ffn_in['lut'], 'L1_ffn_gate_idx': _L1_ffn_in['gate_idx'], 'L1_ffn_up_idx': _L1_ffn_in['up_idx'], 'L1_ffn_down_idx': _L1_ffn_in['down_idx']}
    _x0 = _d['L0_attn_x']
    _d['L0_attn_x'] = jax.random.normal(jax.random.fold_in(jax.random.key(seed), 1), (4, 256, 256), dtype=_x0.dtype)
    del _x0
    return _d

def reference(L0_attn_x, L0_attn_Wqkv, L0_attn_bqkv, L0_attn_Wout, L0_attn_bout, L0_ffn_gate_w, L0_ffn_Wg, L0_ffn_Wu, L0_ffn_Wd, L0_ffn_cWg, L0_ffn_cWu, L0_ffn_cWd, L1_attn_w_in, L1_attn_b_in, L1_attn_fm_in_w, L1_attn_fm_conv_w, L1_attn_fm_conv_b, L1_attn_fm_xproj_w, L1_attn_fm_dt_w, L1_attn_fm_dt_b, L1_attn_fm_A_log, L1_attn_fm_D, L1_attn_fm_out_w, L1_attn_bm_in_w, L1_attn_bm_conv_w, L1_attn_bm_conv_b, L1_attn_bm_xproj_w, L1_attn_bm_dt_w, L1_attn_bm_dt_b, L1_attn_bm_A_log, L1_attn_bm_D, L1_attn_bm_out_w, L1_attn_ln_g, L1_attn_ln_b, L1_attn_w_out, L1_attn_b_out, L1_ffn_lut, L1_ffn_gate_idx, L1_ffn_up_idx, L1_ffn_down_idx):

    def _L0_attn_ref(x, Wqkv, bqkv, Wout, bout):
        import jax, jax.numpy as jnp
        import numpy as np
        B, S, D = (2, 256, 256)
        H, G = (16, 4)
        HD = D // H
        KV = HD * G
        b, s, _ = x.shape
        qkv = x @ Wqkv + bqkv
        q, k, v = jnp.split(qkv, [D, D + KV], axis=-1)
        q = q.reshape(b, s, H, HD)
        k = jnp.tile(k.reshape(b, s, G, HD), (1, 1, H // G, 1))
        v = jnp.tile(v.reshape(b, s, G, HD), (1, 1, H // G, 1))
        scores = jnp.einsum('bqhd,bkhd->bhqk', q, k) / HD
        prob = jax.nn.softmax(scores, axis=-1)
        out = jnp.einsum('bhqk,bkhd->bqhd', prob, v).reshape(b, s, D)
        return out @ Wout + bout

    def _L0_ffn_ref(hidden_states, gate_w, Wg, Wu, Wd, cWg, cWu, cWd):
        import jax, jax.numpy as jnp
        import numpy as np
        HIDDEN = 256
        NUM_EXPERTS = 32
        TOP_K = 4
        MOE_INTER = 96
        GROUP = 2
        NUM_CHUNK = NUM_EXPERTS // GROUP
        CHUNK_INTER = 128
        SMALL_SCALE = 0.05

        def _routing(x2d, gate_w):
            logits = x2d @ gate_w.T
            rw = jax.nn.softmax(logits.astype(jnp.float32), axis=-1)
            scores = jax.nn.sigmoid(logits.astype(jnp.float32))
            _, sel = jax.lax.top_k(scores, TOP_K)
            w = jnp.take_along_axis(rw, sel, axis=-1)
            w = w / w.sum(axis=-1, keepdims=True)
            return (w.astype(x2d.dtype), sel)

        def _moe(x2d, Wg, Wu, Wd, cw):
            g = jnp.einsum('th,ehi->eti', x2d, Wg)
            u = jnp.einsum('th,ehi->eti', x2d, Wu)
            a = jax.nn.silu(g) * u * cw.T[:, :, None]
            return jnp.einsum('eti,eih->th', a, Wd)
        B, S, H = hidden_states.shape
        T = B * S
        x = hidden_states.reshape(T, H)
        w, sel = _routing(x, gate_w)
        rows = jnp.arange(T)[:, None]
        cw_large = jnp.zeros((T, NUM_EXPERTS), x.dtype).at[rows, sel].add(w)
        cw_small = jnp.zeros((T, NUM_CHUNK), x.dtype).at[rows, sel // GROUP].add(w)
        large = _moe(x, Wg, Wu, Wd, cw_large)
        small = _moe(x, cWg, cWu, cWd, cw_small)
        return (large + SMALL_SCALE * small).reshape(B, S, H)

    def _L1_attn_ref(img_patches, w_in, b_in, fm_in_w, fm_conv_w, fm_conv_b, fm_xproj_w, fm_dt_w, fm_dt_b, fm_A_log, fm_D, fm_out_w, bm_in_w, bm_conv_w, bm_conv_b, bm_xproj_w, bm_dt_w, bm_dt_b, bm_A_log, bm_D, bm_out_w, ln_g, ln_b, w_out, b_out):
        import jax, jax.numpy as jnp
        import numpy as np
        B, L, FUSED, DIM = (4, 72, 256, 256)
        DI, DS, DCONV, DTR = (2 * DIM, 16, 4, 128)

        def _mamba_params(key, prefix):
            ks = jax.random.split(key, 6)
            s_in = 1.0 / np.sqrt(DIM)
            s_di = 1.0 / np.sqrt(DI)
            s_dt = 1.0 / np.sqrt(DTR)
            A_log = jnp.log(jnp.broadcast_to(jnp.arange(1, DS + 1, dtype=jnp.float32), (DI, DS)))
            return {prefix + '_in_w': jax.random.normal(ks[0], (2 * DI, DIM), jnp.float32) * s_in, prefix + '_conv_w': jax.random.normal(ks[1], (DI, DCONV), jnp.float32) * 0.5, prefix + '_conv_b': jnp.zeros((DI,), jnp.float32), prefix + '_xproj_w': jax.random.normal(ks[2], (DTR + 2 * DS, DI), jnp.float32) * s_di, prefix + '_dt_w': jax.random.normal(ks[3], (DI, DTR), jnp.float32) * s_dt, prefix + '_dt_b': jax.random.normal(ks[4], (DI,), jnp.float32) * 0.1 - 4.0, prefix + '_A_log': A_log, prefix + '_D': jnp.ones((DI,), jnp.float32), prefix + '_out_w': jax.random.normal(ks[5], (DIM, DI), jnp.float32) * s_di}

        def _dw_conv(x, w, b):
            xt = jnp.transpose(x, (0, 2, 1))
            xp = jnp.pad(xt, ((0, 0), (0, 0), (DCONV - 1, 0)))
            Ln = xt.shape[-1]
            y = b[None, :, None]
            for kk in range(DCONV):
                y = y + w[:, kk][None, :, None] * xp[:, :, kk:kk + Ln]
            return jnp.transpose(y, (0, 2, 1))

        def _selective_scan(xi, dt, Bm, Cm, A, D):

            def step(h, inp):
                dt_t, B_t, C_t, x_t = inp
                dA = jnp.exp(dt_t[..., None] * A)
                h = dA * h + (dt_t * x_t)[..., None] * B_t[:, None, :]
                y = jnp.einsum('bds,bs->bd', h, C_t)
                return (h, y)
            h0 = jnp.zeros((xi.shape[0], DI, DS), xi.dtype)
            inps = (jnp.swapaxes(dt, 0, 1), jnp.swapaxes(Bm, 0, 1), jnp.swapaxes(Cm, 0, 1), jnp.swapaxes(xi, 0, 1))
            _, ys = jax.lax.scan(step, h0, inps)
            return jnp.swapaxes(ys, 0, 1) + xi * D

        def _mamba(x, in_w, conv_w, conv_b, xproj_w, dt_w, dt_b, A_log, D, out_w):
            xz = jnp.einsum('bld,ed->ble', x, in_w)
            xi, z = jnp.split(xz, 2, axis=-1)
            xi = jax.nn.silu(_dw_conv(xi, conv_w, conv_b))
            xdb = jnp.einsum('bld,ed->ble', xi, xproj_w)
            dtr, Bm, Cm = (xdb[..., :DTR], xdb[..., DTR:DTR + DS], xdb[..., DTR + DS:])
            dt = jax.nn.softplus(jnp.einsum('blr,dr->bld', dtr, dt_w) + dt_b)
            y = _selective_scan(xi, dt, Bm, Cm, -jnp.exp(A_log), D)
            y = y * jax.nn.silu(z)
            return jnp.einsum('bld,ed->ble', y, out_w)

        def _layernorm(x, g, b, eps=1e-05):
            mu = jnp.mean(x, -1, keepdims=True)
            var = jnp.mean(jnp.square(x - mu), -1, keepdims=True)
            return (x - mu) * jax.lax.rsqrt(var + eps) * g + b
        h = jax.nn.gelu(jnp.einsum('blf,df->bld', img_patches, w_in) + b_in, approximate=False)
        fwd = _mamba(h, fm_in_w, fm_conv_w, fm_conv_b, fm_xproj_w, fm_dt_w, fm_dt_b, fm_A_log, fm_D, fm_out_w)
        bwd = _mamba(jnp.flip(h, 1), bm_in_w, bm_conv_w, bm_conv_b, bm_xproj_w, bm_dt_w, bm_dt_b, bm_A_log, bm_D, bm_out_w)
        r = fwd + jnp.flip(bwd, 1) + h
        r = _layernorm(r, ln_g, ln_b)
        return jnp.einsum('bld,ed->ble', r, w_out) + b_out

    def _L1_ffn_ref(x, lut, gate_idx, up_idx, down_idx):
        import jax, jax.numpy as jnp
        import numpy as np
        HIDDEN = 256
        INTER = 688
        LUT_SIZE = 16

        def _ghost_linear(x, idx, lut):
            w = lut[idx]
            return jnp.einsum('bsh,oh->bso', x, w)
        gate = _ghost_linear(x, gate_idx, lut)
        up = _ghost_linear(x, up_idx, lut)
        h = jax.nn.silu(gate) * up
        return _ghost_linear(h, down_idx, lut)
    x = L0_attn_x
    x = x + _L0_attn_ref(_layernorm(x, axis=-1), L0_attn_Wqkv, L0_attn_bqkv, L0_attn_Wout, L0_attn_bout)
    x = x + _L0_ffn_ref(_layernorm(x, axis=-1), L0_ffn_gate_w, L0_ffn_Wg, L0_ffn_Wu, L0_ffn_Wd, L0_ffn_cWg, L0_ffn_cWu, L0_ffn_cWd)
    x = x + _L1_attn_ref(_layernorm(x, axis=-1), L1_attn_w_in, L1_attn_b_in, L1_attn_fm_in_w, L1_attn_fm_conv_w, L1_attn_fm_conv_b, L1_attn_fm_xproj_w, L1_attn_fm_dt_w, L1_attn_fm_dt_b, L1_attn_fm_A_log, L1_attn_fm_D, L1_attn_fm_out_w, L1_attn_bm_in_w, L1_attn_bm_conv_w, L1_attn_bm_conv_b, L1_attn_bm_xproj_w, L1_attn_bm_dt_w, L1_attn_bm_dt_b, L1_attn_bm_A_log, L1_attn_bm_D, L1_attn_bm_out_w, L1_attn_ln_g, L1_attn_ln_b, L1_attn_w_out, L1_attn_b_out)
    x = x + _L1_ffn_ref(_layernorm(x, axis=-1), L1_ffn_lut, L1_ffn_gate_idx, L1_ffn_up_idx, L1_ffn_down_idx)
    return x

_drawn_inputs = setup_inputs


def setup_inputs(seed=0):
    import zlib

    import numpy as np

    out = dict(_drawn_inputs(seed))
    spreads = {'L1_attn_b_in': (0.0, 0.341),
     'L1_attn_fm_conv_b': (0.0, 1.137),
     'L1_attn_fm_D': (1.0, 0.6),
     'L1_attn_bm_conv_b': (0.0, 1.051),
     'L1_attn_bm_D': (1.0, 0.6),
     'L1_attn_ln_g': (1.0, 0.2),
     'L1_attn_ln_b': (0.0, 0.413),
     'L1_attn_b_out': (0.0, 0.4)}
    factors = {'L0_attn_bqkv': 5.617,
     'L0_attn_bout': 6.134,
     'L0_ffn_gate_w': 8.0,
     'L0_ffn_Wg': 8.0,
     'L0_ffn_Wu': 8.0,
     'L0_ffn_Wd': 8.0,
     'L0_ffn_cWg': 8.0,
     'L0_ffn_cWu': 8.0,
     'L0_ffn_cWd': 8.0,
     'L1_attn_fm_dt_w': 33.232,
     'L1_attn_fm_dt_b': 64.0,
     'L1_attn_fm_A_log': 2.834,
     'L1_attn_bm_dt_w': 32.136,
     'L1_attn_bm_dt_b': 8.0,
     'L1_attn_bm_A_log': 3.335,
     'L1_attn_fm_xproj_w': 8.0,
     'L1_ffn_lut': 6.757}
    for name, (base, spread) in spreads.items():
        noise = np.random.default_rng([zlib.crc32(name.encode()), seed]).standard_normal(out[name].shape)
        drawn = base * np.exp(spread * noise) if base else spread * noise
        out[name] = jnp.asarray(drawn.astype(out[name].dtype))
    for name, factor in factors.items():
        out[name] = (out[name] * factor).astype(out[name].dtype)
    return out
```

```python
from contextlib import ExitStack

import concourse.bass as bass
from concourse import mybir

ALU = mybir.AluOpType
ACT = mybir.ActivationFunctionType
AX = mybir.AxisListType
F32 = mybir.dt.float32
F32R = mybir.dt.float32r
U32 = mybir.dt.uint32
I32 = mybir.dt.int32

P = 128
D = 256
KC = D // P
NSEQ, SEQ = 4, 256
T = NSEQ * SEQ
NB = T // P
HALF = 512
NH = T // HALF
EPS = 1e-5

HEADS, GROUPS, HD = 16, 4, 16
KV = GROUPS * HD
HJ = HEADS // GROUPS
QB = SEQ // P

NEXP, TOPK, INTER = 32, 4, 96
NCH, CINTER = 16, 128
SMALL = 0.05
EB = NEXP * INTER // P
MOE_IT = 8
MOE_K = 5
MOE_WN = 2 * KC * P + D
ESLOT = [0, 1, 0, 1, 2]
NCW = NEXP + NCH

DI, DS, DCONV, DTR = 512, 16, 4, 128
DB = DI // P
PADC = DCONV - 1
SEGC = SEQ + 2 * PADC
SEGS = SEQ + 1

FI = 688
FB = [(m * P, min(P, FI - m * P)) for m in range((FI + P - 1) // P)]
LUT = 16
LUTW = KC * FI * 2 + len(FB) * D
LCH = 860
assert MOE_K * LCH >= LUTW and 2 * MOE_IT == LUT


class Core:

    def __init__(self, nc, ctx):
        self.nc, self.ctx, self.used, self.from_one = nc, ctx, [], []

    def sem(self, name):
        self.used.append(self.nc.alloc_semaphore(name=name))
        return self.used[-1]

    def counters(self, prefix, names, by):
        found = [self.sem(prefix + n) for n in names.split()]
        for s in found:
            by.sem_inc(s, 1)
        self.from_one += [s.name for s in found]
        return found

    def wait(self, e, s, count):
        e.wait_ge(s, count + 1 if s.name in self.from_one else count)

    def recycle(self):
        self.nc.clear_and_free_semaphores(self.used)
        self.used, self.from_one = [], []
        self.nc.all_engine_barrier()

    def sb(self, ctx, name, shape, dt=F32):
        return ctx.enter_context(self.nc.sbuf_tensor(name, shape, dt))

    def ps(self, ctx, name, shape):
        return ctx.enter_context(self.nc.psum_tensor(name, shape, F32))


def seq_view(ap, seg, lo):
    return ap.rearrange("p (b s) -> p b s", s=seg)[:, :, lo:lo + SEQ]


def constants(c, g):
    nc = c.nc
    s_set, s_const = c.sem("s_set"), c.sem("s_const")
    with nc.Block() as block:
        @block.gpsimd
        def _(e):
            e.memset(g.ident[:, :], 0.0).then_inc(s_set, 1)
            e.memset(g.gmask[:, :], 1.0).then_inc(s_set, 1)
            e.iota(g.iota_e[:, :], [[1, NEXP]], base=0, channel_multiplier=0,
                   allow_small_or_imprecise_dtypes=True).then_inc(s_const, 1)
            e.iota(g.iota_l[:, :], [[1, LUT]], base=0, channel_multiplier=0,
                   allow_small_or_imprecise_dtypes=True).then_inc(s_const, 1)
            c.wait(e, s_set, 2)
            e.affine_select(out=g.ident[:, :], in_=g.ident[:, :], compare_op=ALU.not_equal, fill=1.0,
                            base=0, pattern=[[-1, P]], channel_multiplier=1).then_inc(s_const, 1)
            e.affine_select(out=g.gmask[:, :], in_=g.gmask[:, :], compare_op=ALU.is_ge, fill=0.0,
                            base=0, pattern=[[-HD, 8]], channel_multiplier=1).then_inc(s_set, 1)
            c.wait(e, s_set, 3)
            e.affine_select(out=g.gmask[:, :], in_=g.gmask[:, :], compare_op=ALU.is_ge, fill=0.0,
                            base=HD - 1, pattern=[[HD, 8]], channel_multiplier=-1).then_inc(s_const, 1)
            c.wait(e, s_const, 4)


def layernorm(c, g, name, src, feat, gamma=None, beta=None, hi=None, lo=None, loads=None):
    nc = c.nc
    sem = lambda n: c.sem(f"{name}_{n}")
    s_stat, s_aggr, s_var, s_sd, s_r, s_xn, s_tp, s_ev, s_hi, s_lo = map(
        sem, "stat aggr var sd r xn tp ev hi lo".split())
    with ExitStack() as ctx:
        stats = c.sb(ctx, name + "_stats", [P, NB, 6])
        mv = c.sb(ctx, name + "_mv", [P, NB, 2])
        sm = c.sb(ctx, name + "_sm", [P, 5, NB])
        xn = c.sb(ctx, name + "_xn", [P, NB, D])
        ps = c.ps(ctx, name + "_ps", [P, KC, T])
        var, sd, r, q, nmr = (sm[:, i, :] for i in range(5))
        with nc.Block() as block:
            @block.vector
            def _(e):
                for n in range(NB):
                    if loads:
                        c.wait(e, loads[n], 16)
                    e.bn_stats(stats[:, n, :], src[:, n, :]).then_inc(s_stat, 1)
                for n in range(NB):
                    c.wait(e, s_stat, n + 1)
                    e.bn_aggr(mv[:, n, :], stats[:, n, :]).then_inc(s_aggr, 1)
                c.wait(e, s_aggr, NB)
                e.tensor_scalar(var, mv[:, :, 1], EPS, None, ALU.add).then_inc(s_var, 1)
                c.wait(e, s_sd, 1)
                e.reciprocal(r, sd).then_inc(s_r, 1)
                c.wait(e, s_r, 1)
                e.tensor_tensor(q, r, r, ALU.mult).then_inc(s_r, 1)
                c.wait(e, s_r, 2)
                e.tensor_tensor(q, q, var, ALU.mult).then_inc(s_r, 1)
                c.wait(e, s_r, 3)
                e.tensor_scalar(q, q, -0.5, 1.5, ALU.mult, ALU.add).then_inc(s_r, 1)
                c.wait(e, s_r, 4)
                e.tensor_tensor(r, r, q, ALU.mult).then_inc(s_r, 1)
                c.wait(e, s_r, 5)
                for n in range(NB):
                    e.tensor_scalar(xn[:, n, :], src[:, n, :], mv[:, n, 0:1], r[:, n:n + 1],
                                    ALU.subtract, ALU.mult).then_inc(s_xn, 1)
                for k in range(KC):
                    if lo is not None:
                        c.wait(e, s_hi, k + 1)
                        c.wait(e, s_ev, k + 1)
                        e.tensor_tensor(lo[:, k, :], feat[:, k, :], hi[:, k, :].bitcast(F32),
                                        ALU.subtract).then_inc(s_lo, 1)

            @block.scalar
            def _(e):
                c.wait(e, s_var, 1)
                e.activation(sd, var, ACT.Sqrt).then_inc(s_sd, 1)
                for k in range(KC):
                    c.wait(e, s_tp, NB * (k + 1))
                    if gamma is None:
                        e.activation(feat[:, k, :], ps[:, k, :], ACT.Copy).then_inc(s_ev, 1)
                    else:
                        e.activation(feat[:, k, :], ps[:, k, :], ACT.Identity, bias=beta[:, k:k + 1],
                                     scale=gamma[:, k:k + 1]).then_inc(s_ev, 1)
                    if hi is not None:
                        e.activation(hi[:, k, :], ps[:, k, :], ACT.Copy).then_inc(s_hi, 1)

            @block.tensor
            def _(e):
                for k in range(KC):
                    for n in range(NB):
                        c.wait(e, s_xn, n + 1)
                        e.transpose(ps[:, k, n * P:(n + 1) * P], xn[:, n, k * P:(k + 1) * P],
                                    g.ident[:, :]).then_inc(s_tp, 1)


def attention(c, g, dram):
    nc = c.nc
    sem = c.sem
    s_w = sem("at_w")
    s_q, s_k, s_v, s_qe, s_ke, s_kd, s_ve, s_kb, s_xb = map(
        sem, ["at_q", "at_k", "at_v", "at_qe", "at_ke", "at_kd", "at_ve", "at_kb", "at_xb"])
    s_qc, = c.counters("at_", "qc", nc.gpsimd)
    s_sc, s_pt, s_pv, s_ot, s_op = c.counters("at_", "sc pt pv ot op", nc.tensor)
    s_mx, s_nm, s_pe, s_ri, s_on, s_x = c.counters("at_", "mx nm pe ri on x", nc.vector)
    s_ex, s_oe = c.counters("at_", "ex oe", nc.scalar)
    U = QB * HJ
    with ExitStack() as ctx:
        wqkv = c.sb(ctx, "wqkv", [P, KC, D + 2 * KV])
        wk2 = c.sb(ctx, "wk2", [P, KC, 2 * KV])
        wout = c.sb(ctx, "wout", [P, KC, D])
        bq = c.sb(ctx, "bq", [P, KC])
        bk = c.sb(ctx, "bk", [P, 1])
        bv = c.sb(ctx, "bv", [P, KV])
        bout = c.sb(ctx, "bout", [P, D])
        kbm = c.sb(ctx, "kbm", [P, 8])
        qT = c.sb(ctx, "qT", [P, KC, T])
        kmask = c.sb(ctx, "kmask", [P, 2, GROUPS, T])
        v = c.sb(ctx, "v", [P, NB, KV])
        with ExitStack() as pctx:
            qps = c.ps(pctx, "qps", [P, KC, T])
            kps = c.ps(pctx, "kps", [P, T])
            vps = c.ps(pctx, "vps", [P, NB, KV])
            with nc.Block() as block:
                @block.sync
                def _(e):
                    wsrc = dram["Wqkv"].rearrange("(k p) n -> p k n", p=P)
                    e.dma_start(wqkv[:, :, :], wsrc).then_inc(s_w, 16)
                    e.dma_start(wk2[:, :, 0:KV], wsrc[:, :, D:D + KV]).then_inc(s_w, 16)
                    e.dma_start(wk2[:, :, KV:2 * KV], wsrc[:, :, D:D + KV]).then_inc(s_w, 16)
                    e.dma_start(wout[:, :, :], dram["Wout"].rearrange("(k p) n -> p k n", p=P)).then_inc(s_w, 16)
                    for k in range(KC):
                        e.dma_start(bq[:, k:k + 1], dram["bqkv"][k * P:(k + 1) * P, :]).then_inc(s_w, 16)
                    for k in range(2):
                        e.dma_start(bk[k * KV:(k + 1) * KV, :], dram["bqkv"][D:D + KV, :]).then_inc(s_w, 16)
                    e.dma_start(bv[:, :], dram["bqkv"][D + KV:D + 2 * KV, :].rearrange("n a -> a n")
                                .broadcast_to([P, KV])).then_inc(s_w, 16)
                    e.dma_start(bout[:, :], dram["bout"].broadcast_to([P, D])).then_inc(s_w, 16)

                NW = 10 * 16

                @block.tensor
                def _(e):
                    c.wait(e, s_w, NW)
                    for h in range(NH):
                        for k in range(KC):
                            mm = e.matmul(kps[:, h * HALF:(h + 1) * HALF], wk2[:, k, :],
                                          g.feat[:, k, h * HALF:(h + 1) * HALF], start=k == 0, stop=k == KC - 1)
                    mm.then_inc(s_k, 1)
                    for m in range(KC):
                        for h in range(NH):
                            for k in range(KC):
                                mm = e.matmul(qps[:, m, h * HALF:(h + 1) * HALF], wqkv[:, k, m * P:(m + 1) * P],
                                              g.feat[:, k, h * HALF:(h + 1) * HALF], start=k == 0, stop=k == KC - 1)
                        mm.then_inc(s_q, 1)
                    for n in range(NB):
                        for k in range(KC):
                            mm = e.matmul(vps[:, n, :], g.feat[:, k, n * P:(n + 1) * P],
                                          wqkv[:, k, D + KV:D + 2 * KV], start=k == 0, stop=k == KC - 1)
                    mm.then_inc(s_v, 1)

                @block.gpsimd
                def _(e):
                    c.wait(e, s_w, NW)
                    e.tensor_tensor(kbm[:, :], g.gmask[:, :], bk[:, 0:1].broadcast_to([P, 8]), ALU.mult).then_inc(s_kb, 1)
                    e.tensor_tensor(g.x[:, :, :], g.x[:, :, :],
                                    bout[:, :].unsqueeze(1).broadcast_to([P, NB, D]), ALU.add).then_inc(s_xb, 1)

                @block.vector
                def _(e):
                    c.wait(e, s_w, NW)
                    c.wait(e, s_k, 1)
                    for i in range(8):
                        e.tensor_scalar(kmask[:, i // 4, i % 4, 0:HALF], kps[:, 0:HALF], bk[:, 0:1], g.gmask[:, i:i + 1],
                                        ALU.add, ALU.mult).then_inc(s_kd, 1)
                    c.wait(e, s_v, 1)
                    e.tensor_tensor(v[:, :, :], vps[:, :, :],
                                    bv[:, :].unsqueeze(1).broadcast_to([P, NB, KV]), ALU.add).then_inc(s_ve, 1)

                @block.scalar
                def _(e):
                    c.wait(e, s_k, 1)
                    c.wait(e, s_kb, 1)
                    for i in range(8):
                        e.activation(kmask[:, i // 4, i % 4, HALF:T], kps[:, HALF:T], ACT.Identity, bias=kbm[:, i:i + 1],
                                     scale=g.gmask[:, i:i + 1]).then_inc(s_ke, 1)
                    for m in range(KC):
                        c.wait(e, s_q, m + 1)
                        e.activation(qT[:, m, :], qps[:, m, :], ACT.Identity, bias=bq[:, m:m + 1]).then_inc(s_qe, 1)

        qcur = c.sb(ctx, "qcur", [P, KC, SEQ])
        prob = c.sb(ctx, "prob", [P, 2, GROUPS, SEQ])
        pT = c.sb(ctx, "pT", [P, 2, QB, GROUPS, P])
        mx = c.sb(ctx, "mx", [P, 2, U, GROUPS])
        rs = c.sb(ctx, "rs", [P, U, GROUPS])
        ri = c.sb(ctx, "ri", [P, U, GROUPS])
        on = c.sb(ctx, "on", [P, QB, D])
        oT = c.sb(ctx, "oT", [P, QB, KC, P])
        sps = c.ps(ctx, "sps", [P, 2, GROUPS, SEQ])
        tps = c.ps(ctx, "tps", [P, QB, GROUPS, P])
        ops = c.ps(ctx, "ops", [P, QB, D])
        mps = c.ps(ctx, "mps", [P, 2, D])
        with nc.Block() as block:
            @block.gpsimd
            def _(e):
                with e.Fori(0, NSEQ) as b:
                    c.wait(e, s_sc, b * U)
                    e.tensor_copy(qcur[:, :, :], qT[:, :, bass.ds(b * SEQ, SEQ)]).then_inc(s_qc, 1)

            @block.tensor
            def _(e):
                with e.Fori(0, NSEQ) as b:
                    def scores(u):
                        qb, j = divmod(u, HJ)
                        if u >= 2:
                            c.wait(e, s_ex, b * U + u - 1)
                        for gg in range(0, GROUPS, 2):
                            mm = e.matmul(sps[:, u % 2, gg:gg + 2, :], qcur[:, j // 2, qb * P:(qb + 1) * P],
                                          kmask[:, j % 2, gg:gg + 2, bass.ds(b * SEQ, SEQ)], start=True, stop=True)
                        mm.then_inc(s_sc, 1)

                    def turn(u):
                        c.wait(e, s_ex, b * U + u + 1)
                        c.wait(e, s_pe, b * U + u)
                        for kb in range(QB):
                            for gg in range(GROUPS):
                                mm = e.transpose(tps[:, kb, gg, :], prob[:, u % 2, gg, kb * P:(kb + 1) * P],
                                                 g.ident[:, :])
                        mm.then_inc(s_pt, 1)

                    def values(u):
                        qb, j = divmod(u, HJ)
                        c.wait(e, s_pe, b * U + u + 1)
                        if u == HJ:
                            c.wait(e, s_on, b * QB + 1)
                        for gg in range(GROUPS):
                            for kb in range(QB):
                                h = HJ * j + gg
                                mm = e.matmul(ops[:, qb, h * HD:(h + 1) * HD], pT[:, u % 2, kb, gg, :],
                                              v[:, bass.ds(b * QB + kb, 1), gg * HD:(gg + 1) * HD]
                                              .rearrange("p a d -> p (a d)"),
                                              start=kb == 0, stop=kb == QB - 1)
                        mm.then_inc(s_pv, 1)

                    def out_turn(qb):
                        c.wait(e, s_on, b * QB + qb + 1)
                        c.wait(e, s_x, b * QB + qb)
                        for k in range(KC):
                            mm = e.transpose(mps[:, 0, k * P:(k + 1) * P], on[:, qb, k * P:(k + 1) * P], g.ident[:, :])
                        mm.then_inc(s_ot, 1)

                    def out_proj(qb):
                        c.wait(e, s_oe, b * QB + qb + 1)
                        for k in range(KC):
                            mm = e.matmul(mps[:, 1, :], oT[:, qb, k, :], wout[:, k, :], start=k == 0, stop=k == KC - 1)
                        mm.then_inc(s_op, 1)

                    c.wait(e, s_qc, b + 1)
                    c.wait(e, s_ex, b * U)
                    c.wait(e, s_on, b * QB)
                    for u in range(U):
                        scores(u)
                        if u >= 1:
                            turn(u - 1)
                        if u >= 2:
                            values(u - 2)
                        if u == 7:
                            out_turn(0)
                    turn(U - 1)
                    values(U - 2)
                    out_proj(0)
                    values(U - 1)
                    out_turn(1)
                    out_proj(1)

            @block.vector
            def _(e):
                with e.Fori(0, NSEQ) as b:
                    def maximum(u):
                        c.wait(e, s_sc, b * U + u + 1)
                        if u < 2:
                            c.wait(e, s_ex, b * U)
                        e.tensor_reduce(mx[:, 0, u, :], sps[:, u % 2, :, :], AX.X, ALU.max).then_inc(s_mx, 1)
                        c.wait(e, s_mx, b * U + u + 1)
                        e.tensor_scalar(mx[:, 1, u, :], mx[:, 0, u, :], -1.0 / HD, None, ALU.mult).then_inc(s_nm, 1)

                    def copy_out(u):
                        c.wait(e, s_pt, b * U + u + 1)
                        if u >= 2:
                            c.wait(e, s_pv, b * U + u - 1)
                        else:
                            c.wait(e, s_pv, b * U)
                        e.tensor_copy(pT[:, u % 2, :, :, :], tps[:, :, :, :]).then_inc(s_pe, 1)

                    def normalise(qb):
                        u1 = (qb + 1) * HJ
                        c.wait(e, s_ex, b * U + u1)
                        e.reciprocal(ri[:, u1 - HJ:u1, :], rs[:, u1 - HJ:u1, :]).then_inc(s_ri, 1)
                        c.wait(e, s_ri, b * QB + qb + 1)
                        c.wait(e, s_pv, b * U + u1)
                        c.wait(e, s_ot, b * QB)
                        e.tensor_tensor(on[:, qb, :].rearrange("p (h d) -> p h d", d=HD),
                                        ops[:, qb, :].rearrange("p (h d) -> p h d", d=HD),
                                        ri[:, u1 - HJ:u1, :].rearrange("p j g -> p (j g)").unsqueeze(2)
                                        .broadcast_to([P, HEADS, HD]), ALU.mult).then_inc(s_on, 1)

                    def residual(qb):
                        c.wait(e, s_op, b * QB + qb + 1)
                        xs = g.x[:, bass.ds(b * QB + qb, 1), :].rearrange("p a d -> p (a d)")
                        e.tensor_tensor(xs, mps[:, 1, :], xs, ALU.add).then_inc(s_x, 1)

                    for u in range(U):
                        maximum(u)
                        if u == 6:
                            normalise(0)
                        if u >= 1:
                            copy_out(u - 1)
                    copy_out(U - 1)
                    residual(0)
                    normalise(1)
                    residual(1)

            @block.scalar
            def _(e):
                with e.Fori(0, NSEQ) as b:
                    def exps(u):
                        c.wait(e, s_nm, b * U + u + 1)
                        if u >= 2:
                            c.wait(e, s_pt, b * U + u - 1)
                        else:
                            c.wait(e, s_pt, b * U)
                        if u == 0:
                            c.wait(e, s_ri, b * QB)
                        for gg in range(GROUPS):
                            a = e.activation(prob[:, u % 2, gg, :], sps[:, u % 2, gg, :], ACT.Exp,
                                             bias=mx[:, 1, u, gg:gg + 1], scale=1.0 / HD,
                                             accum_out=rs[:, u, gg:gg + 1])
                        a.then_inc(s_ex, 1)

                    def turn_out(qb):
                        c.wait(e, s_ot, b * QB + qb + 1)
                        c.wait(e, s_op, b * QB)
                        e.activation(oT[:, qb, :, :].rearrange("p k t -> p (k t)"), mps[:, 0, :],
                                     ACT.Copy).then_inc(s_oe, 1)

                    for u in range(U):
                        exps(u)
                    turn_out(0)
                    turn_out(1)


def routing(c, g, dram, hi_lo_feat):
    nc = c.nc
    s_gw, s_lg, s_le, s_m8, s_ix, s_if, s_eq, s_mk, s_sh, s_ex, s_me, s_sm, s_rc, s_cw, s_pr, s_tp, s_te, s_st, s_li = map(
        c.sem, [f"rt_{n}" for n in "gw lg le m8 ix if eq mk sh ex me sm rc cw pr tp te st li".split()])
    with ExitStack() as ctx:
        gw = c.sb(ctx, "gw", [P, KC, NEXP])
        lg = c.sb(ctx, "lg", [P, NB, NEXP])
        m8 = c.sb(ctx, "m8", [P, NB, 8])
        i8 = c.sb(ctx, "i8", [P, NB, 8], U32)
        f8 = c.sb(ctx, "f8", [P, NB, 8])
        eq = c.sb(ctx, "eq", [P, NB, TOPK, NEXP])
        mask = c.sb(ctx, "mask", [P, NB, NEXP])
        ex = c.sb(ctx, "ex", [P, NB, NEXP])
        sm = c.sb(ctx, "rsm", [P, 2, NB])
        cw = c.sb(ctx, "cw", [P, NB, NCW])
        cwT = c.sb(ctx, "cwT", [NCW, T])
        lps = c.ps(ctx, "lps", [P, NB, NEXP])
        tps = c.ps(ctx, "ctps", [NCW, T])
        with nc.Block() as block:
            @block.sync
            def _(e):
                e.dma_start(gw[:, :, :], dram["gate_wT"].rearrange("(k p) n -> p k n", p=P)).then_inc(s_gw, 16)
                e.dma_start(g.lut_i[:, :], dram["lut_idx"]).then_inc(s_li, 16)
                e.dma_start(g.lutb[:, :], dram["lut"].broadcast_to([P, LUT])).then_inc(s_li, 16)
                c.wait(e, s_te, 1)
                e.dma_start(dram["cw"], cwT[:, :]).then_inc(s_st, 16)
                c.wait(e, s_st, 16)
                c.wait(e, s_li, 32)

            @block.tensor
            def _(e):
                c.wait(e, s_gw, 16)
                for n in range(NB):
                    for k in range(KC):
                        mm = e.matmul(lps[:, n, :], g.feat[:, k, n * P:(n + 1) * P], gw[:, k, :],
                                      start=k == 0, stop=k == KC - 1)
                mm.then_inc(s_lg, 1)
                c.wait(e, s_cw, 1)
                c.wait(e, s_pr, 2)
                for n in range(NB):
                    mm = e.transpose(tps[:, n * P:(n + 1) * P], cw[:, n, :], g.ident[:, :])
                mm.then_inc(s_tp, 1)

            @block.vector
            def _(e):
                c.wait(e, s_lg, 1)
                e.tensor_copy(lg[:, :, :], lps[:, :, :]).then_inc(s_le, 1)
                c.wait(e, s_le, 1)
                for n in range(NB):
                    e.max(m8[:, n, :], lg[:, n, :]).then_inc(s_m8, 1)
                c.wait(e, s_m8, NB)
                e.tensor_tensor(ex[:, :, :], lg[:, :, :], m8[:, :, 0:1].broadcast_to([P, NB, NEXP]),
                                ALU.subtract).then_inc(s_sh, 1)
                for n in range(NB):
                    e.max_index(i8[:, n, :], m8[:, n, :], lg[:, n, :]).then_inc(s_ix, 1)
                c.wait(e, s_ix, NB)
                e.tensor_copy(f8[:, :, :], i8[:, :, :]).then_inc(s_if, 1)
                c.wait(e, s_if, 1)
                e.tensor_tensor(eq[:, :, :, :],
                                g.iota_e[:, :].unsqueeze(1).unsqueeze(1).broadcast_to([P, NB, TOPK, NEXP]),
                                f8[:, :, 0:TOPK].unsqueeze(3).broadcast_to([P, NB, TOPK, NEXP]),
                                ALU.is_equal).then_inc(s_eq, 1)
                c.wait(e, s_eq, 1)
                e.tensor_reduce(mask[:, :, :], eq[:, :, :, :].rearrange("p n k e -> p n e k"), AX.X,
                                ALU.add).then_inc(s_mk, 1)
                c.wait(e, s_mk, 1)
                c.wait(e, s_ex, 1)
                e.tensor_tensor(mask[:, :, :], mask[:, :, :], ex[:, :, :], ALU.mult).then_inc(s_me, 1)
                c.wait(e, s_me, 1)
                e.tensor_reduce(sm[:, 0, :], mask[:, :, :], AX.X, ALU.add).then_inc(s_sm, 1)
                c.wait(e, s_sm, 1)
                e.reciprocal(sm[:, 1, :], sm[:, 0, :]).then_inc(s_rc, 1)
                c.wait(e, s_rc, 1)
                e.tensor_tensor(cw[:, :, 0:NEXP], mask[:, :, :], sm[:, 1, :].unsqueeze(2)
                                .broadcast_to([P, NB, NEXP]), ALU.mult).then_inc(s_cw, 1)
                c.wait(e, s_cw, 1)
                pair = cw[:, :, 0:NEXP].rearrange("p n (c a) -> p n c a", a=2)
                e.tensor_tensor(cw[:, :, NEXP:NCW], pair[:, :, :, 0], pair[:, :, :, 1], ALU.add).then_inc(s_pr, 1)
                c.wait(e, s_pr, 1)
                e.tensor_scalar(cw[:, :, NEXP:NCW], cw[:, :, NEXP:NCW], SMALL, None, ALU.mult).then_inc(s_pr, 1)
                c.wait(e, s_li, 32)
                e.tensor_copy(g.lut_f[:, 0:LUTW], g.lut_i[:, :]).then_inc(s_li, 1)
                e.memset(g.lut_f[:, LUTW:], 0.0).then_inc(s_li, 1)
                e.memset(g.lutw[:, :], 0.0).then_inc(s_li, 1)
                c.wait(e, s_tp, 1)
                e.tensor_copy(cwT[:, :], tps[:, :]).then_inc(s_te, 1)

            @block.scalar
            def _(e):
                c.wait(e, s_sh, 1)
                e.activation(ex[:, :, :], ex[:, :, :], ACT.Exp).then_inc(s_ex, 1)


def experts(c, g, dram, xh, xl):
    nc = c.nc
    s_w = [c.sem(f"ex_w{k}") for k in range(MOE_K)]
    s_c = [c.sem(f"ex_c{k}") for k in range(MOE_K)]
    s_z = c.sem("ex_z")
    s_g, s_u, s_d = c.counters("ex_", "g u d", nc.tensor)
    s_wl, s_tc, s_a, s_le = c.counters("ex_", "wl tc a le", nc.vector)
    s_wh, s_si, s_ah = c.counters("ex_", "wh si ah", nc.scalar)
    s_al, s_la = c.counters("ex_", "al la", nc.gpsimd)
    s_ye, s_yt, s_yx = map(c.sem, ["ex_ye", "ex_yt", "ex_yx"])
    K, LAST = MOE_K, MOE_IT * MOE_K
    with ExitStack() as ctx:
        wr = c.sb(ctx, "wr", [P, K, MOE_WN])
        wh = c.sb(ctx, "wh", [P, K, MOE_WN], F32R)
        wl = c.sb(ctx, "wl", [P, K, MOE_WN], F32R)
        cwb = c.sb(ctx, "cwb", [P, 3, T])
        si = c.sb(ctx, "si", [P, 3, T])
        a = c.sb(ctx, "a", [P, 3, T])
        ah = c.sb(ctx, "ah", [P, 3, T], F32R)
        al = c.sb(ctx, "al", [P, 3, T], F32R)
        lt = c.sb(ctx, "lt", [P, 2, LCH])
        gps = c.ps(ctx, "gps", [P, T])
        ups = c.ps(ctx, "ups", [P, T])
        yps = c.ps(ctx, "yps", [P, KC, T])
        yT = a[:, 0:KC, :]
        ZA, ZW = ESLOT[-1], K - 1

        def half(h):
            return slice(h * HALF, (h + 1) * HALF)

        with nc.Block() as block:
            @block.sync
            def _(e):
                def load(index, slot):
                    e.dma_start(wr[:, slot, :], dram["moe_w"][index, :, :].rearrange("a p n -> (a p) n")
                                ).then_inc(s_w[slot], 16)

                load(slice(0, 1), 0)
                with e.Fori(0, MOE_IT) as j:
                    for k in range(K):
                        n, s = j * K + k, ESLOT[k]
                        c.wait(e, s_tc, n + 1 if k >= 2 else n)
                        if k < 3:
                            r0 = k * P
                            cut = (r0 // INTER + 1) * INTER - r0
                            for p0, p1 in [(0, cut), (cut, P)]:
                                e.dma_start(cwb[p0:p1, s, :],
                                            dram["cw"][bass.ds(4 * j + (r0 + p0) // INTER, 1), :]
                                            .broadcast_to([p1 - p0, T])).then_inc(s_c[k], 16)
                        else:
                            e.dma_start(cwb[:, s, :], dram["cw"][bass.ds(2 * j + (NEXP + k - 3), 1), :]
                                        .broadcast_to([P, T])).then_inc(s_c[k], 16)
                        c.wait(e, s_wl, n)
                        load(bass.ds(n + 1, 1), (k + 1) % K)

            def split_high(e, slot, loaded):
                c.wait(e, s_w[slot], loaded)
                e.activation(wh[:, slot, :], wr[:, slot, :], ACT.Copy).then_inc(s_wh, 1)

            def split_low(e, slot, done):
                c.wait(e, s_wh, done)
                e.tensor_tensor(wl[:, slot, :], wr[:, slot, :], wh[:, slot, :].bitcast(F32),
                                ALU.subtract).then_inc(s_wl, 1)

            @block.scalar
            def _(e):
                split_high(e, 0, 16)
                with e.Fori(0, MOE_IT) as j:
                    for k in range(K):
                        n, s = j * K + k, ESLOT[k]
                        c.wait(e, s_g, n + 1)
                        e.activation(si[:, s, :], gps[:, :], ACT.Silu).then_inc(s_si, 1)
                        c.wait(e, s_d, n + 1)
                        c.wait(e, s_wl, n + 1)
                        split_high(e, (k + 1) % K, j * 16 + (16 if k < K - 1 else 32))
                        c.wait(e, s_a, n + 1)
                        e.activation(ah[:, s, :], a[:, s, :], ACT.Copy).then_inc(s_ah, 1)
                c.wait(e, s_d, LAST + 2)
                c.wait(e, s_al, LAST)
                for q in range(KC):
                    e.activation(yT[:, q, :], yps[:, q, :], ACT.Copy).then_inc(s_ye, 1)

            @block.vector
            def _(e):
                e.memset(ah[:, ZA, :].bitcast(F32), 0.0).then_inc(s_z, 1)
                e.memset(wh[:, ZW, :].bitcast(F32), 0.0).then_inc(s_tc, 1)
                e.memset(wl[:, ZW, :].bitcast(F32), 0.0).then_inc(s_tc, 1)
                split_low(e, 0, 1)
                with e.Fori(0, MOE_IT) as j:
                    for k in range(K):
                        n, s = j * K + k, ESLOT[k]
                        c.wait(e, s_si, n + 1)
                        c.wait(e, s_c[k], (j + 1) * (32 if k < 3 else 16))
                        e.tensor_tensor(si[:, s, :], si[:, s, :], cwb[:, s, :], ALU.mult).then_inc(s_tc, 1)
                        c.wait(e, s_la, 2 * n)
                        for q in range(2):
                            e.tensor_scalar(lt[:, q, :], g.lut_f[:, k * LCH:(k + 1) * LCH],
                                            g.iota_l[:, bass.ds(2 * j + q, 1)], g.lutb[:, bass.ds(2 * j + q, 1)],
                                            ALU.is_equal, ALU.mult).then_inc(s_le, 1)
                        split_low(e, (k + 1) % K, n + 2)
                        c.wait(e, s_tc, n + 3)
                        c.wait(e, s_u, n + 1)
                        e.tensor_tensor(a[:, s, :], ups[:, :], si[:, s, :], ALU.mult).then_inc(s_a, 1)
                for n in range(NB):
                    c.wait(e, s_yt, n // 2 + 1)
                    yb = gps if n < NB // 2 else ups
                    e.tensor_tensor(g.x[:, n, :], yb[:, (n % 4) * D:(n % 4 + 1) * D], g.x[:, n, :],
                                    ALU.add).then_inc(s_yx, 1)

            @block.gpsimd
            def _(e):
                e.memset(al[:, ZA, :].bitcast(F32), 0.0).then_inc(s_z, 1)
                with e.Fori(0, MOE_IT) as j:
                    for k in range(K):
                        n, s = j * K + k, ESLOT[k]
                        for q in range(2):
                            c.wait(e, s_le, n * 2 + q + 1)
                            c.wait(e, s_la, n * 2 + q)
                            part = g.lutw[:, k * LCH:(k + 1) * LCH]
                            e.tensor_tensor(part, part, lt[:, q, :], ALU.add).then_inc(s_la, 1)
                        c.wait(e, s_ah, n + 1)
                        e.tensor_tensor(al[:, s, :], a[:, s, :], ah[:, s, :].bitcast(F32),
                                        ALU.subtract).then_inc(s_al, 1)

            @block.tensor
            def _(e):
                def rows(ps, slot, part, sem):
                    for h in range(NH):
                        terms = [(w, x, q) for q in range(KC) for w, x in ((wh, xh), (wh, xl), (wl, xh))]
                        for i, (w, x, q) in enumerate(terms):
                            o = (part * KC + q) * P
                            mm = e.matmul(ps[:, half(h)], w[:, slot, o:o + P], x[:, q, half(h)],
                                          start=i == 0, stop=i == len(terms) - 1)
                    mm.then_inc(sem, 1)

                def down(slot, wslot, first=False):
                    for q in range(KC):
                        o = 2 * KC * P + q * P
                        for i, (w, x) in enumerate(((wh, ah), (wl, ah), (wh, al))):
                            for h in range(NH):
                                mm = e.matmul(yps[:, q, half(h)], w[:, wslot, o:o + P], x[:, slot, half(h)],
                                              start=first and i == 0, stop=False, skip_group_check=True)
                    mm.then_inc(s_d, 1)

                c.wait(e, s_z, 2)
                c.wait(e, s_tc, 2)
                down(ZA, ZW, first=True)
                with e.Fori(0, MOE_IT) as j:
                    for k in range(K):
                        n = j * K + k
                        c.wait(e, s_wl, n + 1)
                        c.wait(e, s_si, n)
                        rows(gps, k, 0, s_g)
                        c.wait(e, s_a, n)
                        rows(ups, k, 1, s_u)
                        c.wait(e, s_al, n)
                        down(ESLOT[k - 1], (k - 1) % K)
                c.wait(e, s_al, LAST)
                down(ZA, ZW)
                for n in range(NB):
                    c.wait(e, s_ye, KC)
                    yb = gps if n < NB // 2 else ups
                    for q in range(KC):
                        o = (n % 4) * D + q * P
                        mm = e.transpose(yb[:, o:o + P], yT[:, q, n * P:(n + 1) * P], g.ident[:, :])
                    if n % 2:
                        mm.then_inc(s_yt, 1)


def mamba_input(c, g, dram, hT):
    nc = c.nc
    s_w, s_mm, s_h = map(c.sem, ["mi_w", "mi_mm", "mi_h"])
    with ExitStack() as ctx:
        w = c.sb(ctx, "mi_wt", [P, KC, D])
        b = c.sb(ctx, "mi_b", [P, KC])
        ps = c.ps(ctx, "mi_ps", [P, KC, T])
        with nc.Block() as block:
            @block.sync
            def _(e):
                e.dma_start(w[:, :, :], dram["w_inT"].rearrange("(k p) n -> p k n", p=P)).then_inc(s_w, 16)
                e.dma_start(b[:, :], dram["b_in"]).then_inc(s_w, 16)

            @block.tensor
            def _(e):
                c.wait(e, s_w, 32)
                for m in range(KC):
                    for h in range(NH):
                        for k in range(KC):
                            mm = e.matmul(ps[:, m, h * HALF:(h + 1) * HALF], w[:, k, m * P:(m + 1) * P],
                                          g.feat[:, k, h * HALF:(h + 1) * HALF], start=k == 0, stop=k == KC - 1)
                    mm.then_inc(s_mm, 1)

            @block.scalar
            def _(e):
                for m in range(KC):
                    c.wait(e, s_mm, m + 1)
                    e.activation(hT[:, m, :], ps[:, m, :], ACT.Gelu, bias=b[:, m:m + 1]).then_inc(s_h, 1)


def mamba_project(c, g, dram, dr, rev, hT, w, xi, sz, dt, u, ctx0):
    nc = c.nc
    s_w, s_in, s_pad, s_cp, s_cv, s_xi, s_sz, s_xp, s_xe, s_bc, s_dm, s_ab, s_e1, s_l1, s_mx, s_dt, s_u, s_A = map(
        c.sem, [f"{dr}_{n}" for n in "w in pad cp cv xi sz xp xe bc dm ab e1 l1 mx dt u A".split()])
    with ExitStack() as ctx:
        win = c.sb(ctx, dr + "_win", [P, KC, 2 * DI])
        wxp = c.sb(ctx, dr + "_wxp", [P, DB, DTR + 2 * DS])
        wdt = c.sb(ctx, dr + "_wdt", [P, DI])
        cvw = c.sb(ctx, dr + "_cvw", [P, DB, DCONV])
        cvb = c.sb(ctx, dr + "_cvb", [P, DB])
        dtb = c.sb(ctx, dr + "_dtb", [P, DB])
        raw = c.sb(ctx, dr + "_raw", [P, 2, NSEQ * SEGC])
        cv = c.sb(ctx, dr + "_cv", [P, 2, T])
        dtr = c.sb(ctx, dr + "_dtr", [P, T])
        bcr = c.sb(ctx, dr + "_bcr", [2 * DS, T])
        sp = c.sb(ctx, dr + "_sp", [P, 3, T])
        ps = [c.ps(ctx, f"{dr}_ps{i}", [P, T]) for i in range(4)]
        NW = 9 * 16
        with nc.Block() as block:
            @block.sync
            def _(e):
                e.dma_start(win[:, :, :], dram[dr + "_in_wT"].rearrange("(k p) n -> p k n", p=P)).then_inc(s_w, 16)
                e.dma_start(wxp[:, :, :], dram[dr + "_xproj_wT"].rearrange("(k p) n -> p k n", p=P)).then_inc(s_w, 16)
                e.dma_start(wdt[:, :], dram[dr + "_dt_wT"]).then_inc(s_w, 16)
                e.dma_start(cvw[:, :, :], dram[dr + "_conv_w"].rearrange("(k p) n -> p k n", p=P)).then_inc(s_w, 16)
                e.dma_start(cvb[:, :], dram[dr + "_conv_b"]).then_inc(s_w, 16)
                e.dma_start(dtb[:, :], dram[dr + "_dt_b"]).then_inc(s_w, 16)
                e.dma_start(w.A[:, :, :], dram[dr + "_A_log"].rearrange("(k p) n -> p k n", p=P)).then_inc(s_w, 16)
                e.dma_start(w.Dv[:, :], dram[dr + "_D"]).then_inc(s_w, 16)
                e.dma_start(w.out[:, :, :], dram[dr + "_out_wT"].rearrange("(k p) n -> p k n", p=P)).then_inc(s_w, 16)
                c.wait(e, s_xe, 2)
                e.dma_start(dram["bc"], bcr[:, :]).then_inc(s_bc, 16)
                c.wait(e, s_bc, 16)

            @block.tensor
            def _(e):
                c.wait(e, s_w, NW)
                def in_proj(m):
                    if m >= 4:
                        c.wait(e, s_cp, m - 3)
                    for h in range(NH):
                        for k in range(KC):
                            mm = e.matmul(ps[m % 4][:, h * HALF:(h + 1) * HALF], win[:, k, m * P:(m + 1) * P],
                                          hT[:, k, h * HALF:(h + 1) * HALF], start=k == 0, stop=k == KC - 1)
                    mm.then_inc(s_in, 1)
                for m in range(8):
                    in_proj(m)
                c.wait(e, s_xi, DB)
                for i, (lo, hi) in enumerate([(0, DTR), (DTR, DTR + 2 * DS)]):
                    c.wait(e, s_sz, i + 1)
                    for h in range(NH):
                        for k in range(DB):
                            mm = e.matmul(ps[i][0:hi - lo, h * HALF:(h + 1) * HALF], wxp[:, k, lo:hi],
                                          xi[:, k, h * HALF:(h + 1) * HALF], start=k == 0, stop=k == DB - 1)
                    mm.then_inc(s_xp, 1)
                c.wait(e, s_xe, 1)
                for d in range(DB):
                    b = (d + 2) % 4
                    if d < 2:
                        c.wait(e, s_sz, d + 3)
                    else:
                        c.wait(e, s_xe, 2)
                    for h in range(NH):
                        mm = e.matmul(ps[b][:, h * HALF:(h + 1) * HALF], wdt[:, d * P:(d + 1) * P],
                                      dtr[:, h * HALF:(h + 1) * HALF], start=True, stop=True)
                    mm.then_inc(s_dm, 1)

            @block.gpsimd
            def _(e):
                e.memset(raw[:, :, :], 0.0).then_inc(s_pad, 1)
                for d in range(DB):
                    c.wait(e, s_l1, d + 1)
                    c.wait(e, s_mx, d + 1)
                    e.tensor_tensor(dt[:, d, :], dt[:, d, :], sp[:, 2, :], ALU.add).then_inc(s_dt, 1)
                    c.wait(e, s_dt, d + 1)
                    e.tensor_tensor(u[:, d, :], dt[:, d, :], xi[:, d, :], ALU.mult).then_inc(s_u, 1)

            @block.scalar
            def _(e):
                c.wait(e, s_pad, 1)
                def copy_in(m):
                    if m >= 2:
                        c.wait(e, s_cv, DCONV * (m - 1))
                    c.wait(e, s_in, m + 1)
                    e.activation(seq_view(raw[:, m % 2, :], SEGC, PADC), ps[m][:, :].rearrange("p (b s) -> p b s", s=SEQ),
                                 ACT.Copy).then_inc(s_cp, 1)

                def silu_x(m):
                    c.wait(e, s_cv, DCONV * (m + 1))
                    e.activation(xi[:, m, :], cv[:, m % 2, :], ACT.Silu).then_inc(s_xi, 1)

                def silu_z(m):
                    c.wait(e, s_in, DB + m + 1)
                    e.activation(sz[:, m, :], ps[m][:, :], ACT.Silu).then_inc(s_sz, 1)

                copy_in(0)
                copy_in(1)
                silu_x(0)
                copy_in(2)
                silu_x(1)
                copy_in(3)
                silu_x(2)
                silu_z(0)
                silu_x(3)
                silu_z(1)
                silu_z(2)
                silu_z(3)
                c.wait(e, s_w, NW)
                e.activation(w.A[:, :, :], w.A[:, :, :], ACT.Exp).then_inc(s_A, 1)
                for i, dst in enumerate([dtr[:, :], bcr[:, :]]):
                    c.wait(e, s_xp, i + 1)
                    e.activation(dst, ps[i][0:dst.shape[0], :], ACT.Copy).then_inc(s_xe, 1)
                for d in range(DB):
                    b = (d + 2) % 4
                    c.wait(e, s_dm, d + 1)
                    c.wait(e, s_e1, d)
                    e.activation(sp[:, 0, :], ps[b][:, :], ACT.Abs, bias=dtb[:, d:d + 1]).then_inc(s_ab, 1)
                    c.wait(e, s_ab, d + 1)
                    c.wait(e, s_l1, d)
                    e.activation(sp[:, 1, :], sp[:, 0, :], ACT.Exp, scale=-1.0).then_inc(s_e1, 1)
                    c.wait(e, s_e1, d + 1)
                    e.activation(dt[:, d, :], sp[:, 1, :], ACT.Ln, bias=1.0).then_inc(s_l1, 1)

            @block.vector
            def _(e):
                c.wait(e, s_w, NW)
                for m in range(DB):
                    c.wait(e, s_cp, m + 1)
                    if m >= 2:
                        c.wait(e, s_xi, m - 1)
                    out = cv[:, m % 2, :].rearrange("p (b s) -> p b s", s=SEQ)
                    for t in range(DCONV):
                        src = seq_view(raw[:, m % 2, :], SEGC, 2 * PADC - t if rev else t)
                        if t == 0:
                            e.tensor_scalar(out, src, cvw[:, m, 0:1], cvb[:, m:m + 1],
                                            ALU.mult, ALU.add).then_inc(s_cv, 1)
                        else:
                            c.wait(e, s_cv, m * DCONV + t)
                            e.scalar_tensor_tensor(out, src, cvw[:, m, t:t + 1], out,
                                                   ALU.mult, ALU.add).then_inc(s_cv, 1)
                c.wait(e, s_A, 1)
                e.tensor_scalar(w.A[:, :, :], w.A[:, :, :], -1.0, None, ALU.mult).then_inc(s_A, 1)
                for d in range(DB):
                    c.wait(e, s_ab, d + 1)
                    c.wait(e, s_dt, d)
                    e.tensor_scalar(sp[:, 2, :], ps[(d + 2) % 4][:, :], dtb[:, d:d + 1], 0.0,
                                    ALU.add, ALU.max).then_inc(s_mx, 1)


def mamba_scan(c, g, dram, dr, rev, w, xi, sz, dt, u, acc, last):
    nc = c.nc
    s_bb = [c.sem(f"{dr}_bb{i}") for i in range(2)]
    s_z, s_dd, s_y, s_om, s_oa = map(c.sem, [f"{dr}s_{n}" for n in "z dd y om oa".split()])
    s_da, = c.counters(dr, "s_da", nc.scalar)
    s_ub, = c.counters(dr, "s_ub", nc.gpsimd)
    s_sc, s_hc = c.counters(dr, "s_sc s_hc", nc.vector)
    s_ac, = c.counters(dr, "s_ac", nc.tensor)
    lo = 0 if rev else 1
    U = 2 * DB
    with ExitStack() as ctx:
        Bb = c.sb(ctx, dr + "_Bb", [P, 2, T])
        Cb = c.sb(ctx, dr + "_Cb", [P, 2, T])
        dA = c.sb(ctx, dr + "_dA", [P, 2, NSEQ * SEGS])
        uB = c.sb(ctx, dr + "_uB", [P, 2, NSEQ * SEGS])
        hh = c.sb(ctx, dr + "_hh", [P, 2, NSEQ * SEGS])
        hC = c.sb(ctx, dr + "_hC", [P, 2, T])
        dD = c.sb(ctx, dr + "_dD", [P, DB, P])
        with ExitStack() as pctx:
            y = [c.ps(pctx, f"{dr}_y{d}", [P, T]) for d in range(DB)]
            with nc.Block() as block:
                @block.sync
                def _(e):
                    with e.Fori(0, DS // 2) as j:
                        for q in range(2):
                            c.wait(e, s_hc, j * U)
                            e.dma_start(Bb[:, q, :], dram["bc"][bass.ds(2 * j + q, 1), :].broadcast_to([P, T])
                                        ).then_inc(s_bb[q], 16)
                            e.dma_start(Cb[:, q, :], dram["bc"][bass.ds(2 * j + q + DS, 1), :].broadcast_to([P, T])
                                        ).then_inc(s_bb[q], 16)

                @block.gpsimd
                def _(e):
                    e.memset(dA[:, :, :], 0.0).then_inc(s_z, 1)
                    e.memset(uB[:, :, :], 0.0).then_inc(s_z, 1)
                    c.wait(e, s_z, 2)
                    with e.Fori(0, DS // 2) as j:
                        for i in range(U):
                            n, q, d = j * U + i, i // DB, i % DB
                            if d == 0:
                                c.wait(e, s_bb[q], (j + 1) * 32)
                            c.wait(e, s_sc, n - 1 if i >= 2 else j * U)
                            e.tensor_tensor(seq_view(uB[:, i % 2, :], SEGS, lo),
                                            u[:, d, :].rearrange("p (b s) -> p b s", s=SEQ),
                                            Bb[:, q, :].rearrange("p (b s) -> p b s", s=SEQ),
                                            ALU.mult).then_inc(s_ub, 1)

                @block.scalar
                def _(e):
                    c.wait(e, s_z, 2)
                    with e.Fori(0, DS // 2) as j:
                        for i in range(U):
                            n, q, d = j * U + i, i // DB, i % DB
                            c.wait(e, s_sc, n - 1 if i >= 2 else j * U)
                            e.activation(seq_view(dA[:, i % 2, :], SEGS, lo),
                                         dt[:, d, :].rearrange("p (b s) -> p b s", s=SEQ), ACT.Exp,
                                         scale=w.A[:, d, bass.ds(2 * j + q, 1)]).then_inc(s_da, 1)

                @block.vector
                def _(e):
                    for d in range(DB):
                        e.tensor_scalar(dD[:, d, :], g.ident[:, :], w.Dv[:, d:d + 1], None, ALU.mult).then_inc(s_dd, 1)
                    with e.Fori(0, DS // 2) as j:
                        for i in range(U):
                            n, q, d, b = j * U + i, i // DB, i % DB, i % 2
                            c.wait(e, s_da, n + 1)
                            c.wait(e, s_ub, n + 1)
                            c.wait(e, s_hc, n - 1 if i >= 2 else j * U)
                            way = slice(None, None, -1) if rev else slice(None)
                            e.tensor_tensor_scan(hh[:, b, way], dA[:, b, way], uB[:, b, way], 0.0,
                                                 ALU.mult, ALU.add).then_inc(s_sc, 1)
                            if d == 0:
                                c.wait(e, s_bb[q], (j + 1) * 32)
                            c.wait(e, s_sc, n + 1)
                            c.wait(e, s_ac, n - 1 if i >= 2 else j * U)
                            e.tensor_tensor(hC[:, b, :].rearrange("p (b s) -> p b s", s=SEQ),
                                            seq_view(hh[:, b, :], SEGS, lo),
                                            Cb[:, q, :].rearrange("p (b s) -> p b s", s=SEQ),
                                            ALU.mult).then_inc(s_hc, 1)
                    for d in range(DB):
                        c.wait(e, s_ac, DS * DB)
                        e.tensor_tensor(u[:, d, :], y[d][:, :], sz[:, d, :], ALU.mult).then_inc(s_y, 1)

                @block.tensor
                def _(e):
                    c.wait(e, s_dd, DB)
                    for d in range(DB):
                        for h in range(NH):
                            e.matmul(y[d][:, h * HALF:(h + 1) * HALF], dD[:, d, :], xi[:, d, h * HALF:(h + 1) * HALF],
                                     start=True, stop=False, skip_group_check=True)
                    with e.Fori(0, DS // 2) as j:
                        for i in range(U):
                            n, d = j * U + i, i % DB
                            c.wait(e, s_hc, n + 1)
                            for h in range(NH):
                                mm = e.matmul(y[d][:, h * HALF:(h + 1) * HALF], g.ident[:, :],
                                              hC[:, i % 2, h * HALF:(h + 1) * HALF], start=False, stop=False,
                                              skip_group_check=True)
                            mm.then_inc(s_ac, 1)
        ops = c.ps(ctx, dr + "_ops", [P, KC, T])
        with nc.Block() as block:
            @block.tensor
            def _(e):
                for m in range(KC):
                    for h in range(NH):
                        for k in range(DB):
                            mm = e.matmul(ops[:, m, h * HALF:(h + 1) * HALF], w.out[:, k, m * P:(m + 1) * P],
                                          u[:, k, h * HALF:(h + 1) * HALF], start=k == 0, stop=k == DB - 1)
                    mm.then_inc(s_om, 1)

            @block.vector
            def _(e):
                for m in range(KC):
                    c.wait(e, s_om, m + 1)
                    e.tensor_tensor(acc[:, m, :], ops[:, m, :], acc[:, m, :], ALU.add).then_inc(s_oa, 1)


def to_tokens(c, g, name, feat, tok):
    nc = c.nc
    s_t, s_e = c.sem(name + "_t"), c.sem(name + "_e")
    with ExitStack() as ctx:
        ps = c.ps(ctx, name + "_ps", [P, NB, D])
        with nc.Block() as block:
            @block.tensor
            def _(e):
                for n in range(NB):
                    for k in range(KC):
                        mm = e.transpose(ps[:, n, k * P:(k + 1) * P], feat[:, k, n * P:(n + 1) * P], g.ident[:, :])
                    mm.then_inc(s_t, 1)

            @block.scalar
            def _(e):
                for q in range(2):
                    c.wait(e, s_t, 4 * (q + 1))
                    e.activation(tok[:, 4 * q:4 * q + 4, :], ps[:, 4 * q:4 * q + 4, :], ACT.Copy).then_inc(s_e, 1)


def mamba_output(c, g, dram):
    nc = c.nc
    s_w, s_mm, s_b, s_x = map(c.sem, ["mo_w", "mo_mm", "mo_b", "mo_x"])
    with ExitStack() as ctx:
        w = c.sb(ctx, "mo_wt", [P, KC, D])
        b = c.sb(ctx, "mo_bb", [P, D])
        ps = c.ps(ctx, "mo_ps", [P, NB, D])
        with nc.Block() as block:
            @block.sync
            def _(e):
                e.dma_start(w[:, :, :], dram["w_outT"].rearrange("(k p) n -> p k n", p=P)).then_inc(s_w, 16)
                e.dma_start(b[:, :], dram["b_out"].broadcast_to([P, D])).then_inc(s_w, 16)

            @block.tensor
            def _(e):
                c.wait(e, s_w, 32)
                for n in range(NB):
                    for k in range(KC):
                        mm = e.matmul(ps[:, n, :], g.feat[:, k, n * P:(n + 1) * P], w[:, k, :],
                                      start=k == 0, stop=k == KC - 1)
                    if n % 2:
                        mm.then_inc(s_mm, 1)

            @block.gpsimd
            def _(e):
                c.wait(e, s_w, 32)
                e.tensor_tensor(g.x[:, :, :], g.x[:, :, :], b[:, :].unsqueeze(1).broadcast_to([P, NB, D]),
                                ALU.add).then_inc(s_b, 1)

            @block.vector
            def _(e):
                c.wait(e, s_b, 1)
                for n in range(NB):
                    c.wait(e, s_mm, n // 2 + 1)
                    e.tensor_tensor(g.x[:, n, :], ps[:, n, :], g.x[:, n, :], ALU.add).then_inc(s_x, 1)


def table_ffn(c, g, out):
    nc = c.nc
    s_g, s_u, s_si, s_a, s_y, s_x, s_o = map(c.sem, [f"ff_{n}" for n in "g u si a y x o".split()])
    M = len(FB)
    wg = g.lutw[:, 0:KC * FI].rearrange("p (k n) -> p k n", k=KC)
    wu = g.lutw[:, KC * FI:2 * KC * FI].rearrange("p (k n) -> p k n", k=KC)
    wd = g.lutw[:, 2 * KC * FI:LUTW].rearrange("p (m n) -> p m n", m=M)
    with ExitStack() as ctx:
        si = c.sb(ctx, "ff_si", [P, 2, T])
        a = c.sb(ctx, "ff_a", [P, M, T])
        ps = [c.ps(ctx, f"ff_p{i}", [P, T]) for i in range(4)]
        with nc.Block() as block:
            @block.tensor
            def _(e):
                for m, (o, r) in enumerate(FB):
                    for w, b, sem in ((wg, 2 * (m % 2), s_g), (wu, 2 * (m % 2) + 1, s_u)):
                        if m >= 2:
                            c.wait(e, s_a, m - 1)
                        for h in range(NH):
                            for k in range(KC):
                                mm = e.matmul(ps[b][0:r, h * HALF:(h + 1) * HALF], w[:, k, o:o + r],
                                              g.feat[:, k, h * HALF:(h + 1) * HALF], start=k == 0, stop=k == KC - 1)
                        mm.then_inc(sem, 1)
                c.wait(e, s_a, M)
                for n in range(NB):
                    for m, (o, r) in enumerate(FB):
                        mm = e.matmul(ps[n // 4][:, (n % 4) * D:(n % 4 + 1) * D], a[0:r, m, n * P:(n + 1) * P],
                                      wd[0:r, m, :], start=m == 0, stop=m == M - 1)
                    if n % 2:
                        mm.then_inc(s_y, 1)

            @block.scalar
            def _(e):
                for m, (o, r) in enumerate(FB):
                    c.wait(e, s_g, m + 1)
                    if m >= 2:
                        c.wait(e, s_a, m - 1)
                    e.activation(si[0:r, m % 2, :], ps[2 * (m % 2)][0:r, :], ACT.Silu).then_inc(s_si, 1)

            @block.vector
            def _(e):
                for m, (o, r) in enumerate(FB):
                    c.wait(e, s_si, m + 1)
                    c.wait(e, s_u, m + 1)
                    e.tensor_tensor(a[0:r, m, :], ps[2 * (m % 2) + 1][0:r, :], si[0:r, m % 2, :],
                                    ALU.mult).then_inc(s_a, 1)
                for n in range(NB):
                    c.wait(e, s_y, n // 2 + 1)
                    e.tensor_tensor(g.x[:, n, :], ps[n // 4][:, (n % 4) * D:(n % 4 + 1) * D], g.x[:, n, :],
                                    ALU.add).then_inc(s_x, 1)

            @block.sync
            def _(e):
                for n in range(NB):
                    c.wait(e, s_x, n + 1)
                    e.dma_start(out[n * P:(n + 1) * P, :], g.x[:, n, :]).then_inc(s_o, 16)
                c.wait(e, s_o, NB * 16)


class Shared:
    pass


def build(nc, dram, out, stop=None):
    with ExitStack() as ctx:
        c = Core(nc, ctx)
        g = Shared()
        g.x = c.sb(ctx, "x", [P, NB, D])
        g.feat = c.sb(ctx, "feat", [P, KC, T])
        g.lutw = c.sb(ctx, "lutw", [P, MOE_K * LCH])
        g.ident = c.sb(ctx, "ident", [P, P])
        g.gmask = c.sb(ctx, "gmask", [P, 8])
        g.iota_e = c.sb(ctx, "iota_e", [P, NEXP])
        g.iota_l = c.sb(ctx, "iota_l", [P, LUT])
        g.lutb = c.sb(ctx, "lutb", [P, LUT])
        dram["cw"] = nc.dram_tensor("cw_rows", (NCW, T), F32, kind="Internal").ap()
        dram["bc"] = nc.dram_tensor("bc_rows", (2 * DS, T), F32, kind="Internal").ap()
        s_x = [c.sem(f"x_in{n}") for n in range(NB)]
        for n in range(NB):
            nc.sync.dma_start(g.x[:, n, :], dram["x"][n * P:(n + 1) * P, :]).then_inc(s_x[n], 16)
        constants(c, g)
        layernorm(c, g, "ln1", g.x, g.feat, loads=s_x)
        attention(c, g, dram)
        with ExitStack() as moe:
            g.lut_f = c.sb(moe, "lut_f", [P, MOE_K * LCH])
            xh = c.sb(moe, "xh", [P, KC, T], F32R)
            xl = c.sb(moe, "xl", [P, KC, T], F32R)
            layernorm(c, g, "ln2", g.x, g.feat, hi=xh, lo=xl)
            with ExitStack() as idx:
                g.lut_i = c.sb(idx, "lut_i", [P, LUTW], I32)
                routing(c, g, dram, None)
            experts(c, g, dram, xh, xl)
        c.recycle()
        layernorm(c, g, "ln3", g.x, g.feat)
        with ExitStack() as mm:
            hT = c.sb(mm, "hT", [P, KC, T])
            acc = c.sb(mm, "acc", [P, KC, T])
            gb = c.sb(mm, "gb", [P, 2, KC])
            w = Shared()
            w.A = c.sb(mm, "A", [P, DB, DS])
            w.Dv = c.sb(mm, "Dv", [P, DB])
            w.out = c.sb(mm, "w_o", [P, DB, D])
            xi = c.sb(mm, "xi", [P, DB, T])
            sz = c.sb(mm, "sz", [P, DB, T])
            dt = c.sb(mm, "dt", [P, DB, T])
            u = c.sb(mm, "u", [P, DB, T])
            mamba_input(c, g, dram, hT)
            s_hc, s_gb = c.sem("h_copy"), c.sem("gb_in")
            with nc.Block() as block:
                @block.vector
                def _(e):
                    e.tensor_copy(acc[:, :, :], hT[:, :, :]).then_inc(s_hc, 1)

                @block.sync
                def _(e):
                    e.dma_start(gb[:, 0, :], dram["ln_g"]).then_inc(s_gb, 16)
                    e.dma_start(gb[:, 1, :], dram["ln_b"]).then_inc(s_gb, 16)
                    c.wait(e, s_gb, 32)
            for dr, rev in (("fm", False), ("bm", True)):
                mamba_project(c, g, dram, dr, rev, hT, w, xi, sz, dt, u, mm)
                mamba_scan(c, g, dram, dr, rev, w, xi, sz, dt, u, acc, dr == "bm")
                c.recycle()
            rt = c.sb(mm, "r_tok", [P, NB, D])
            to_tokens(c, g, "rt_tok", acc, rt)
            layernorm(c, g, "lnm", rt, g.feat, gamma=gb[:, 0, :], beta=gb[:, 1, :])
        mamba_output(c, g, dram)
        layernorm(c, g, "ln4", g.x, g.feat)
        table_ffn(c, g, out)


def kernel(**inputs):
    import numpy as np
    import concourse.bacc as bacc
    from concourse.bass_utils import run_bass_kernel_spmd

    f = {k: np.asarray(v) for k, v in inputs.items()}

    def columns(v):
        return v.reshape(-1, P).T

    def by_hidden(gate, up, down, count):
        rows = count * P
        flat = [w.transpose(1, 0, 2).reshape(KC, P, count, P).transpose(2, 1, 0, 3).reshape(count, P, KC * P)
                for w in (gate, up)]
        return np.concatenate(flat + [down.reshape(rows, D).reshape(count, P, D)], axis=2)

    large = by_hidden(f["L0_ffn_Wg"], f["L0_ffn_Wu"], f["L0_ffn_Wd"], EB).reshape(MOE_IT, 3, P, MOE_WN)
    small = by_hidden(f["L0_ffn_cWg"], f["L0_ffn_cWu"], f["L0_ffn_cWd"], NCH).reshape(MOE_IT, 2, P, MOE_WN)
    moe = np.concatenate([large, small], axis=1).reshape(MOE_IT * MOE_K, P, MOE_WN)
    moe = np.concatenate([moe, moe[:1]], axis=0)

    def table_rows(idx):
        return idx.T.reshape(KC, P, FI).transpose(1, 0, 2).reshape(P, KC * FI)

    down = np.zeros((len(FB) * P, D), f["L1_ffn_down_idx"].dtype)
    down[:FI] = f["L1_ffn_down_idx"].T
    down = down.reshape(len(FB), P, D).transpose(1, 0, 2).reshape(P, len(FB) * D)
    arrays = {
        "x": f["L0_attn_x"].reshape(T, D), "Wqkv": f["L0_attn_Wqkv"], "bqkv": f["L0_attn_bqkv"].reshape(-1, 1),
        "Wout": f["L0_attn_Wout"], "bout": f["L0_attn_bout"].reshape(1, D), "gate_wT": f["L0_ffn_gate_w"].T,
        "moe_w": moe, "lut": f["L1_ffn_lut"].reshape(1, LUT),
        "lut_idx": np.concatenate([table_rows(f["L1_ffn_gate_idx"]), table_rows(f["L1_ffn_up_idx"]), down], axis=1),
        "w_inT": f["L1_attn_w_in"].T, "b_in": columns(f["L1_attn_b_in"]),
        "ln_g": columns(f["L1_attn_ln_g"]), "ln_b": columns(f["L1_attn_ln_b"]),
        "w_outT": f["L1_attn_w_out"].T, "b_out": f["L1_attn_b_out"].reshape(1, D),
    }
    for dr in ("fm", "bm"):
        n = f"L1_attn_{dr}_"
        arrays |= {
            dr + "_in_wT": f[n + "in_w"].T, dr + "_xproj_wT": f[n + "xproj_w"].T, dr + "_dt_wT": f[n + "dt_w"].T,
            dr + "_conv_w": f[n + "conv_w"], dr + "_conv_b": columns(f[n + "conv_b"]),
            dr + "_dt_b": columns(f[n + "dt_b"]), dr + "_A_log": f[n + "A_log"], dr + "_D": columns(f[n + "D"]),
            dr + "_out_wT": f[n + "out_w"].T,
        }
    nc = bacc.Bacc("TRN2", target_bir_lowering=False, num_devices=1)
    arrays = {f"in_{k}": np.ascontiguousarray(v) for k, v in arrays.items()}
    dram = {k[3:]: nc.dram_tensor(k, v.shape, mybir.dt.from_np(v.dtype), kind="ExternalInput").ap()
            for k, v in arrays.items()}
    out = nc.dram_tensor("out", (T, D), F32, kind="ExternalOutput").ap()
    build(nc, dram, out)
    r = run_bass_kernel_spmd(nc, [arrays], core_ids=[0])
    return r.results[0]["out"].reshape(NSEQ, SEQ, D)
```

```python
from contextlib import ExitStack

import concourse.bass as bass
from concourse import mybir

ALU = mybir.AluOpType
ACT = mybir.ActivationFunctionType
AX = mybir.AxisListType
F32 = mybir.dt.float32
F32R = mybir.dt.float32r
U32 = mybir.dt.uint32
I32 = mybir.dt.int32

P = 128
D = 256
KC = D // P
NSEQ, SEQ = 4, 256
T = NSEQ * SEQ
NB = T // P
HALF = 512
NH = T // HALF
EPS = 1e-5

HEADS, GROUPS, HD = 16, 4, 16
KV = GROUPS * HD
HJ = HEADS // GROUPS
QB = SEQ // P

NEXP, TOPK, INTER = 32, 4, 96
NCH, CINTER = 16, 128
SMALL = 0.05
EB = NEXP * INTER // P
MOE_IT = 8
MOE_K = 5
MOE_WN = 2 * KC * P + D
ESLOT = [0, 1, 0, 1, 2]
NCW = NEXP + NCH

DI, DS, DCONV, DTR = 512, 16, 4, 128
DB = DI // P
PADC = DCONV - 1
SEGC = SEQ + 2 * PADC
SEGS = SEQ + 1

FI = 688
FB = [(m * P, min(P, FI - m * P)) for m in range((FI + P - 1) // P)]
LUT = 16
LUTW = KC * FI * 2 + len(FB) * D
LCH = 860
assert MOE_K * LCH >= LUTW and 2 * MOE_IT == LUT


START = 3


class Core:

    def __init__(self, nc, ctx):
        self.nc, self.ctx, self.used, self.offset = nc, ctx, [], []

    def sem(self, name):
        self.used.append(self.nc.alloc_semaphore(name=name))
        return self.used[-1]

    def counters(self, prefix, names, by):
        found = [self.sem(prefix + n) for n in names.split()]
        for s in found:
            by.sem_inc(s, START)
        self.offset += [s.name for s in found]
        return found

    def wait(self, e, s, count):
        e.wait_ge(s, count + START if s.name in self.offset else count)

    def kept(self, name):
        return self.nc.alloc_semaphore(name=name)

    def recycle(self):
        self.nc.clear_and_free_semaphores(self.used)
        self.used, self.offset = [], []
        self.nc.all_engine_barrier()

    def sb(self, ctx, name, shape, dt=F32):
        return ctx.enter_context(self.nc.sbuf_tensor(name, shape, dt))

    def ps(self, ctx, name, shape):
        return ctx.enter_context(self.nc.psum_tensor(name, shape, F32))


def seq_view(ap, seg, lo):
    return ap.rearrange("p (b s) -> p b s", s=seg)[:, :, lo:lo + SEQ]


def constants(c, g):
    nc = c.nc
    s_set, s_const = c.sem("s_set"), c.sem("s_const")
    with nc.Block() as block:
        @block.gpsimd
        def _(e):
            e.memset(g.ident[:, :], 0.0).then_inc(s_set, 1)
            e.memset(g.gmask[:, :], 1.0).then_inc(s_set, 1)
            e.iota(g.iota_e[:, :], [[1, NEXP]], base=0, channel_multiplier=0,
                   allow_small_or_imprecise_dtypes=True).then_inc(s_const, 1)
            e.iota(g.iota_l[:, :], [[1, LUT]], base=0, channel_multiplier=0,
                   allow_small_or_imprecise_dtypes=True).then_inc(s_const, 1)
            c.wait(e, s_set, 2)
            e.affine_select(out=g.ident[:, :], in_=g.ident[:, :], compare_op=ALU.not_equal, fill=1.0,
                            base=0, pattern=[[-1, P]], channel_multiplier=1).then_inc(s_const, 1)
            e.affine_select(out=g.gmask[:, :], in_=g.gmask[:, :], compare_op=ALU.is_ge, fill=0.0,
                            base=0, pattern=[[-HD, 8]], channel_multiplier=1).then_inc(s_set, 1)
            c.wait(e, s_set, 3)
            e.affine_select(out=g.gmask[:, :], in_=g.gmask[:, :], compare_op=ALU.is_ge, fill=0.0,
                            base=HD - 1, pattern=[[HD, 8]], channel_multiplier=-1).then_inc(s_const, 1)
            c.wait(e, s_const, 4)


def layernorm(c, g, name, src, feat, gamma=None, beta=None, hi=None, lo=None, loads=None):
    nc = c.nc
    sem = lambda n: c.sem(f"{name}_{n}")
    s_stat, s_aggr, s_var, s_sd, s_r, s_xn, s_tp, s_ev, s_hi, s_lo = map(
        sem, "stat aggr var sd r xn tp ev hi lo".split())
    with ExitStack() as ctx:
        stats = c.sb(ctx, name + "_stats", [P, NB, 6])
        mv = c.sb(ctx, name + "_mv", [P, NB, 2])
        sm = c.sb(ctx, name + "_sm", [P, 5, NB])
        xn = c.sb(ctx, name + "_xn", [P, NB, D])
        ps = c.ps(ctx, name + "_ps", [P, KC, T])
        var, sd, r, q = (sm[:, i, :] for i in range(4))
        vector_copies = [1] if gamma is None and hi is None else []
        with nc.Block() as block:
            @block.vector
            def _(e):
                for n in range(NB):
                    if loads:
                        c.wait(e, loads[n], 16)
                    e.bn_stats(stats[:, n, :], src[:, n, :]).then_inc(s_stat, 1)
                for n in range(NB):
                    c.wait(e, s_stat, n + 1)
                    e.bn_aggr(mv[:, n, :], stats[:, n, :]).then_inc(s_aggr, 1)
                c.wait(e, s_aggr, NB)
                e.tensor_scalar(var, mv[:, :, 1], EPS, None, ALU.add).then_inc(s_var, 1)
                c.wait(e, s_sd, 1)
                e.reciprocal(r, sd).then_inc(s_r, 1)
                c.wait(e, s_r, 1)
                e.tensor_tensor(q, r, r, ALU.mult).then_inc(s_r, 1)
                c.wait(e, s_r, 2)
                e.tensor_tensor(q, q, var, ALU.mult).then_inc(s_r, 1)
                c.wait(e, s_r, 3)
                e.tensor_scalar(q, q, -0.5, 1.5, ALU.mult, ALU.add).then_inc(s_r, 1)
                c.wait(e, s_r, 4)
                e.tensor_tensor(r, r, q, ALU.mult).then_inc(s_r, 1)
                c.wait(e, s_r, 5)
                for n in range(NB):
                    e.tensor_scalar(xn[:, n, :], src[:, n, :], mv[:, n, 0:1], r[:, n:n + 1],
                                    ALU.subtract, ALU.mult).then_inc(s_xn, 1)
                for k in vector_copies:
                    c.wait(e, s_tp, NB * (k + 1))
                    e.tensor_copy(feat[:, k, :], ps[:, k, :]).then_inc(s_ev, 1)
                for k in range(KC):
                    if lo is not None:
                        c.wait(e, s_hi, k + 1)
                        c.wait(e, s_ev, k + 1)
                        e.tensor_tensor(lo[:, k, :], feat[:, k, :], hi[:, k, :].bitcast(F32),
                                        ALU.subtract).then_inc(s_lo, 1)

            @block.scalar
            def _(e):
                c.wait(e, s_var, 1)
                e.activation(sd, var, ACT.Sqrt).then_inc(s_sd, 1)
                for k in range(KC):
                    if k in vector_copies:
                        continue
                    c.wait(e, s_tp, NB * (k + 1))
                    if gamma is None:
                        e.activation(feat[:, k, :], ps[:, k, :], ACT.Copy).then_inc(s_ev, 1)
                    else:
                        e.activation(feat[:, k, :], ps[:, k, :], ACT.Identity, bias=beta[:, k:k + 1],
                                     scale=gamma[:, k:k + 1]).then_inc(s_ev, 1)
                    if hi is not None:
                        e.activation(hi[:, k, :], ps[:, k, :], ACT.Copy).then_inc(s_hi, 1)

            @block.tensor
            def _(e):
                for k in range(KC):
                    for n in range(NB):
                        c.wait(e, s_xn, n + 1)
                        e.transpose(ps[:, k, n * P:(n + 1) * P], xn[:, n, k * P:(k + 1) * P],
                                    g.ident[:, :]).then_inc(s_tp, 1)


def attention(c, g, wt):
    nc = c.nc
    sem = c.sem
    s_q, s_k, s_v, s_qh, s_ql, s_kf, s_kh, s_kl, s_ke, s_kd, s_ve, s_km, s_xb = map(
        sem, [f"at_{n}" for n in "q k v qh ql kf kh kl ke kd ve km xb".split()])
    s_vz = c.sem("at_vz")
    s_qc, s_vc, s_pn = c.counters("at_", "qc vc pn", nc.gpsimd)
    s_sc, s_pt, s_pv, s_op = c.counters("at_", "sc pt pv op", nc.tensor)
    s_mx, s_nm, s_pe, s_ri, s_x = c.counters("at_", "mx nm pe ri x", nc.vector)
    s_ex, s_oe, s_qd = c.counters("at_", "ex oe qd", nc.scalar)
    NP = 3
    PAIR = 2
    G = PAIR * QB
    U = G * HJ
    with ExitStack() as ctx:
        qs = c.sb(ctx, "qs", [P, HJ, T], F32R)
        kh = c.sb(ctx, "kh", [P, GROUPS, T], F32R)
        kl = c.sb(ctx, "kl", [P, GROUPS, T], F32R)
        v = c.sb(ctx, "v", [P, NB, KV])
        with ExitStack() as pctx:
            kf = c.sb(pctx, "kf", [P, T])
            khf = c.sb(pctx, "khf", [P, T], F32R)
            klf = c.sb(pctx, "klf", [P, T])
            m2 = c.sb(pctx, "m2", [P, GROUPS])
            qps = [c.ps(pctx, f"qps{i}", [P, T]) for i in range(2)]
            kps = c.ps(pctx, "kps", [P, T])
            vps = c.ps(pctx, "vps", [P, NB, KV])
            with nc.Block() as block:
                @block.tensor
                def _(e):
                    c.wait(e, wt.at_in, wt.at_n)
                    def rows(ps, w):
                        for h in range(NH):
                            for k in range(KC):
                                mm = e.matmul(ps[:, h * HALF:(h + 1) * HALF], w[:, k, :],
                                              g.feat[:, k, h * HALF:(h + 1) * HALF], start=k == 0, stop=k == KC - 1)
                        return mm
                    rows(kps, wt.wk2).then_inc(s_k, 1)
                    for j in range(HJ):
                        if j >= 2:
                            c.wait(e, s_ql, j - 1)
                        rows(qps[j % 2], wt.wq2[:, :, j * P:(j + 1) * P]).then_inc(s_q, 1)
                    for n in range(NB):
                        for k in range(KC):
                            mm = e.matmul(vps[:, n, :], g.feat[:, k, n * P:(n + 1) * P], wt.wv[:, k, :],
                                          start=k == 0, stop=k == KC - 1)
                    mm.then_inc(s_v, 1)

                @block.gpsimd
                def _(e):
                    e.tensor_tensor(m2[:, :], g.gmask[:, 0:GROUPS], g.gmask[:, GROUPS:], ALU.add).then_inc(s_km, 1)
                    c.wait(e, wt.at_in, wt.at_n)
                    e.tensor_tensor(g.x[:, :, :], g.x[:, :, :],
                                    wt.bout[:, :].unsqueeze(1).broadcast_to([P, NB, D]), ALU.add).then_inc(s_xb, 1)

                @block.vector
                def _(e):
                    c.wait(e, s_k, 1)
                    e.tensor_scalar(kf[:, :], kps[:, :], wt.bk[:, 0:1], None, ALU.add).then_inc(s_kf, 1)
                    c.wait(e, s_kh, 1)
                    e.tensor_tensor(klf[:, :], kf[:, :], khf[:, :].bitcast(F32), ALU.subtract).then_inc(s_kl, 1)
                    c.wait(e, s_kl, 1)
                    c.wait(e, s_km, 1)
                    for i in range(GROUPS):
                        e.tensor_scalar(kl[:, i, :], klf[:, :], m2[:, i:i + 1], None, ALU.mult).then_inc(s_kd, 1)
                        c.wait(e, s_qh, i + 1)
                        e.scalar_tensor_tensor(qs[KV:P, i, :], qps[i % 2][KV:P, :], wt.bq2[KV:P, i:i + 1],
                                               qs[KV:P, i, :].bitcast(F32), ALU.add, ALU.subtract).then_inc(s_ql, 1)
                    c.wait(e, s_v, 1)
                    e.tensor_tensor(v[:, :, :], vps[:, :, :],
                                    wt.bv[:, :].unsqueeze(1).broadcast_to([P, NB, KV]), ALU.add).then_inc(s_ve, 1)

                @block.scalar
                def _(e):
                    c.wait(e, s_kf, 1)
                    e.activation(khf[:, :], kf[:, :], ACT.Copy).then_inc(s_kh, 1)
                    c.wait(e, s_km, 1)
                    for j in range(HJ):
                        c.wait(e, s_q, j + 1)
                        e.activation(qs[:, j, :], qps[j % 2][:, :], ACT.Identity,
                                     bias=wt.bq2[:, j:j + 1]).then_inc(s_qh, 1)
                        c.wait(e, s_kh, 1)
                        e.activation(kh[:, j, :], khf[:, :].bitcast(F32), ACT.Copy,
                                     scale=m2[:, j:j + 1]).then_inc(s_ke, 1)

        qcur = c.sb(ctx, "qcur", [P, HJ, PAIR * SEQ], F32R)
        vcur = c.sb(ctx, "vcur", [P, PAIR * QB, GROUPS, KV])
        prob = c.sb(ctx, "prob", [P, NP, GROUPS, SEQ])
        pT = c.sb(ctx, "pT", [P, 2, QB, GROUPS, P])
        mx = c.sb(ctx, "mx", [P, 2, U, GROUPS])
        rs = c.sb(ctx, "rs", [P, U, GROUPS])
        ri = c.sb(ctx, "ri", [P, U, GROUPS])
        oT = c.sb(ctx, "oT", [P, 2, KC, P])
        sps = c.ps(ctx, "sps", [P, 2, GROUPS, SEQ])
        tps = c.ps(ctx, "tps", [P, QB, GROUPS, P])
        ops = c.ps(ctx, "ops", [P, HALF])
        mps = c.ps(ctx, "mps", [P, HALF])
        steps = range(U + 8)

        def query_block(t, after):
            n, rest = divmod(t - after - (HJ - 1), HJ)
            return [n] if rest == 0 and 0 <= n < G else []

        with nc.Block() as block:
            @block.gpsimd
            def _(e):
                e.memset(vcur[:, :, :, :], 0.0).then_inc(s_vz, 1)
                c.wait(e, s_vz, 1)
                with e.Fori(0, NSEQ // PAIR) as b:
                    c.wait(e, s_pv, b * U)
                    for gg in range(GROUPS):
                        e.tensor_copy(vcur[:, :, gg, gg * HD:(gg + 1) * HD],
                                      v[:, bass.ds(b * (PAIR * QB), PAIR * QB), gg * HD:(gg + 1) * HD]
                                      ).then_inc(s_vc, 1)
                    c.wait(e, s_sc, b * U)
                    e.tensor_copy(qcur[:, :, SEQ:], qs[:, :, bass.ds(b * (PAIR * SEQ) + SEQ, SEQ)].bitcast(F32)
                                  ).then_inc(s_qc, 1)
                    for u in range(U):
                        c.wait(e, s_ri, b * U + (u + 1))
                        e.tensor_tensor(prob[:, u % NP, :, :], prob[:, u % NP, :, :],
                                        ri[:, u, :].unsqueeze(2).broadcast_to([P, GROUPS, SEQ]), ALU.mult
                                        ).then_inc(s_pn, 1)

            @block.tensor
            def _(e):
                with e.Fori(0, NSEQ // PAIR) as b:
                    def scores(u):
                        qb, j = divmod(u, HJ)
                        if u == 0:
                            c.wait(e, s_qd, b + 1)
                        if u == U // PAIR:
                            c.wait(e, s_qc, b + 1)
                        c.wait(e, s_ex, b * U + (u - 1))
                        for gg in range(0, GROUPS, 2):
                            for i, k in enumerate((kh, kl)):
                                mm = e.matmul(sps[:, u % 2, gg:gg + 2, :], qcur[:, j, qb * P:(qb + 1) * P],
                                              k[:, gg:gg + 2, bass.ds(b * (PAIR * SEQ) + qb // QB * SEQ, SEQ)],
                                              start=i == 0, stop=i == 1)
                        mm.then_inc(s_sc, 1)

                    def turn(u):
                        c.wait(e, s_pn, b * U + (u + 1))
                        c.wait(e, s_pe, b * U + u)
                        for kb in range(QB):
                            for gg in range(GROUPS):
                                mm = e.transpose(tps[:, kb, gg, :], prob[:, u % NP, gg, kb * P:(kb + 1) * P],
                                                 g.ident[:, :])
                        mm.then_inc(s_pt, 1)

                    def values(u):
                        qb, j = divmod(u, HJ)
                        c.wait(e, s_pe, b * U + (u + 1))
                        if u == 0:
                            c.wait(e, s_vc, (b + 1) * GROUPS)
                        if j == 0:
                            c.wait(e, s_oe, b * G + qb)
                        r0 = j % 2 * KV
                        terms = [(gg, kb) for gg in range(GROUPS) for kb in range(QB)]
                        for i, (gg, kb) in enumerate(terms):
                            mm = e.matmul(ops[r0:r0 + KV, j // 2 * P:(j // 2 + 1) * P],
                                          vcur[:, qb // QB * QB + kb, gg, :], pT[:, u % 2, kb, gg, :],
                                          start=i == 0, stop=i == len(terms) - 1)
                        mm.then_inc(s_pv, 1)

                    def out_proj(q):
                        c.wait(e, s_oe, b * G + (q + 1))
                        c.wait(e, s_x, b * G + q)
                        for k in range(KC):
                            mm = e.matmul(mps[:, 0:D], oT[:, q % 2, k, :], wt.wout[:, k, :],
                                          start=k == 0, stop=k == KC - 1)
                        mm.then_inc(s_op, 1)

                    for t in steps:
                        if t < U:
                            scores(t)
                        if 2 <= t <= U + 1:
                            turn(t - 2)
                        if 3 <= t <= U + 2:
                            values(t - 3)
                        for q in query_block(t, 4):
                            out_proj(q)

            @block.vector
            def _(e):
                with e.Fori(0, NSEQ // PAIR) as b:
                    def maximum(u):
                        c.wait(e, s_sc, b * U + (u + 1))
                        if u == 0:
                            c.wait(e, s_ex, b * U)
                        e.tensor_reduce(mx[:, 0, u, :], sps[:, u % 2, :, :], AX.X, ALU.max).then_inc(s_mx, 1)
                        c.wait(e, s_mx, b * U + (u + 1))
                        e.tensor_scalar(mx[:, 1, u, :], mx[:, 0, u, :], -1.0 / HD, None, ALU.mult).then_inc(s_nm, 1)

                    def inverse(u):
                        c.wait(e, s_ex, b * U + (u + 1))
                        if u == 0:
                            c.wait(e, s_pn, b * U)
                        e.reciprocal(ri[:, u, :], rs[:, u, :]).then_inc(s_ri, 1)

                    def copy_out(u):
                        c.wait(e, s_pt, b * U + (u + 1))
                        c.wait(e, s_pv, b * U + (u - 1))
                        e.tensor_copy(pT[:, u % 2, :, :, :], tps[:, :, :, :]).then_inc(s_pe, 1)

                    def residual(q):
                        c.wait(e, s_op, b * G + (q + 1))
                        xs = g.x[:, bass.ds(b * G + q, 1), :].rearrange("p a d -> p (a d)")
                        e.tensor_tensor(xs, mps[:, 0:D], xs, ALU.add).then_inc(s_x, 1)

                    for t in steps:
                        if t < U:
                            maximum(t)
                        if 1 <= t <= U:
                            inverse(t - 1)
                        if 2 <= t <= U + 1:
                            copy_out(t - 2)
                        for q in query_block(t, 5):
                            residual(q)

            @block.scalar
            def _(e):
                with e.Fori(0, NSEQ // PAIR) as b:
                    def exps(u):
                        c.wait(e, s_nm, b * U + (u + 1))
                        c.wait(e, s_pt, b * U + (u - NP + 1 if u >= NP else 0))
                        if u == 0:
                            c.wait(e, s_ri, b * U)
                        for gg in range(GROUPS):
                            a = e.activation(prob[:, u % NP, gg, :], sps[:, u % 2, gg, :], ACT.Exp,
                                             bias=mx[:, 1, u, gg:gg + 1], scale=1.0 / HD,
                                             accum_out=rs[:, u, gg:gg + 1])
                        a.then_inc(s_ex, 1)

                    def heads_out(q):
                        c.wait(e, s_pv, b * U + (q + 1) * HJ)
                        c.wait(e, s_op, b * G + (q - 1))
                        e.activation(oT[:, q % 2, :, :].rearrange("p k t -> p (k t)"), ops[:, 0:KC * P],
                                     ACT.Copy).then_inc(s_oe, 1)

                    c.wait(e, s_sc, b * U)
                    e.activation(qcur[:, :, 0:SEQ], qs[:, :, bass.ds(b * (PAIR * SEQ), SEQ)].bitcast(F32),
                                 ACT.Copy).then_inc(s_qd, 1)
                    for t in steps:
                        if t < U:
                            exps(t)
                        for q in query_block(t, 3):
                            heads_out(q)


def routing(c, g, dram, wt):
    nc = c.nc
    s_lg, s_le, s_m8, s_ix, s_if, s_eq, s_mk, s_sh, s_ex, s_me, s_sm, s_rc, s_cw, s_pr, s_tp, s_te, s_st, s_li = map(
        c.sem, [f"rt_{n}" for n in "lg le m8 ix if eq mk sh ex me sm rc cw pr tp te st li".split()])
    with ExitStack() as ctx:
        lg = c.sb(ctx, "lg", [P, NB, NEXP])
        m8 = c.sb(ctx, "m8", [P, NB, 8])
        i8 = c.sb(ctx, "i8", [P, NB, 8], U32)
        f8 = c.sb(ctx, "f8", [P, NB, 8])
        eq = c.sb(ctx, "eq", [P, NB, TOPK, NEXP])
        mask = c.sb(ctx, "mask", [P, NB, NEXP])
        ex = c.sb(ctx, "ex", [P, NB, NEXP])
        sm = c.sb(ctx, "rsm", [P, 2, NB])
        cw = c.sb(ctx, "cw", [P, NB, NCW])
        cwT = c.sb(ctx, "cwT", [NCW, T])
        lps = c.ps(ctx, "lps", [P, NB, NEXP])
        tps = c.ps(ctx, "ctps", [NCW, T])
        with nc.Block() as block:
            @block.sync
            def _(e):
                e.dma_start(g.lut_i[:, :], dram["lut_idx"]).then_inc(s_li, 16)
                c.wait(e, s_te, 1)
                e.dma_start(dram["cw"], cwT[:, :]).then_inc(s_st, 16)
                c.wait(e, s_st, 16)
                c.wait(e, s_li, 16)

            @block.tensor
            def _(e):
                c.wait(e, wt.late_in, wt.late_n)
                for n in range(NB):
                    for k in range(KC):
                        mm = e.matmul(lps[:, n, :], g.feat[:, k, n * P:(n + 1) * P], wt.gate[:, k, :],
                                      start=k == 0, stop=k == KC - 1)
                mm.then_inc(s_lg, 1)
                c.wait(e, s_cw, 1)
                c.wait(e, s_pr, 2)
                for n in range(NB):
                    mm = e.transpose(tps[:, n * P:(n + 1) * P], cw[:, n, :], g.ident[:, :])
                mm.then_inc(s_tp, 1)

            @block.vector
            def _(e):
                c.wait(e, s_lg, 1)
                e.tensor_copy(lg[:, :, :], lps[:, :, :]).then_inc(s_le, 1)
                c.wait(e, s_le, 1)
                for n in range(NB):
                    e.max(m8[:, n, :], lg[:, n, :]).then_inc(s_m8, 1)
                c.wait(e, s_m8, NB)
                e.tensor_tensor(ex[:, :, :], lg[:, :, :], m8[:, :, 0:1].broadcast_to([P, NB, NEXP]),
                                ALU.subtract).then_inc(s_sh, 1)
                for n in range(NB):
                    e.max_index(i8[:, n, :], m8[:, n, :], lg[:, n, :]).then_inc(s_ix, 1)
                c.wait(e, s_ix, NB)
                e.tensor_copy(f8[:, :, :], i8[:, :, :]).then_inc(s_if, 1)
                c.wait(e, s_if, 1)
                e.tensor_tensor(eq[:, :, :, :],
                                g.iota_e[:, :].unsqueeze(1).unsqueeze(1).broadcast_to([P, NB, TOPK, NEXP]),
                                f8[:, :, 0:TOPK].unsqueeze(3).broadcast_to([P, NB, TOPK, NEXP]),
                                ALU.is_equal).then_inc(s_eq, 1)
                c.wait(e, s_eq, 1)
                e.tensor_reduce(mask[:, :, :], eq[:, :, :, :].rearrange("p n k e -> p n e k"), AX.X,
                                ALU.add).then_inc(s_mk, 1)
                c.wait(e, s_mk, 1)
                c.wait(e, s_ex, 1)
                e.tensor_tensor(mask[:, :, :], mask[:, :, :], ex[:, :, :], ALU.mult).then_inc(s_me, 1)
                c.wait(e, s_me, 1)
                e.tensor_reduce(sm[:, 0, :], mask[:, :, :], AX.X, ALU.add).then_inc(s_sm, 1)
                c.wait(e, s_sm, 1)
                e.reciprocal(sm[:, 1, :], sm[:, 0, :]).then_inc(s_rc, 1)
                c.wait(e, s_rc, 1)
                e.tensor_tensor(cw[:, :, 0:NEXP], mask[:, :, :], sm[:, 1, :].unsqueeze(2)
                                .broadcast_to([P, NB, NEXP]), ALU.mult).then_inc(s_cw, 1)
                c.wait(e, s_cw, 1)
                pair = cw[:, :, 0:NEXP].rearrange("p n (c a) -> p n c a", a=2)
                e.tensor_tensor(cw[:, :, NEXP:NCW], pair[:, :, :, 0], pair[:, :, :, 1], ALU.add).then_inc(s_pr, 1)
                c.wait(e, s_pr, 1)
                e.tensor_scalar(cw[:, :, NEXP:NCW], cw[:, :, NEXP:NCW], SMALL, None, ALU.mult).then_inc(s_pr, 1)
                c.wait(e, s_li, 16)
                e.tensor_copy(g.lut_f[:, 0:LUTW], g.lut_i[:, :]).then_inc(s_li, 1)
                e.memset(g.lut_f[:, LUTW:], 0.0).then_inc(s_li, 1)
                e.memset(g.lutw[:, :], 0.0).then_inc(s_li, 1)
                c.wait(e, s_tp, 1)
                e.tensor_copy(cwT[:, :], tps[:, :]).then_inc(s_te, 1)

            @block.scalar
            def _(e):
                c.wait(e, s_sh, 1)
                e.activation(ex[:, :, :], ex[:, :, :], ACT.Exp).then_inc(s_ex, 1)


def experts(c, g, dram, xh, xl):
    nc = c.nc
    s_w = [c.sem(f"ex_w{k}") for k in range(MOE_K)]
    s_c = [c.sem(f"ex_c{k}") for k in range(MOE_K)]
    s_z = c.sem("ex_z")
    s_g, s_u, s_d = c.counters("ex_", "g u d", nc.tensor)
    s_wl, s_tc, s_a, s_le = c.counters("ex_", "wl tc a le", nc.vector)
    s_wh, s_si, s_ah = c.counters("ex_", "wh si ah", nc.scalar)
    s_al, s_la = c.counters("ex_", "al la", nc.gpsimd)
    s_ye, s_yt, s_yx = map(c.sem, ["ex_ye", "ex_yt", "ex_yx"])
    K, LAST = MOE_K, MOE_IT * MOE_K
    with ExitStack() as ctx:
        wr = c.sb(ctx, "wr", [P, K, MOE_WN])
        wh = c.sb(ctx, "wh", [P, K, MOE_WN], F32R)
        wl = c.sb(ctx, "wl", [P, K, MOE_WN], F32R)
        cwb = c.sb(ctx, "cwb", [P, 3, T])
        si = c.sb(ctx, "si", [P, 3, T])
        a = c.sb(ctx, "a", [P, 3, T])
        ah = c.sb(ctx, "ah", [P, 3, T], F32R)
        al = c.sb(ctx, "al", [P, 3, T], F32R)
        lt = c.sb(ctx, "lt", [P, 2, LCH])
        gps = c.ps(ctx, "gps", [P, T])
        ups = c.ps(ctx, "ups", [P, T])
        yps = c.ps(ctx, "yps", [P, KC, T])
        yT = a[:, 0:KC, :]
        ZA, ZW = ESLOT[-1], K - 1

        def half(h):
            return slice(h * HALF, (h + 1) * HALF)

        with nc.Block() as block:
            @block.sync
            def _(e):
                def load(index, slot):
                    e.dma_start(wr[:, slot, :], dram["moe_w"][index, :, :].rearrange("a p n -> (a p) n")
                                ).then_inc(s_w[slot], 16)

                load(slice(0, 1), 0)
                with e.Fori(0, MOE_IT) as j:
                    for k in range(K):
                        n, s = j * K + k, ESLOT[k]
                        c.wait(e, s_tc, n + 1 if k >= 2 else n)
                        if k < 3:
                            r0 = k * P
                            cut = (r0 // INTER + 1) * INTER - r0
                            for p0, p1 in [(0, cut), (cut, P)]:
                                e.dma_start(cwb[p0:p1, s, :],
                                            dram["cw"][bass.ds(4 * j + (r0 + p0) // INTER, 1), :]
                                            .broadcast_to([p1 - p0, T])).then_inc(s_c[k], 16)
                        else:
                            e.dma_start(cwb[:, s, :], dram["cw"][bass.ds(2 * j + (NEXP + k - 3), 1), :]
                                        .broadcast_to([P, T])).then_inc(s_c[k], 16)
                        c.wait(e, s_wl, n)
                        load(bass.ds(n + 1, 1), (k + 1) % K)

            def split_high(e, slot, loaded):
                c.wait(e, s_w[slot], loaded)
                e.activation(wh[:, slot, :], wr[:, slot, :], ACT.Copy).then_inc(s_wh, 1)

            def split_low(e, slot, done):
                c.wait(e, s_wh, done)
                e.tensor_tensor(wl[:, slot, :], wr[:, slot, :], wh[:, slot, :].bitcast(F32),
                                ALU.subtract).then_inc(s_wl, 1)

            @block.scalar
            def _(e):
                split_high(e, 0, 16)
                with e.Fori(0, MOE_IT) as j:
                    for k in range(K):
                        n, s = j * K + k, ESLOT[k]
                        c.wait(e, s_g, n + 1)
                        e.activation(si[:, s, :], gps[:, :], ACT.Silu).then_inc(s_si, 1)
                        c.wait(e, s_d, n + 1)
                        c.wait(e, s_wl, n + 1)
                        split_high(e, (k + 1) % K, j * 16 + (16 if k < K - 1 else 32))
                        c.wait(e, s_a, n + 1)
                        e.activation(ah[:, s, :], a[:, s, :], ACT.Copy).then_inc(s_ah, 1)
                c.wait(e, s_d, LAST + 2)
                c.wait(e, s_al, LAST)
                for q in range(KC):
                    e.activation(yT[:, q, :], yps[:, q, :], ACT.Copy).then_inc(s_ye, 1)

            @block.vector
            def _(e):
                e.memset(ah[:, ZA, :].bitcast(F32), 0.0).then_inc(s_z, 1)
                e.memset(wh[:, ZW, :].bitcast(F32), 0.0).then_inc(s_tc, 1)
                e.memset(wl[:, ZW, :].bitcast(F32), 0.0).then_inc(s_tc, 1)
                split_low(e, 0, 1)
                with e.Fori(0, MOE_IT) as j:
                    for k in range(K):
                        n, s = j * K + k, ESLOT[k]
                        c.wait(e, s_si, n + 1)
                        c.wait(e, s_c[k], (j + 1) * (32 if k < 3 else 16))
                        e.tensor_tensor(si[:, s, :], si[:, s, :], cwb[:, s, :], ALU.mult).then_inc(s_tc, 1)
                        c.wait(e, s_la, 2 * n)
                        for q in range(2):
                            e.tensor_scalar(lt[:, q, :], g.lut_f[:, k * LCH:(k + 1) * LCH],
                                            g.iota_l[:, bass.ds(2 * j + q, 1)], g.lutb[:, bass.ds(2 * j + q, 1)],
                                            ALU.is_equal, ALU.mult).then_inc(s_le, 1)
                        split_low(e, (k + 1) % K, n + 2)
                        c.wait(e, s_tc, n + 3)
                        c.wait(e, s_u, n + 1)
                        e.tensor_tensor(a[:, s, :], ups[:, :], si[:, s, :], ALU.mult).then_inc(s_a, 1)
                for n in range(NB):
                    c.wait(e, s_yt, n // 2 + 1)
                    yb = gps if n < NB // 2 else ups
                    e.tensor_tensor(g.x[:, n, :], yb[:, (n % 4) * D:(n % 4 + 1) * D], g.x[:, n, :],
                                    ALU.add).then_inc(s_yx, 1)

            @block.gpsimd
            def _(e):
                e.memset(al[:, ZA, :].bitcast(F32), 0.0).then_inc(s_z, 1)
                with e.Fori(0, MOE_IT) as j:
                    for k in range(K):
                        n, s = j * K + k, ESLOT[k]
                        for q in range(2):
                            c.wait(e, s_le, n * 2 + q + 1)
                            c.wait(e, s_la, n * 2 + q)
                            part = g.lutw[:, k * LCH:(k + 1) * LCH]
                            e.tensor_tensor(part, part, lt[:, q, :], ALU.add).then_inc(s_la, 1)
                        c.wait(e, s_ah, n + 1)
                        e.tensor_tensor(al[:, s, :], a[:, s, :], ah[:, s, :].bitcast(F32),
                                        ALU.subtract).then_inc(s_al, 1)

            @block.tensor
            def _(e):
                def rows(ps, slot, part, sem):
                    for h in range(NH):
                        terms = [(w, x, q) for q in range(KC) for w, x in ((wh, xh), (wh, xl), (wl, xh))]
                        for i, (w, x, q) in enumerate(terms):
                            o = (part * KC + q) * P
                            mm = e.matmul(ps[:, half(h)], w[:, slot, o:o + P], x[:, q, half(h)],
                                          start=i == 0, stop=i == len(terms) - 1)
                    mm.then_inc(sem, 1)

                def down(slot, wslot, first=False):
                    for q in range(KC):
                        o = 2 * KC * P + q * P
                        for i, (w, x) in enumerate(((wh, ah), (wl, ah), (wh, al))):
                            for h in range(NH):
                                mm = e.matmul(yps[:, q, half(h)], w[:, wslot, o:o + P], x[:, slot, half(h)],
                                              start=first and i == 0, stop=False, skip_group_check=True)
                    mm.then_inc(s_d, 1)

                c.wait(e, s_z, 2)
                c.wait(e, s_tc, 2)
                down(ZA, ZW, first=True)
                with e.Fori(0, MOE_IT) as j:
                    for k in range(K):
                        n = j * K + k
                        c.wait(e, s_wl, n + 1)
                        c.wait(e, s_si, n)
                        rows(gps, k, 0, s_g)
                        c.wait(e, s_a, n)
                        rows(ups, k, 1, s_u)
                        c.wait(e, s_al, n)
                        down(ESLOT[k - 1], (k - 1) % K)
                c.wait(e, s_al, LAST)
                down(ZA, ZW)
                for n in range(NB):
                    c.wait(e, s_ye, KC)
                    yb = gps if n < NB // 2 else ups
                    for q in range(KC):
                        o = (n % 4) * D + q * P
                        mm = e.transpose(yb[:, o:o + P], yT[:, q, n * P:(n + 1) * P], g.ident[:, :])
                    if n % 2:
                        mm.then_inc(s_yt, 1)


def mamba_input(c, g, wt, hT):
    nc = c.nc
    s_mm, s_h = map(c.sem, ["mi_mm", "mi_h"])
    w, b = wt.w_in, wt.b_in
    with ExitStack() as ctx:
        ps = c.ps(ctx, "mi_ps", [P, KC, T])
        with nc.Block() as block:
            @block.tensor
            def _(e):
                for m in range(KC):
                    for h in range(NH):
                        for k in range(KC):
                            mm = e.matmul(ps[:, m, h * HALF:(h + 1) * HALF], w[:, k, m * P:(m + 1) * P],
                                          g.feat[:, k, h * HALF:(h + 1) * HALF], start=k == 0, stop=k == KC - 1)
                    mm.then_inc(s_mm, 1)

            @block.scalar
            def _(e):
                for m in range(KC):
                    c.wait(e, s_mm, m + 1)
                    e.activation(hT[:, m, :], ps[:, m, :], ACT.Gelu, bias=b[:, m:m + 1]).then_inc(s_h, 1)


def mamba_project(c, g, dram, dr, rev, hT, w, xi, sz, dt, u, sc):
    nc = c.nc
    sc.landed = [c.sem(f"{dr}_bb{i}") for i in range(2)]
    s_w, s_in, s_pad, s_cp, s_cv, s_xi, s_sz, s_xp, s_xe, s_bc, s_dm, s_ab, s_e1, s_l1, s_mx, s_dt, s_u, s_A = map(
        c.sem, [f"{dr}_{n}" for n in "w in pad cp cv xi sz xp xe bc dm ab e1 l1 mx dt u A".split()])
    with ExitStack() as ctx:
        win = c.sb(ctx, dr + "_win", [P, KC, 2 * DI])
        wxp = c.sb(ctx, dr + "_wxp", [P, DB, DTR + 2 * DS])
        wdt = c.sb(ctx, dr + "_wdt", [P, DI])
        cvw = c.sb(ctx, dr + "_cvw", [P, DB, DCONV])
        cvb = c.sb(ctx, dr + "_cvb", [P, DB])
        dtb = c.sb(ctx, dr + "_dtb", [P, DB])
        raw = c.sb(ctx, dr + "_raw", [P, 2, NSEQ * SEGC])
        cv = c.sb(ctx, dr + "_cv", [P, 2, T])
        dtr = c.sb(ctx, dr + "_dtr", [P, T])
        bcr = c.sb(ctx, dr + "_bcr", [2 * DS, T])
        sp = c.sb(ctx, dr + "_sp", [P, 3, T])
        ps = [c.ps(ctx, f"{dr}_ps{i}", [P, T]) for i in range(4)]
        NW = 9 * 16
        with nc.Block() as block:
            @block.sync
            def _(e):
                e.dma_start(win[:, :, :], dram[dr + "_in_wT"].rearrange("(k p) n -> p k n", p=P)).then_inc(s_w, 16)
                e.dma_start(wxp[:, :, :], dram[dr + "_xproj_wT"].rearrange("(k p) n -> p k n", p=P)).then_inc(s_w, 16)
                e.dma_start(wdt[:, :], dram[dr + "_dt_wT"]).then_inc(s_w, 16)
                e.dma_start(cvw[:, :, :], dram[dr + "_conv_w"].rearrange("(k p) n -> p k n", p=P)).then_inc(s_w, 16)
                e.dma_start(cvb[:, :], dram[dr + "_conv_b"]).then_inc(s_w, 16)
                e.dma_start(dtb[:, :], dram[dr + "_dt_b"]).then_inc(s_w, 16)
                e.dma_start(w.A[:, :, :], dram[dr + "_A_log"].rearrange("(k p) n -> p k n", p=P)).then_inc(s_w, 16)
                e.dma_start(w.Dv[:, :], dram[dr + "_D"]).then_inc(s_w, 16)
                e.dma_start(w.out[:, :, :], dram[dr + "_out_wT"].rearrange("(k p) n -> p k n", p=P)).then_inc(s_w, 16)
                c.wait(e, s_xe, 1)
                e.dma_start(dram["bc"], bcr[:, :]).then_inc(s_bc, 16)
                c.wait(e, s_bc, 16)
                for q in range(2):
                    load_state(e, dram, sc, q, slice(q, q + 1), slice(DS + q, DS + q + 1))

            @block.tensor
            def _(e):
                c.wait(e, s_w, NW)
                def in_proj(m):
                    if m >= 4:
                        c.wait(e, s_cp, m - 3)
                    for h in range(NH):
                        for k in range(KC):
                            mm = e.matmul(ps[m % 4][:, h * HALF:(h + 1) * HALF], win[:, k, m * P:(m + 1) * P],
                                          hT[:, k, h * HALF:(h + 1) * HALF], start=k == 0, stop=k == KC - 1)
                    mm.then_inc(s_in, 1)
                for m in range(8):
                    in_proj(m)
                c.wait(e, s_xi, DB)
                for i, (lo, hi) in enumerate([(DTR, DTR + 2 * DS), (0, DTR)]):
                    c.wait(e, s_sz, i + 1)
                    for h in range(NH):
                        for k in range(DB):
                            mm = e.matmul(ps[i][0:hi - lo, h * HALF:(h + 1) * HALF], wxp[:, k, lo:hi],
                                          xi[:, k, h * HALF:(h + 1) * HALF], start=k == 0, stop=k == DB - 1)
                    mm.then_inc(s_xp, 1)
                c.wait(e, s_xe, 2)
                for d in range(DB):
                    b = (d + 2) % 4
                    if d < 2:
                        c.wait(e, s_sz, d + 3)
                    for h in range(NH):
                        mm = e.matmul(ps[b][:, h * HALF:(h + 1) * HALF], wdt[:, d * P:(d + 1) * P],
                                      dtr[:, h * HALF:(h + 1) * HALF], start=True, stop=True)
                    mm.then_inc(s_dm, 1)

            @block.gpsimd
            def _(e):
                e.memset(raw[:, :, :], 0.0).then_inc(s_pad, 1)
                e.memset(sc.dA[:, :, :], 0.0).then_inc(s_pad, 1)
                e.memset(sc.uB[:, :, :], 0.0).then_inc(s_pad, 1)
                for d in range(DB):
                    c.wait(e, s_l1, d + 1)
                    c.wait(e, s_mx, d + 1)
                    e.tensor_tensor(dt[:, d, :], dt[:, d, :], sp[:, 2, :], ALU.add).then_inc(s_dt, 1)
                    c.wait(e, s_dt, d + 1)
                    e.tensor_tensor(u[:, d, :], dt[:, d, :], xi[:, d, :], ALU.mult).then_inc(s_u, 1)

            @block.scalar
            def _(e):
                c.wait(e, s_pad, 1)
                def copy_in(m):
                    if m >= 2:
                        c.wait(e, s_cv, DCONV * (m - 1))
                    c.wait(e, s_in, m + 1)
                    e.activation(seq_view(raw[:, m % 2, :], SEGC, PADC), ps[m][:, :].rearrange("p (b s) -> p b s", s=SEQ),
                                 ACT.Copy).then_inc(s_cp, 1)

                def silu_x(m):
                    c.wait(e, s_cv, DCONV * (m + 1))
                    e.activation(xi[:, m, :], cv[:, m % 2, :], ACT.Silu).then_inc(s_xi, 1)

                def silu_z(m):
                    c.wait(e, s_in, DB + m + 1)
                    e.activation(sz[:, m, :], ps[m][:, :], ACT.Silu).then_inc(s_sz, 1)

                copy_in(0)
                copy_in(1)
                silu_x(0)
                copy_in(2)
                silu_x(1)
                copy_in(3)
                silu_x(2)
                silu_z(0)
                silu_x(3)
                silu_z(1)
                silu_z(2)
                silu_z(3)
                c.wait(e, s_w, NW)
                e.activation(w.A[:, :, :], w.A[:, :, :], ACT.Exp).then_inc(s_A, 1)
                for i, dst in enumerate([bcr[:, :], dtr[:, :]]):
                    c.wait(e, s_xp, i + 1)
                    e.activation(dst, ps[i][0:dst.shape[0], :], ACT.Copy).then_inc(s_xe, 1)
                for d in range(DB):
                    b = (d + 2) % 4
                    c.wait(e, s_dm, d + 1)
                    c.wait(e, s_e1, d)
                    e.activation(sp[:, 0, :], ps[b][:, :], ACT.Abs, bias=dtb[:, d:d + 1]).then_inc(s_ab, 1)
                    c.wait(e, s_ab, d + 1)
                    c.wait(e, s_l1, d)
                    e.activation(sp[:, 1, :], sp[:, 0, :], ACT.Exp, scale=-1.0).then_inc(s_e1, 1)
                    c.wait(e, s_e1, d + 1)
                    e.activation(dt[:, d, :], sp[:, 1, :], ACT.Ln, bias=1.0).then_inc(s_l1, 1)

            @block.vector
            def _(e):
                c.wait(e, s_w, NW)
                for m in range(DB):
                    c.wait(e, s_cp, m + 1)
                    if m >= 2:
                        c.wait(e, s_xi, m - 1)
                    out = cv[:, m % 2, :].rearrange("p (b s) -> p b s", s=SEQ)
                    for t in range(DCONV):
                        src = seq_view(raw[:, m % 2, :], SEGC, 2 * PADC - t if rev else t)
                        if t == 0:
                            e.tensor_scalar(out, src, cvw[:, m, 0:1], cvb[:, m:m + 1],
                                            ALU.mult, ALU.add).then_inc(s_cv, 1)
                        else:
                            c.wait(e, s_cv, m * DCONV + t)
                            e.scalar_tensor_tensor(out, src, cvw[:, m, t:t + 1], out,
                                                   ALU.mult, ALU.add).then_inc(s_cv, 1)
                c.wait(e, s_A, 1)
                e.tensor_scalar(w.A[:, :, :], w.A[:, :, :], -1.0, None, ALU.mult).then_inc(s_A, 1)
                for d in range(DB):
                    c.wait(e, s_ab, d + 1)
                    c.wait(e, s_dt, d)
                    e.tensor_scalar(sp[:, 2, :], ps[(d + 2) % 4][:, :], dtb[:, d:d + 1], 0.0,
                                    ALU.add, ALU.max).then_inc(s_mx, 1)


def load_state(e, dram, sc, q, b_row, c_row):
    e.dma_start(sc.Bb[:, q, :], dram["bc"][b_row, :].broadcast_to([P, T])).then_inc(sc.landed[q], 16)
    e.dma_start(sc.Cb[:, q, :], dram["bc"][c_row, :].broadcast_to([P, T])).then_inc(sc.landed[q], 16)


def mamba_scan(c, g, dram, dr, rev, w, xi, sz, dt, u, acc, sc):
    nc = c.nc
    s_bb = sc.landed
    s_dd, s_y, s_om, s_oa = map(c.sem, [f"{dr}s_{n}" for n in "dd y om oa".split()])
    s_da, = c.counters(dr, "s_da", nc.scalar)
    s_ub, = c.counters(dr, "s_ub", nc.gpsimd)
    s_sc, s_hc = c.counters(dr, "s_sc s_hc", nc.vector)
    s_ac, = c.counters(dr, "s_ac", nc.tensor)
    lo = 0 if rev else 1
    U = 2 * DB
    with ExitStack() as ctx:
        Bb, Cb, dA, uB = sc.Bb, sc.Cb, sc.dA, sc.uB
        hh = c.sb(ctx, dr + "_hh", [P, 2, NSEQ * SEGS])
        hC = c.sb(ctx, dr + "_hC", [P, 2, T])
        dD = c.sb(ctx, dr + "_dD", [P, DB, P])
        with ExitStack() as pctx:
            y = [c.ps(pctx, f"{dr}_y{d}", [P, T]) for d in range(DB)]
            with nc.Block() as block:
                @block.sync
                def _(e):
                    with e.Fori(0, DS // 2 - 1) as j:
                        for q in range(2):
                            c.wait(e, s_hc, j * U + (q + 1) * DB)
                            load_state(e, dram, sc, q, bass.ds(2 * j + (q + 2), 1), bass.ds(2 * j + (q + 2 + DS), 1))

                @block.gpsimd
                def _(e):
                    with e.Fori(0, DS // 2) as j:
                        for i in range(U):
                            q, d = i // DB, i % DB
                            if d == 0:
                                c.wait(e, s_bb[q], (j + 1) * 32)
                            c.wait(e, s_sc, j * U + (i - 1))
                            e.tensor_tensor(seq_view(uB[:, i % 2, :], SEGS, lo),
                                            u[:, d, :].rearrange("p (b s) -> p b s", s=SEQ),
                                            Bb[:, q, :].rearrange("p (b s) -> p b s", s=SEQ),
                                            ALU.mult).then_inc(s_ub, 1)

                @block.scalar
                def _(e):
                    with e.Fori(0, DS // 2) as j:
                        for i in range(U):
                            q, d = i // DB, i % DB
                            c.wait(e, s_sc, j * U + (i - 1))
                            e.activation(seq_view(dA[:, i % 2, :], SEGS, lo),
                                         dt[:, d, :].rearrange("p (b s) -> p b s", s=SEQ), ACT.Exp,
                                         scale=w.A[:, d, bass.ds(2 * j + q, 1)]).then_inc(s_da, 1)

                @block.vector
                def _(e):
                    for d in range(DB):
                        e.tensor_scalar(dD[:, d, :], g.ident[:, :], w.Dv[:, d:d + 1], None, ALU.mult).then_inc(s_dd, 1)
                    with e.Fori(0, DS // 2) as j:
                        for i in range(U):
                            n, q, d, b = j * U + i, i // DB, i % DB, i % 2
                            c.wait(e, s_da, n + 1)
                            c.wait(e, s_ub, n + 1)
                            c.wait(e, s_hc, j * U + (i - 1))
                            way = slice(None, None, -1) if rev else slice(None)
                            e.tensor_tensor_scan(hh[:, b, way], dA[:, b, way], uB[:, b, way], 0.0,
                                                 ALU.mult, ALU.add).then_inc(s_sc, 1)
                            if d == 0:
                                c.wait(e, s_bb[q], (j + 1) * 32)
                            c.wait(e, s_sc, n + 1)
                            c.wait(e, s_ac, j * U + (i - 1))
                            e.tensor_tensor(hC[:, b, :].rearrange("p (b s) -> p b s", s=SEQ),
                                            seq_view(hh[:, b, :], SEGS, lo),
                                            Cb[:, q, :].rearrange("p (b s) -> p b s", s=SEQ),
                                            ALU.mult).then_inc(s_hc, 1)
                    for d in range(DB):
                        c.wait(e, s_ac, (DS - 1) * DB + d + 1)
                        e.tensor_tensor(u[:, d, :], y[d][:, :], sz[:, d, :], ALU.mult).then_inc(s_y, 1)
                    for m in range(KC):
                        c.wait(e, s_om, 1)
                        e.tensor_tensor(acc[:, m, :], y[m][:, :], acc[:, m, :], ALU.add).then_inc(s_oa, 1)

                @block.tensor
                def _(e):
                    c.wait(e, s_dd, DB)
                    for d in range(DB):
                        for h in range(NH):
                            e.matmul(y[d][:, h * HALF:(h + 1) * HALF], dD[:, d, :], xi[:, d, h * HALF:(h + 1) * HALF],
                                     start=True, stop=False, skip_group_check=True)
                    with e.Fori(0, DS // 2) as j:
                        for i in range(U):
                            n, d = j * U + i, i % DB
                            c.wait(e, s_hc, n + 1)
                            for h in range(NH):
                                mm = e.matmul(y[d][:, h * HALF:(h + 1) * HALF], g.ident[:, :],
                                              hC[:, i % 2, h * HALF:(h + 1) * HALF], start=False, stop=False,
                                              skip_group_check=True)
                            mm.then_inc(s_ac, 1)
                    for k in range(DB):
                        c.wait(e, s_y, max(k + 1, KC))
                        for m in range(KC):
                            for h in range(NH):
                                mm = e.matmul(y[m][:, h * HALF:(h + 1) * HALF], w.out[:, k, m * P:(m + 1) * P],
                                              u[:, k, h * HALF:(h + 1) * HALF], start=k == 0, stop=k == DB - 1,
                                              skip_group_check=True)
                    mm.then_inc(s_om, 1)


def to_tokens(c, g, name, feat, tok):
    nc = c.nc
    s_t, s_e = c.sem(name + "_t"), c.sem(name + "_e")
    with ExitStack() as ctx:
        ps = c.ps(ctx, name + "_ps", [P, NB, D])
        with nc.Block() as block:
            @block.tensor
            def _(e):
                for n in range(NB):
                    for k in range(KC):
                        mm = e.transpose(ps[:, n, k * P:(k + 1) * P], feat[:, k, n * P:(n + 1) * P], g.ident[:, :])
                    mm.then_inc(s_t, 1)

            @block.scalar
            def _(e):
                for q in range(2):
                    c.wait(e, s_t, 4 * (q + 1))
                    e.activation(tok[:, 4 * q:4 * q + 4, :], ps[:, 4 * q:4 * q + 4, :], ACT.Copy).then_inc(s_e, 1)


def mamba_output(c, g, wt):
    nc = c.nc
    s_mm, s_b, s_x = map(c.sem, ["mo_mm", "mo_b", "mo_x"])
    w, b = wt.w_out, wt.b_out
    with ExitStack() as ctx:
        ps = c.ps(ctx, "mo_ps", [P, NB, D])
        with nc.Block() as block:
            @block.tensor
            def _(e):
                for n in range(NB):
                    for k in range(KC):
                        mm = e.matmul(ps[:, n, :], g.feat[:, k, n * P:(n + 1) * P], w[:, k, :],
                                      start=k == 0, stop=k == KC - 1)
                    if n % 2:
                        mm.then_inc(s_mm, 1)

            @block.gpsimd
            def _(e):
                e.tensor_tensor(g.x[:, :, :], g.x[:, :, :], b[:, :].unsqueeze(1).broadcast_to([P, NB, D]),
                                ALU.add).then_inc(s_b, 1)

            @block.vector
            def _(e):
                c.wait(e, s_b, 1)
                for n in range(NB):
                    c.wait(e, s_mm, n // 2 + 1)
                    e.tensor_tensor(g.x[:, n, :], ps[:, n, :], g.x[:, n, :], ALU.add).then_inc(s_x, 1)


def table_ffn(c, g, out):
    nc = c.nc
    s_g, s_u, s_si, s_a, s_y, s_x, s_o = map(c.sem, [f"ff_{n}" for n in "g u si a y x o".split()])
    M = len(FB)
    wg = g.lutw[:, 0:KC * FI].rearrange("p (k n) -> p k n", k=KC)
    wu = g.lutw[:, KC * FI:2 * KC * FI].rearrange("p (k n) -> p k n", k=KC)
    wd = g.lutw[:, 2 * KC * FI:LUTW].rearrange("p (m n) -> p m n", m=M)
    with ExitStack() as ctx:
        si = c.sb(ctx, "ff_si", [P, 2, T])
        a = c.sb(ctx, "ff_a", [P, M, T])
        ps = [c.ps(ctx, f"ff_p{i}", [P, T]) for i in range(4)]
        with nc.Block() as block:
            @block.tensor
            def _(e):
                for m, (o, r) in enumerate(FB):
                    for w, b, sem in ((wg, 2 * (m % 2), s_g), (wu, 2 * (m % 2) + 1, s_u)):
                        if m >= 2:
                            c.wait(e, s_a, m - 1)
                        for h in range(NH):
                            for k in range(KC):
                                mm = e.matmul(ps[b][0:r, h * HALF:(h + 1) * HALF], w[:, k, o:o + r],
                                              g.feat[:, k, h * HALF:(h + 1) * HALF], start=k == 0, stop=k == KC - 1)
                        mm.then_inc(sem, 1)
                c.wait(e, s_a, M)
                for n in range(NB):
                    for m, (o, r) in enumerate(FB):
                        mm = e.matmul(ps[n // 4][:, (n % 4) * D:(n % 4 + 1) * D], a[0:r, m, n * P:(n + 1) * P],
                                      wd[0:r, m, :], start=m == 0, stop=m == M - 1)
                    if n % 2:
                        mm.then_inc(s_y, 1)

            @block.scalar
            def _(e):
                for m, (o, r) in enumerate(FB):
                    c.wait(e, s_g, m + 1)
                    if m >= 2:
                        c.wait(e, s_a, m - 1)
                    e.activation(si[0:r, m % 2, :], ps[2 * (m % 2)][0:r, :], ACT.Silu).then_inc(s_si, 1)

            @block.vector
            def _(e):
                for m, (o, r) in enumerate(FB):
                    c.wait(e, s_si, m + 1)
                    c.wait(e, s_u, m + 1)
                    e.tensor_tensor(a[0:r, m, :], ps[2 * (m % 2) + 1][0:r, :], si[0:r, m % 2, :],
                                    ALU.mult).then_inc(s_a, 1)
                for n in range(NB):
                    c.wait(e, s_y, n // 2 + 1)
                    e.tensor_tensor(g.x[:, n, :], ps[n // 4][:, (n % 4) * D:(n % 4 + 1) * D], g.x[:, n, :],
                                    ALU.add).then_inc(s_x, 1)

            @block.sync
            def _(e):
                for n in range(NB):
                    c.wait(e, s_x, n + 1)
                    e.dma_start(out[n * P:(n + 1) * P, :], g.x[:, n, :]).then_inc(s_o, 16)
                c.wait(e, s_o, NB * 16)


class Shared:
    pass


def fetch(nc, s, pairs):
    for dst, src in pairs:
        nc.sync.dma_start(dst, src).then_inc(s, 16)
    return 16 * len(pairs)


def build(nc, dram, out):
    with ExitStack() as ctx:
        c = Core(nc, ctx)
        g = Shared()
        g.x = c.sb(ctx, "x", [P, NB, D])
        g.feat = c.sb(ctx, "feat", [P, KC, T])
        g.lutw = c.sb(ctx, "lutw", [P, MOE_K * LCH])
        g.ident = c.sb(ctx, "ident", [P, P])
        g.gmask = c.sb(ctx, "gmask", [P, 8])
        g.iota_e = c.sb(ctx, "iota_e", [P, NEXP])
        g.iota_l = c.sb(ctx, "iota_l", [P, LUT])
        g.lutb = c.sb(ctx, "lutb", [P, LUT])
        dram["cw"] = nc.dram_tensor("cw_rows", (NCW, T), F32, kind="Internal").ap()
        dram["bc"] = nc.dram_tensor("bc_rows", (2 * DS, T), F32, kind="Internal").ap()
        wt = Shared()
        chunks = lambda name: dram[name].rearrange("(k p) n -> p k n", p=P)
        wt.gate, wt.w_in, wt.w_out = (c.sb(ctx, n, [P, KC, w]) for n, w in
                                      (("gate", NEXP), ("w_in", D), ("w_out", D)))
        wt.b_in, wt.b_out = c.sb(ctx, "b_in", [P, KC]), c.sb(ctx, "b_out", [P, D])
        wt.ln = c.sb(ctx, "ln_gb", [P, 2, KC])
        s_x = [c.kept(f"x_in{n}") for n in range(NB)]
        wt.at_in, wt.late_in = c.kept("at_in"), c.kept("late_in")
        at = ctx.enter_context(ExitStack())
        wt.wq2, wt.wk2, wt.wv, wt.wout = (c.sb(at, n, [P, KC, w]) for n, w in (
            ("wq2", HJ * P), ("wk2", P), ("wv", KV), ("wout", D)))
        wt.bq2, wt.bk, wt.bv, wt.bout = (c.sb(at, n, [P, w]) for n, w in (
            ("bq2", HJ), ("bk", 1), ("bv", KV), ("bout", D)))
        for n in range(NB):
            nc.sync.dma_start(g.x[:, n, :], dram["x"][n * P:(n + 1) * P, :]).then_inc(s_x[n], 16)
        wt.at_n = fetch(nc, wt.at_in, [
            (wt.wk2[:, :, :], chunks("wk2")), (wt.bk[:, :], dram["bk2"]), (wt.wq2[:, :, :], chunks("wq2")),
            (wt.bq2[:, :], dram["bq2"]), (wt.wv[:, :, :], chunks("wv")), (wt.wout[:, :, :], chunks("Wout")),
            (wt.bv[:, :], dram["bv"].broadcast_to([P, KV])), (wt.bout[:, :], dram["bout"].broadcast_to([P, D]))])
        wt.late_n = fetch(nc, wt.late_in, [
            (wt.gate[:, :, :], chunks("gate_wT")), (wt.w_in[:, :, :], chunks("w_inT")), (wt.b_in[:, :], dram["b_in"]),
            (wt.w_out[:, :, :], chunks("w_outT")), (wt.b_out[:, :], dram["b_out"].broadcast_to([P, D])),
            (wt.ln[:, 0, :], dram["ln_g"]), (wt.ln[:, 1, :], dram["ln_b"]),
            (g.lutb[:, :], dram["lut"].broadcast_to([P, LUT]))])
        constants(c, g)
        layernorm(c, g, "ln1", g.x, g.feat, loads=s_x)
        attention(c, g, wt)
        at.close()
        with ExitStack() as moe:
            g.lut_f = c.sb(moe, "lut_f", [P, MOE_K * LCH])
            xh = c.sb(moe, "xh", [P, KC, T], F32R)
            xl = c.sb(moe, "xl", [P, KC, T], F32R)
            layernorm(c, g, "ln2", g.x, g.feat, hi=xh, lo=xl)
            with ExitStack() as idx:
                g.lut_i = c.sb(idx, "lut_i", [P, LUTW], I32)
                routing(c, g, dram, wt)
            experts(c, g, dram, xh, xl)
        c.recycle()
        layernorm(c, g, "ln3", g.x, g.feat)
        with ExitStack() as mm:
            hT = c.sb(mm, "hT", [P, KC, T])
            acc = c.sb(mm, "acc", [P, KC, T])
            w = Shared()
            w.A = c.sb(mm, "A", [P, DB, DS])
            w.Dv = c.sb(mm, "Dv", [P, DB])
            w.out = c.sb(mm, "w_o", [P, DB, D])
            xi = c.sb(mm, "xi", [P, DB, T])
            sz = c.sb(mm, "sz", [P, DB, T])
            dt = c.sb(mm, "dt", [P, DB, T])
            u = c.sb(mm, "u", [P, DB, T])
            sc = Shared()
            sc.Bb, sc.Cb = (c.sb(mm, n, [P, 2, T]) for n in ("Bb", "Cb"))
            sc.dA, sc.uB = (c.sb(mm, n, [P, 2, NSEQ * SEGS]) for n in ("dA", "uB"))
            mamba_input(c, g, wt, hT)
            s_hc = c.sem("h_copy")
            with nc.Block() as block:
                @block.vector
                def _(e):
                    e.tensor_copy(acc[:, :, :], hT[:, :, :]).then_inc(s_hc, 1)
            for dr, rev in (("fm", False), ("bm", True)):
                mamba_project(c, g, dram, dr, rev, hT, w, xi, sz, dt, u, sc)
                mamba_scan(c, g, dram, dr, rev, w, xi, sz, dt, u, acc, sc)
                c.recycle()
            rt = c.sb(mm, "r_tok", [P, NB, D])
            to_tokens(c, g, "rt_tok", acc, rt)
            layernorm(c, g, "lnm", rt, g.feat, gamma=wt.ln[:, 0, :], beta=wt.ln[:, 1, :])
        mamba_output(c, g, wt)
        layernorm(c, g, "ln4", g.x, g.feat)
        table_ffn(c, g, out)


def kernel(**inputs):
    import numpy as np
    import concourse.bacc as bacc
    from concourse.bass_utils import run_bass_kernel_spmd

    f = {k: np.asarray(v) for k, v in inputs.items()}

    def columns(v):
        return v.reshape(-1, P).T

    def by_hidden(gate, up, down, count):
        rows = count * P
        flat = [w.transpose(1, 0, 2).reshape(KC, P, count, P).transpose(2, 1, 0, 3).reshape(count, P, KC * P)
                for w in (gate, up)]
        return np.concatenate(flat + [down.reshape(rows, D).reshape(count, P, D)], axis=2)

    large = by_hidden(f["L0_ffn_Wg"], f["L0_ffn_Wu"], f["L0_ffn_Wd"], EB).reshape(MOE_IT, 3, P, MOE_WN)
    small = by_hidden(f["L0_ffn_cWg"], f["L0_ffn_cWu"], f["L0_ffn_cWd"], NCH).reshape(MOE_IT, 2, P, MOE_WN)
    moe = np.concatenate([large, small], axis=1).reshape(MOE_IT * MOE_K, P, MOE_WN)
    moe = np.concatenate([moe, moe[:1]], axis=0)

    def twice(w):
        return np.repeat(w.reshape(len(w), -1, 1, KV), 2, axis=2).reshape(len(w), -1)

    wqkv, bqkv = f["L0_attn_Wqkv"], f["L0_attn_bqkv"].reshape(1, -1)

    def table_rows(idx):
        return idx.T.reshape(KC, P, FI).transpose(1, 0, 2).reshape(P, KC * FI)

    down = np.zeros((len(FB) * P, D), f["L1_ffn_down_idx"].dtype)
    down[:FI] = f["L1_ffn_down_idx"].T
    down = down.reshape(len(FB), P, D).transpose(1, 0, 2).reshape(P, len(FB) * D)
    arrays = {
        "x": f["L0_attn_x"].reshape(T, D), "wq2": twice(wqkv[:, :D]), "wk2": twice(wqkv[:, D:D + KV]),
        "wv": wqkv[:, D + KV:], "bq2": columns(twice(bqkv[:, :D]).ravel()), "bk2": columns(twice(bqkv[:, D:D + KV]).ravel()),
        "bv": bqkv[:, D + KV:],
        "Wout": f["L0_attn_Wout"], "bout": f["L0_attn_bout"].reshape(1, D), "gate_wT": f["L0_ffn_gate_w"].T,
        "moe_w": moe, "lut": f["L1_ffn_lut"].reshape(1, LUT),
        "lut_idx": np.concatenate([table_rows(f["L1_ffn_gate_idx"]), table_rows(f["L1_ffn_up_idx"]), down], axis=1),
        "w_inT": f["L1_attn_w_in"].T, "b_in": columns(f["L1_attn_b_in"]),
        "ln_g": columns(f["L1_attn_ln_g"]), "ln_b": columns(f["L1_attn_ln_b"]),
        "w_outT": f["L1_attn_w_out"].T, "b_out": f["L1_attn_b_out"].reshape(1, D),
    }
    for dr in ("fm", "bm"):
        n = f"L1_attn_{dr}_"
        arrays |= {
            dr + "_in_wT": f[n + "in_w"].T, dr + "_xproj_wT": f[n + "xproj_w"].T, dr + "_dt_wT": f[n + "dt_w"].T,
            dr + "_conv_w": f[n + "conv_w"], dr + "_conv_b": columns(f[n + "conv_b"]),
            dr + "_dt_b": columns(f[n + "dt_b"]), dr + "_A_log": f[n + "A_log"], dr + "_D": columns(f[n + "D"]),
            dr + "_out_wT": f[n + "out_w"].T,
        }
    nc = bacc.Bacc("TRN2", target_bir_lowering=False, num_devices=1)
    arrays = {f"in_{k}": np.ascontiguousarray(v) for k, v in arrays.items()}
    dram = {k[3:]: nc.dram_tensor(k, v.shape, mybir.dt.from_np(v.dtype), kind="ExternalInput").ap()
            for k, v in arrays.items()}
    out = nc.dram_tensor("out", (T, D), F32, kind="ExternalOutput").ap()
    build(nc, dram, out)
    r = run_bass_kernel_spmd(nc, [arrays], core_ids=[0])
    return r.results[0]["out"].reshape(NSEQ, SEQ, D)
```

```python
from contextlib import ExitStack

import numpy as np
import concourse.bass as bass
from concourse import mybir

ALU = mybir.AluOpType
ACT = mybir.ActivationFunctionType
AX = mybir.AxisListType
F32 = mybir.dt.float32
F32R = mybir.dt.float32r
U32 = mybir.dt.uint32
I32 = mybir.dt.int32

P = 128
D = 256
KC = D // P
NSEQ, SEQ = 4, 256
T = NSEQ * SEQ
NB = T // P
HALF = 512
NH = T // HALF
EPS = 1e-5

HEADS, GROUPS, HD = 16, 4, 16
KV = GROUPS * HD
HJ = HEADS // GROUPS
QB = SEQ // P

NEXP, TOPK, INTER = 32, 4, 96
NCH, CINTER = 16, 128
SMALL = 0.05
EB = NEXP * INTER // P
MOE_IT = 8
MOE_K = 5
MOE_WN = 2 * KC * P + D
ESLOT = [0, 1, 0, 1, 2]
NCW = NEXP + NCH

DI, DS, DCONV, DTR = 512, 16, 4, 128
DB = DI // P
PADC = DCONV - 1
SEGC = SEQ + 2 * PADC
SEGS = SEQ + 1

FI = 688
FB = [(m * P, min(P, FI - m * P)) for m in range((FI + P - 1) // P)]
LUT = 16
LUTW = KC * FI * 2 + len(FB) * D
LCH = 860
assert MOE_K * LCH >= LUTW and 2 * MOE_IT == LUT


START = 5


class Core:

    def __init__(self, nc, ctx):
        self.nc, self.ctx, self.used, self.offset = nc, ctx, [], []

    def sem(self, name):
        self.used.append(self.nc.alloc_semaphore(name=name))
        return self.used[-1]

    def counters(self, prefix, names, by):
        found = [self.sem(prefix + n) for n in names.split()]
        for s in found:
            by.sem_inc(s, START)
        self.offset += [s.name for s in found]
        return found

    def wait(self, e, s, count):
        e.wait_ge(s, count + START if s.name in self.offset else count)

    def kept(self, name):
        return self.nc.alloc_semaphore(name=name)

    def recycle(self):
        self.nc.clear_and_free_semaphores(self.used)
        self.used, self.offset = [], []
        self.nc.all_engine_barrier()

    def sb(self, ctx, name, shape, dt=F32):
        return ctx.enter_context(self.nc.sbuf_tensor(name, shape, dt))

    def sb_twice(self, ctx, name, shape, over, over_shape):
        under = self.sb(ctx, name, shape)
        size = 4 * int(np.prod(shape[1:]))
        assert size % 32 == 0 and np.prod(over_shape[1:]) <= np.prod(shape[1:])
        return under, self.nc.alloc_sbuf_tensor_at(over, over_shape, F32R, offset=self.nc.sbuf_base - size)

    def ps(self, ctx, name, shape):
        return ctx.enter_context(self.nc.psum_tensor(name, shape, F32))


def seq_view(ap, seg, lo):
    return ap.rearrange("p (b s) -> p b s", s=seg)[:, :, lo:lo + SEQ]


def constants(c, g):
    nc = c.nc
    s_set, s_const = c.sem("s_set"), c.sem("s_const")
    with nc.Block() as block:
        @block.gpsimd
        def _(e):
            e.memset(g.ident[:, :], 0.0).then_inc(s_set, 1)
            e.memset(g.gmask[:, :], 1.0).then_inc(s_set, 1)
            e.iota(g.iota_e[:, :], [[1, NEXP]], base=0, channel_multiplier=0,
                   allow_small_or_imprecise_dtypes=True).then_inc(s_const, 1)
            e.iota(g.iota_l[:, :], [[1, LUT]], base=0, channel_multiplier=0,
                   allow_small_or_imprecise_dtypes=True).then_inc(s_const, 1)
            c.wait(e, s_set, 2)
            e.affine_select(out=g.ident[:, :], in_=g.ident[:, :], compare_op=ALU.not_equal, fill=1.0,
                            base=0, pattern=[[-1, P]], channel_multiplier=1).then_inc(s_const, 1)
            e.affine_select(out=g.gmask[:, :], in_=g.gmask[:, :], compare_op=ALU.is_ge, fill=0.0,
                            base=0, pattern=[[-HD, 8]], channel_multiplier=1).then_inc(s_set, 1)
            c.wait(e, s_set, 3)
            e.affine_select(out=g.gmask[:, :], in_=g.gmask[:, :], compare_op=ALU.is_ge, fill=0.0,
                            base=HD - 1, pattern=[[HD, 8]], channel_multiplier=-1).then_inc(s_const, 1)
            c.wait(e, s_const, 4)


def layernorm(c, g, name, src, feat=None, gamma=None, beta=None, hi=None, lo=None, loads=None, stats=None,
              beside=None):
    nc = c.nc
    sem = lambda n: c.sem(f"{name}_{n}")
    s_stat, s_aggr, s_var, s_sd, s_r, s_xn, s_tp, s_ev, s_hi, s_lo = map(
        sem, "stat aggr var sd r xn tp ev hi lo".split())
    with ExitStack() as ctx:
        taken = stats is not None
        stats = stats if taken else c.sb(ctx, name + "_stats", [P, NB, 6])
        mv = c.sb(ctx, name + "_mv", [P, NB, 2])
        sm = c.sb(ctx, name + "_sm", [P, 5, NB])
        xn = c.sb(ctx, name + "_xn", [P, NB, D])
        ps = c.ps(ctx, name + "_ps", [P, KC, T])
        var, sd, r, q = (sm[:, i, :] for i in range(4))
        vector_copies = [1] if gamma is None and hi is None else []
        with nc.Block() as block:
            @block.sync
            def _(e):
                if beside:
                    beside()

            @block.vector
            def _(e):
                for n in range(NB) if not taken else ():
                    if loads:
                        c.wait(e, loads[n // 2], 16)
                    e.bn_stats(stats[:, n, :], src[:, n, :]).then_inc(s_stat, 1)
                for n in range(NB):
                    if not taken:
                        c.wait(e, s_stat, n + 1)
                    e.bn_aggr(mv[:, n, :], stats[:, n, :]).then_inc(s_aggr, 1)
                c.wait(e, s_aggr, NB)
                e.tensor_scalar(var, mv[:, :, 1], EPS, None, ALU.add).then_inc(s_var, 1)
                c.wait(e, s_sd, 1)
                e.reciprocal(r, sd).then_inc(s_r, 1)
                c.wait(e, s_r, 1)
                e.tensor_tensor(q, r, r, ALU.mult).then_inc(s_r, 1)
                c.wait(e, s_r, 2)
                e.tensor_tensor(q, q, var, ALU.mult).then_inc(s_r, 1)
                c.wait(e, s_r, 3)
                e.tensor_scalar(q, q, -0.5, 1.5, ALU.mult, ALU.add).then_inc(s_r, 1)
                c.wait(e, s_r, 4)
                e.tensor_tensor(r, r, q, ALU.mult).then_inc(s_r, 1)
                c.wait(e, s_r, 5)
                for n in range(NB):
                    e.tensor_scalar(xn[:, n, :], src[:, n, :], mv[:, n, 0:1], r[:, n:n + 1],
                                    ALU.subtract, ALU.mult).then_inc(s_xn, 1)
                for k in vector_copies:
                    c.wait(e, s_tp, NB * (k + 1))
                    e.tensor_copy(feat[:, k, :], ps[:, k, :]).then_inc(s_ev, 1)
                for k in range(KC):
                    if lo is not None:
                        c.wait(e, s_hi, k + 1)
                        e.tensor_tensor(lo[:, k, :], ps[:, k, :], hi[:, k, :].bitcast(F32),
                                        ALU.subtract).then_inc(s_lo, 1)

            @block.scalar
            def _(e):
                c.wait(e, s_var, 1)
                e.activation(sd, var, ACT.Sqrt).then_inc(s_sd, 1)
                for k in range(KC):
                    if k in vector_copies:
                        continue
                    c.wait(e, s_tp, NB * (k + 1))
                    if hi is not None:
                        e.activation(hi[:, k, :], ps[:, k, :], ACT.Copy).then_inc(s_hi, 1)
                    elif gamma is None:
                        e.activation(feat[:, k, :], ps[:, k, :], ACT.Copy).then_inc(s_ev, 1)
                    else:
                        e.activation(feat[:, k, :], ps[:, k, :], ACT.Identity, bias=beta[:, k:k + 1],
                                     scale=gamma[:, k:k + 1]).then_inc(s_ev, 1)
                for k in range(KC) if hi is not None and feat is not None else ():
                    c.wait(e, s_lo, k + 1)
                    e.activation(feat[:, k, :], ps[:, k, :], ACT.Copy).then_inc(s_ev, 1)

            @block.tensor
            def _(e):
                for k in range(KC):
                    for n in range(NB):
                        c.wait(e, s_xn, n + 1)
                        e.transpose(ps[:, k, n * P:(n + 1) * P], xn[:, n, k * P:(k + 1) * P],
                                    g.ident[:, :]).then_inc(s_tp, 1)


def attention(c, g, wt, beside):
    nc = c.nc
    sem = c.sem
    s_q, s_k, s_v, s_qh, s_ql, s_kf, s_kh, s_kl, s_ke, s_kd, s_ve, s_km, s_xb = map(
        sem, [f"at_{n}" for n in "q k v qh ql kf kh kl ke kd ve km xb".split()])
    s_vz, s_bn = c.sem("at_vz"), c.sem("at_bn")
    s_vc, s_pn = c.counters("at_", "vc pn", nc.gpsimd)
    s_sc, s_pt, s_pv, s_op = c.counters("at_", "sc pt pv op", nc.tensor)
    s_mx, s_nm, s_pe, s_ri, s_x = c.counters("at_", "mx nm pe ri x", nc.vector)
    s_ex, s_oe, s_qc = c.counters("at_", "ex oe qc", nc.scalar)
    NP = 4
    U = QB * HJ
    SCORES, NORMAL, TURN, VALUES, PROJECT, RESIDUAL = 3, 4, 5, 6, 7, 8
    with ExitStack() as ctx:
        qs = c.sb(ctx, "qs", [P, HJ, T], F32R)
        kh = c.sb(ctx, "kh", [P, GROUPS, T], F32R)
        kl = c.sb(ctx, "kl", [P, GROUPS, T], F32R)
        v = c.sb(ctx, "v", [P, NB, KV])
        with ExitStack() as pctx:
            kf = c.sb(pctx, "kf", [P, T])
            khf = c.sb(pctx, "khf", [P, T], F32R)
            klf = c.sb(pctx, "klf", [P, T])
            m2 = c.sb(pctx, "m2", [P, GROUPS])
            qps = [c.ps(pctx, f"qps{i}", [P, T]) for i in range(2)]
            kps = c.ps(pctx, "kps", [P, T])
            vps = c.ps(pctx, "vps", [P, NB, KV])
            with nc.Block() as block:
                @block.sync
                def _(e):
                    beside()

                @block.tensor
                def _(e):
                    c.wait(e, wt.at_in, wt.at_n)
                    def rows(ps, w):
                        for h in range(NH):
                            for k in range(KC):
                                mm = e.matmul(ps[:, h * HALF:(h + 1) * HALF], w[:, k, :],
                                              g.feat[:, k, h * HALF:(h + 1) * HALF], start=k == 0, stop=k == KC - 1)
                        return mm
                    rows(kps, wt.wk2).then_inc(s_k, 1)
                    for j in range(HJ):
                        if j >= 2:
                            c.wait(e, s_ql, j - 1)
                        rows(qps[j % 2], wt.wq2[:, :, j * P:(j + 1) * P]).then_inc(s_q, 1)
                    for n in range(NB):
                        for k in range(KC):
                            mm = e.matmul(vps[:, n, :], g.feat[:, k, n * P:(n + 1) * P], wt.wv[:, k, :],
                                          start=k == 0, stop=k == KC - 1)
                    mm.then_inc(s_v, 1)

                @block.gpsimd
                def _(e):
                    e.tensor_tensor(m2[:, :], g.gmask[:, 0:GROUPS], g.gmask[:, GROUPS:], ALU.add).then_inc(s_km, 1)
                    c.wait(e, wt.at_in, wt.at_n)
                    e.tensor_tensor(g.x[:, :, :], g.x[:, :, :],
                                    wt.bout[:, :].unsqueeze(1).broadcast_to([P, NB, D]), ALU.add).then_inc(s_xb, 1)

                @block.vector
                def _(e):
                    c.wait(e, s_k, 1)
                    e.tensor_scalar(kf[:, :], kps[:, :], wt.bk[:, 0:1], None, ALU.add).then_inc(s_kf, 1)
                    c.wait(e, s_kh, 1)
                    e.tensor_tensor(klf[:, :], kf[:, :], khf[:, :].bitcast(F32), ALU.subtract).then_inc(s_kl, 1)
                    c.wait(e, s_kl, 1)
                    c.wait(e, s_km, 1)
                    for i in range(GROUPS):
                        e.tensor_scalar(kl[:, i, :], klf[:, :], m2[:, i:i + 1], None, ALU.mult).then_inc(s_kd, 1)
                        c.wait(e, s_qh, i + 1)
                        e.scalar_tensor_tensor(qs[KV:P, i, :], qps[i % 2][KV:P, :], wt.bq2[KV:P, i:i + 1],
                                               qs[KV:P, i, :].bitcast(F32), ALU.add, ALU.subtract).then_inc(s_ql, 1)
                    c.wait(e, s_v, 1)
                    e.tensor_tensor(v[:, :, :], vps[:, :, :],
                                    wt.bv[:, :].unsqueeze(1).broadcast_to([P, NB, KV]), ALU.add).then_inc(s_ve, 1)

                @block.scalar
                def _(e):
                    c.wait(e, s_kf, 1)
                    e.activation(khf[:, :], kf[:, :], ACT.Copy).then_inc(s_kh, 1)
                    c.wait(e, s_km, 1)
                    for j in range(HJ):
                        c.wait(e, s_q, j + 1)
                        e.activation(qs[:, j, :], qps[j % 2][:, :], ACT.Identity,
                                     bias=wt.bq2[:, j:j + 1]).then_inc(s_qh, 1)
                        c.wait(e, s_kh, 1)
                        e.activation(kh[:, j, :], khf[:, :].bitcast(F32), ACT.Copy,
                                     scale=m2[:, j:j + 1]).then_inc(s_ke, 1)

        VW = KV + HD
        qcur = c.sb(ctx, "qcur", [P, HJ, SEQ], F32R)
        vcur = c.sb(ctx, "vcur", [P, QB, GROUPS * VW])
        prob = c.sb(ctx, "prob", [P, NP, GROUPS, SEQ])
        pT = c.sb(ctx, "pT", [P, 2, QB, GROUPS, P])
        mx = c.sb(ctx, "mx", [P, 2, U, GROUPS])
        rs = c.sb(ctx, "rs", [P, U, GROUPS])
        ri = c.sb(ctx, "ri", [P, U, GROUPS])
        oT = c.sb(ctx, "oT", [P, 2, KC, P])
        sps = c.ps(ctx, "sps", [P, 2, GROUPS, SEQ])
        tps = c.ps(ctx, "tps", [P, QB, GROUPS, P])
        ops = c.ps(ctx, "ops", [P, HALF])
        mps = c.ps(ctx, "mps", [P, HALF])

        def pipeline(e, *stages):
            def step(b, i):
                for lag, run in stages:
                    back, u = divmod(i - lag, U)
                    n = b * U + (i - lag)
                    if not isinstance(b, int) or 0 <= n < NSEQ * U:
                        run(n, u, b + back)

            for i in range(U):
                step(0, i)
            with e.Fori(1, NSEQ) as b:
                for i in range(U):
                    step(b, i)
            for i in range(U):
                step(NSEQ, i)

        def at_query_block(run):
            return lambda n, u, s: run(s * QB + u // HJ, u // HJ) if u % HJ == HJ - 1 else None

        with nc.Block() as block:
            @block.gpsimd
            def _(e):
                e.memset(vcur[:, :, :], 0.0).then_inc(s_vz, 1)
                c.wait(e, s_vz, 1)

                def copy_values(n, u, s):
                    if u == 0:
                        c.wait(e, s_pv, n)
                        e.tensor_copy(vcur[:, :, :].rearrange("p k (g w) -> p k g w", w=VW)[:, :, :, 0:HD],
                                      v[:, bass.ds(s * QB, QB), :].rearrange("p k (g w) -> p k g w", w=HD)
                                      ).then_inc(s_vc, 1)

                def normalise(n, u, s):
                    c.wait(e, s_ri, n + 1)
                    e.tensor_tensor(prob[:, u % NP, :, :], prob[:, u % NP, :, :],
                                    ri[:, u, :].unsqueeze(2).broadcast_to([P, GROUPS, SEQ]), ALU.mult
                                    ).then_inc(s_pn, 1)

                pipeline(e, (VALUES, copy_values), (NORMAL, normalise))

            @block.tensor
            def _(e):
                def scores(n, u, s):
                    qb, j = divmod(u, HJ)
                    if j == 0:
                        c.wait(e, s_qc, s * QB + (qb + 1))
                    c.wait(e, s_ex, n - 1)
                    for gg in range(0, GROUPS, 2):
                        for i, k in enumerate((kh, kl)):
                            mm = e.matmul(sps[:, u % 2, gg:gg + 2, :], qcur[:, j, qb * P:(qb + 1) * P],
                                          k[:, gg:gg + 2, bass.ds(s * SEQ, SEQ)], start=i == 0, stop=i == 1)
                    mm.then_inc(s_sc, 1)

                def turn(n, u, s):
                    c.wait(e, s_pn, n + 1)
                    c.wait(e, s_pe, n)
                    for kb in range(QB):
                        for gg in range(GROUPS):
                            mm = e.transpose(tps[:, kb, gg, :], prob[:, u % NP, gg, kb * P:(kb + 1) * P],
                                             g.ident[:, :])
                    mm.then_inc(s_pt, 1)

                def values(n, u, s):
                    qb, j = divmod(u, HJ)
                    c.wait(e, s_pe, n + 1)
                    if u == 0:
                        c.wait(e, s_vc, s + 1)
                    if j == 0:
                        c.wait(e, s_oe, s * QB + qb)
                    r0 = j % 2 * KV
                    terms = [(gg, kb) for gg in range(GROUPS) for kb in range(QB)]
                    for i, (gg, kb) in enumerate(terms):
                        mm = e.matmul(ops[r0:r0 + KV, j // 2 * P:(j // 2 + 1) * P],
                                      vcur[:, kb, gg * KV:(gg + 1) * KV], pT[:, u % 2, kb, gg, :],
                                      start=i == 0, stop=i == len(terms) - 1)
                    mm.then_inc(s_pv, 1)

                def out_proj(q, qb):
                    c.wait(e, s_oe, q + 1)
                    c.wait(e, s_x, q)
                    for k in range(KC):
                        mm = e.matmul(mps[:, 0:D], oT[:, qb, k, :], wt.wout[:, k, :],
                                      start=k == 0, stop=k == KC - 1)
                    mm.then_inc(s_op, 1)

                pipeline(e, (SCORES, scores), (TURN, turn), (VALUES, values), (PROJECT, at_query_block(out_proj)))

            @block.vector
            def _(e):
                def maximum(n, u, s):
                    c.wait(e, s_sc, n + 1)
                    e.tensor_reduce(mx[:, 0, u, :], sps[:, u % 2, :, :], AX.X, ALU.max).then_inc(s_mx, 1)
                    c.wait(e, s_mx, n + 1)
                    e.tensor_scalar(mx[:, 1, u, :], mx[:, 0, u, :], -1.0 / HD, None, ALU.mult).then_inc(s_nm, 1)

                def inverse(n, u, s):
                    c.wait(e, s_ex, n + 1)
                    e.reciprocal(ri[:, u, :], rs[:, u, :]).then_inc(s_ri, 1)

                def copy_out(n, u, s):
                    c.wait(e, s_pt, n + 1)
                    c.wait(e, s_pv, n - 1)
                    e.tensor_copy(pT[:, u % 2, :, :, :], tps[:, :, :, :]).then_inc(s_pe, 1)

                def residual(q, qb):
                    c.wait(e, s_op, q + 1)
                    xs = g.x[:, bass.ds(q, 1), :].rearrange("p a d -> p (a d)")
                    e.tensor_tensor(xs, mps[:, 0:D], xs, ALU.add).then_inc(s_x, 1)
                    c.wait(e, s_x, q + 1)
                    e.bn_stats(g.stats[:, bass.ds(q, 1), :].rearrange("p a d -> p (a d)"), xs).then_inc(s_bn, 1)

                pipeline(e, (NORMAL, inverse), (SCORES, maximum), (TURN, copy_out),
                         (RESIDUAL, at_query_block(residual)))

            @block.scalar
            def _(e):
                def copy_queries(n, u, s):
                    qb, j = divmod(u, HJ)
                    if j == 0:
                        c.wait(e, s_sc, n - HJ)
                        e.activation(qcur[:, :, qb * P:(qb + 1) * P],
                                     qs[:, :, bass.ds(s * SEQ + qb * P, P)].bitcast(F32), ACT.Copy).then_inc(s_qc, 1)

                def exps(n, u, s):
                    c.wait(e, s_nm, n + 1)
                    c.wait(e, s_pt, n - (NP - 1))
                    for gg in range(GROUPS):
                        a = e.activation(prob[:, u % NP, gg, :], sps[:, u % 2, gg, :], ACT.Exp,
                                         bias=mx[:, 1, u, gg:gg + 1], scale=1.0 / HD,
                                         accum_out=rs[:, u, gg:gg + 1])
                    a.then_inc(s_ex, 1)

                def heads_out(q, qb):
                    c.wait(e, s_pv, (q + 1) * HJ)
                    c.wait(e, s_op, q - 1)
                    e.activation(oT[:, qb, :, :].rearrange("p k t -> p (k t)"), ops[:, 0:KC * P],
                                 ACT.Copy).then_inc(s_oe, 1)

                pipeline(e, (0, copy_queries), (SCORES, exps), (VALUES, at_query_block(heads_out)))


def routing(c, g, dram, wt):
    nc = c.nc
    s_lg, s_le, s_m8, s_ix, s_if, s_eq, s_mk, s_sh, s_ex, s_me, s_sm, s_rc, s_cw, s_pr, s_tp, s_te, s_st, s_li = map(
        c.sem, [f"rt_{n}" for n in "lg le m8 ix if eq mk sh ex me sm rc cw pr tp te st li".split()])
    with ExitStack() as ctx:
        lg = c.sb(ctx, "lg", [P, NB, NEXP])
        m8 = c.sb(ctx, "m8", [P, NB, 8])
        i8 = c.sb(ctx, "i8", [P, NB, 8], U32)
        f8 = c.sb(ctx, "f8", [P, NB, 8])
        eq = c.sb(ctx, "eq", [P, NB, TOPK, NEXP])
        mask = c.sb(ctx, "mask", [P, NB, NEXP])
        ex = c.sb(ctx, "ex", [P, NB, NEXP])
        sm = c.sb(ctx, "rsm", [P, 2, NB])
        cw = c.sb(ctx, "cw", [P, NB, NCW])
        cwT = c.sb(ctx, "cwT", [NCW, T])
        lps = c.ps(ctx, "lps", [P, NB, NEXP])
        tps = c.ps(ctx, "ctps", [NCW, T])
        with nc.Block() as block:
            @block.sync
            def _(e):
                e.dma_start(g.lut_i[:, :], dram["lut_idx"]).then_inc(s_li, 16)
                c.wait(e, s_te, 1)
                e.dma_start(dram["cw"], cwT[:, :]).then_inc(s_st, 16)
                c.wait(e, s_st, 16)
                c.wait(e, s_li, 16)

            @block.tensor
            def _(e):
                c.wait(e, wt.late_in, wt.late_n)
                for n in range(NB):
                    for k in range(KC):
                        mm = e.matmul(lps[:, n, :], g.feat[:, k, n * P:(n + 1) * P], wt.gate[:, k, :],
                                      start=k == 0, stop=k == KC - 1)
                mm.then_inc(s_lg, 1)
                c.wait(e, s_cw, 1)
                c.wait(e, s_pr, 2)
                for n in range(NB):
                    mm = e.transpose(tps[:, n * P:(n + 1) * P], cw[:, n, :], g.ident[:, :])
                mm.then_inc(s_tp, 1)

            @block.vector
            def _(e):
                c.wait(e, s_lg, 1)
                e.tensor_copy(lg[:, :, :], lps[:, :, :]).then_inc(s_le, 1)
                c.wait(e, s_le, 1)
                for n in range(NB):
                    e.max(m8[:, n, :], lg[:, n, :]).then_inc(s_m8, 1)
                c.wait(e, s_m8, NB)
                e.tensor_tensor(ex[:, :, :], lg[:, :, :], m8[:, :, 0:1].broadcast_to([P, NB, NEXP]),
                                ALU.subtract).then_inc(s_sh, 1)
                for n in range(NB):
                    e.max_index(i8[:, n, :], m8[:, n, :], lg[:, n, :]).then_inc(s_ix, 1)
                c.wait(e, s_ix, NB)
                e.tensor_copy(f8[:, :, :], i8[:, :, :]).then_inc(s_if, 1)
                c.wait(e, s_if, 1)
                e.tensor_tensor(eq[:, :, :, :],
                                g.iota_e[:, :].unsqueeze(1).unsqueeze(1).broadcast_to([P, NB, TOPK, NEXP]),
                                f8[:, :, 0:TOPK].unsqueeze(3).broadcast_to([P, NB, TOPK, NEXP]),
                                ALU.is_equal).then_inc(s_eq, 1)
                c.wait(e, s_eq, 1)
                e.tensor_reduce(mask[:, :, :], eq[:, :, :, :].rearrange("p n k e -> p n e k"), AX.X,
                                ALU.add).then_inc(s_mk, 1)
                c.wait(e, s_mk, 1)
                c.wait(e, s_ex, 1)
                e.tensor_tensor(mask[:, :, :], mask[:, :, :], ex[:, :, :], ALU.mult).then_inc(s_me, 1)
                c.wait(e, s_me, 1)
                e.tensor_reduce(sm[:, 0, :], mask[:, :, :], AX.X, ALU.add).then_inc(s_sm, 1)
                c.wait(e, s_sm, 1)
                e.reciprocal(sm[:, 1, :], sm[:, 0, :]).then_inc(s_rc, 1)
                c.wait(e, s_rc, 1)
                e.tensor_tensor(cw[:, :, 0:NEXP], mask[:, :, :], sm[:, 1, :].unsqueeze(2)
                                .broadcast_to([P, NB, NEXP]), ALU.mult).then_inc(s_cw, 1)
                c.wait(e, s_cw, 1)
                pair = cw[:, :, 0:NEXP].rearrange("p n (c a) -> p n c a", a=2)
                e.tensor_tensor(cw[:, :, NEXP:NCW], pair[:, :, :, 0], pair[:, :, :, 1], ALU.add).then_inc(s_pr, 1)
                c.wait(e, s_pr, 1)
                e.tensor_scalar(cw[:, :, NEXP:NCW], cw[:, :, NEXP:NCW], SMALL, None, ALU.mult).then_inc(s_pr, 1)
                c.wait(e, s_li, 16)
                e.tensor_copy(g.lut_f[:, 0:LUTW], g.lut_i[:, :]).then_inc(s_li, 1)
                e.memset(g.lut_f[:, LUTW:], 0.0).then_inc(s_li, 1)
                e.memset(g.lutw[:, :], 0.0).then_inc(s_li, 1)
                c.wait(e, s_tp, 1)
                e.tensor_copy(cwT[:, :], tps[:, :]).then_inc(s_te, 1)

            @block.scalar
            def _(e):
                c.wait(e, s_sh, 1)
                e.activation(ex[:, :, :], ex[:, :, :], ACT.Exp).then_inc(s_ex, 1)


def experts(c, g, dram, xh, xl):
    nc = c.nc
    s_w = [c.sem(f"ex_w{k}") for k in range(MOE_K)]
    s_c = [c.sem(f"ex_c{k}") for k in range(MOE_K)]
    s_z = c.sem("ex_z")
    s_g, s_u, s_d = c.counters("ex_", "g u d", nc.tensor)
    s_wl, s_tc, s_a, s_le = c.counters("ex_", "wl tc a le", nc.vector)
    s_wh, s_si, s_ah = c.counters("ex_", "wh si ah", nc.scalar)
    s_al, s_la = c.counters("ex_", "al la", nc.gpsimd)
    s_ye, s_yt, s_yx = map(c.sem, ["ex_ye", "ex_yt", "ex_yx"])
    K, LAST = MOE_K, MOE_IT * MOE_K
    with ExitStack() as ctx:
        wr = c.sb(ctx, "wr", [P, K, MOE_WN])
        wh = c.sb(ctx, "wh", [P, K, MOE_WN], F32R)
        wl = c.sb(ctx, "wl", [P, K, MOE_WN], F32R)
        cwb = c.sb(ctx, "cwb", [P, 3, T])
        si = c.sb(ctx, "si", [P, 3, T])
        a = c.sb(ctx, "a", [P, 3, T])
        ah = c.sb(ctx, "ah", [P, 3, T], F32R)
        al = c.sb(ctx, "al", [P, 3, T], F32R)
        lt = c.sb(ctx, "lt", [P, 2, LCH])
        gps = c.ps(ctx, "gps", [P, T])
        ups = c.ps(ctx, "ups", [P, T])
        yps = c.ps(ctx, "yps", [P, KC, T])
        yT = a[:, 0:KC, :]
        ZA, ZW = ESLOT[-1], K - 1

        def half(h):
            return slice(h * HALF, (h + 1) * HALF)

        with nc.Block() as block:
            @block.sync
            def _(e):
                def load(index, slot):
                    e.dma_start(wr[:, slot, :], dram["moe_w"][index, :, :].rearrange("a p n -> (a p) n")
                                ).then_inc(s_w[slot], 16)

                load(slice(0, 1), 0)
                with e.Fori(0, MOE_IT) as j:
                    for k in range(K):
                        n, s = j * K + k, ESLOT[k]
                        c.wait(e, s_tc, n + 1 if k >= 2 else n)
                        if k < 3:
                            r0 = k * P
                            cut = (r0 // INTER + 1) * INTER - r0
                            for p0, p1 in [(0, cut), (cut, P)]:
                                e.dma_start(cwb[p0:p1, s, :],
                                            dram["cw"][bass.ds(4 * j + (r0 + p0) // INTER, 1), :]
                                            .broadcast_to([p1 - p0, T])).then_inc(s_c[k], 16)
                        else:
                            e.dma_start(cwb[:, s, :], dram["cw"][bass.ds(2 * j + (NEXP + k - 3), 1), :]
                                        .broadcast_to([P, T])).then_inc(s_c[k], 16)
                        c.wait(e, s_wl, n)
                        load(bass.ds(n + 1, 1), (k + 1) % K)

            def split_high(e, slot, loaded):
                c.wait(e, s_w[slot], loaded)
                e.activation(wh[:, slot, :], wr[:, slot, :], ACT.Copy).then_inc(s_wh, 1)

            def split_low(e, slot, done):
                c.wait(e, s_wh, done)
                e.tensor_tensor(wl[:, slot, :], wr[:, slot, :], wh[:, slot, :].bitcast(F32),
                                ALU.subtract).then_inc(s_wl, 1)

            @block.scalar
            def _(e):
                split_high(e, 0, 16)
                with e.Fori(0, MOE_IT) as j:
                    for k in range(K):
                        n, s = j * K + k, ESLOT[k]
                        c.wait(e, s_g, n + 1)
                        e.activation(si[:, s, :], gps[:, :], ACT.Silu).then_inc(s_si, 1)
                        c.wait(e, s_d, n + 1)
                        c.wait(e, s_wl, n + 1)
                        split_high(e, (k + 1) % K, j * 16 + (16 if k < K - 1 else 32))
                        c.wait(e, s_a, n + 1)
                        e.activation(ah[:, s, :], a[:, s, :], ACT.Copy).then_inc(s_ah, 1)
                c.wait(e, s_d, LAST + 2)
                c.wait(e, s_al, LAST)
                for q in range(KC):
                    e.activation(yT[:, q, :], yps[:, q, :], ACT.Copy).then_inc(s_ye, 1)

            @block.vector
            def _(e):
                e.memset(ah[:, ZA, :].bitcast(F32), 0.0).then_inc(s_z, 1)
                e.memset(wh[:, ZW, :].bitcast(F32), 0.0).then_inc(s_tc, 1)
                e.memset(wl[:, ZW, :].bitcast(F32), 0.0).then_inc(s_tc, 1)
                split_low(e, 0, 1)
                with e.Fori(0, MOE_IT) as j:
                    for k in range(K):
                        n, s = j * K + k, ESLOT[k]
                        c.wait(e, s_si, n + 1)
                        c.wait(e, s_c[k], (j + 1) * (32 if k < 3 else 16))
                        e.tensor_tensor(si[:, s, :], si[:, s, :], cwb[:, s, :], ALU.mult).then_inc(s_tc, 1)
                        c.wait(e, s_la, 2 * n)
                        for q in range(2):
                            e.tensor_scalar(lt[:, q, :], g.lut_f[:, k * LCH:(k + 1) * LCH],
                                            g.iota_l[:, bass.ds(2 * j + q, 1)], g.lutb[:, bass.ds(2 * j + q, 1)],
                                            ALU.is_equal, ALU.mult).then_inc(s_le, 1)
                        split_low(e, (k + 1) % K, n + 2)
                        c.wait(e, s_tc, n + 3)
                        c.wait(e, s_u, n + 1)
                        e.tensor_tensor(a[:, s, :], ups[:, :], si[:, s, :], ALU.mult).then_inc(s_a, 1)
                for n in range(NB):
                    c.wait(e, s_yt, n // 2 + 1)
                    yb = gps if n < NB // 2 else ups
                    e.tensor_tensor(g.x[:, n, :], yb[:, (n % 4) * D:(n % 4 + 1) * D], g.x[:, n, :],
                                    ALU.add).then_inc(s_yx, 1)

            @block.gpsimd
            def _(e):
                e.memset(al[:, ZA, :].bitcast(F32), 0.0).then_inc(s_z, 1)
                with e.Fori(0, MOE_IT) as j:
                    for k in range(K):
                        n, s = j * K + k, ESLOT[k]
                        for q in range(2):
                            c.wait(e, s_le, n * 2 + q + 1)
                            c.wait(e, s_la, n * 2 + q)
                            part = g.lutw[:, k * LCH:(k + 1) * LCH]
                            e.tensor_tensor(part, part, lt[:, q, :], ALU.add).then_inc(s_la, 1)
                        c.wait(e, s_ah, n + 1)
                        e.tensor_tensor(al[:, s, :], a[:, s, :], ah[:, s, :].bitcast(F32),
                                        ALU.subtract).then_inc(s_al, 1)

            @block.tensor
            def _(e):
                def rows(ps, slot, part, sem):
                    for h in range(NH):
                        terms = [(w, x, q) for q in range(KC) for w, x in ((wh, xh), (wh, xl), (wl, xh))]
                        for i, (w, x, q) in enumerate(terms):
                            o = (part * KC + q) * P
                            mm = e.matmul(ps[:, half(h)], w[:, slot, o:o + P], x[:, q, half(h)],
                                          start=i == 0, stop=i == len(terms) - 1)
                    mm.then_inc(sem, 1)

                def down(slot, wslot, first=False):
                    for q in range(KC):
                        o = 2 * KC * P + q * P
                        for i, (w, x) in enumerate(((wh, ah), (wl, ah), (wh, al))):
                            for h in range(NH):
                                mm = e.matmul(yps[:, q, half(h)], w[:, wslot, o:o + P], x[:, slot, half(h)],
                                              start=first and i == 0, stop=False, skip_group_check=True)
                    mm.then_inc(s_d, 1)

                c.wait(e, s_z, 2)
                c.wait(e, s_tc, 2)
                down(ZA, ZW, first=True)
                with e.Fori(0, MOE_IT) as j:
                    for k in range(K):
                        n = j * K + k
                        c.wait(e, s_wl, n + 1)
                        c.wait(e, s_si, n)
                        rows(gps, k, 0, s_g)
                        c.wait(e, s_a, n)
                        rows(ups, k, 1, s_u)
                        c.wait(e, s_al, n)
                        down(ESLOT[k - 1], (k - 1) % K)
                c.wait(e, s_al, LAST)
                down(ZA, ZW)
                for n in range(NB):
                    c.wait(e, s_ye, KC)
                    yb = gps if n < NB // 2 else ups
                    for q in range(KC):
                        o = (n % 4) * D + q * P
                        mm = e.transpose(yb[:, o:o + P], yT[:, q, n * P:(n + 1) * P], g.ident[:, :])
                    if n % 2:
                        mm.then_inc(s_yt, 1)


def mamba_input(c, g, wt, acc, hh, hl, w, sc):
    nc = c.nc
    s_mm, s_h, s_hh, s_hl = map(c.sem, [f"mi_{n}" for n in "mm h hh hl".split()])
    split_high, split_low = split_weights(c, "fm", sc)
    b = wt.b_in
    with ExitStack() as ctx:
        ps = c.ps(ctx, "mi_ps", [P, KC, T])
        with nc.Block() as block:
            @block.tensor
            def _(e):
                for m in range(KC):
                    for h in range(NH):
                        for k in range(KC):
                            mm = e.matmul(ps[:, m, h * HALF:(h + 1) * HALF], wt.w_in[:, k, m * P:(m + 1) * P],
                                          g.feat[:, k, h * HALF:(h + 1) * HALF], start=k == 0, stop=k == KC - 1)
                    mm.then_inc(s_mm, 1)

            @block.scalar
            def _(e):
                split_high(e, w)
                for m in range(KC):
                    c.wait(e, s_mm, m + 1)
                    e.activation(acc[:, m, :], ps[:, m, :], ACT.Gelu, bias=b[:, m:m + 1]).then_inc(s_h, 1)
                    c.wait(e, s_h, m + 1)
                    e.activation(hh[:, m, :], acc[:, m, :], ACT.Copy).then_inc(s_hh, 1)

            @block.vector
            def _(e):
                split_low(e, w)
                for m in range(KC):
                    c.wait(e, s_hh, m + 1)
                    e.tensor_tensor(hl[:, m, :], acc[:, m, :], hh[:, m, :].bitcast(F32), ALU.subtract).then_inc(s_hl, 1)


def split_weights(c, name, sc):
    s_wh, s_wl = c.sem(name + "_wh"), c.sem(name + "_wl")
    parts = [slice(i * D, (i + 1) * D) for i in range(2 * DI // D)]

    def high(e, w):
        c.wait(e, w.ready, w.count)
        for p in parts:
            e.activation(sc.wh[:, :, p], w.win[:, :, p], ACT.Copy).then_inc(s_wh, 1)

    def low(e, w):
        for i, p in enumerate(parts):
            c.wait(e, s_wh, i + 1)
            e.tensor_tensor(sc.wl[:, :, p], w.win[:, :, p], sc.wh[:, :, p].bitcast(F32),
                            ALU.subtract).then_inc(s_wl, 1)

    return high, low


def mamba_weights(c, dram, dr, w):
    chunks = lambda n: dram[f"{dr}_{n}"].rearrange("(k p) n -> p k n", p=P)
    w.ready = c.kept(dr + "_w_in")
    w.count = fetch(c.nc, w.ready, [
        (w.win[:, :, :], chunks("in_wT")), (w.cvw[:, :, :], chunks("conv_w")), (w.cvb[:, :], dram[dr + "_conv_b"]),
        (w.xp[:, :, :], chunks("xproj_wT")), (w.dt[:, :], dram[dr + "_dt_wT"]), (w.dtb[:, :], dram[dr + "_dt_b"]),
        (w.A[:, :, :], chunks("A_log")), (w.Dv[:, :], dram[dr + "_D"]), (w.out[:, :, :], chunks("out_wT"))])


def mamba_direction(c, g, dram, dr, rev, hh, hl, w, xi, sz, dt, u, acc, sc):
    project = mamba_project(c, g, dram, dr, rev, hh, hl, w, xi, sz, dt, u, sc)
    scan = mamba_scan(c, g, dram, dr, rev, w, xi, sz, dt, u, acc, sc)
    with c.nc.Block() as block:
        for on, *parts in zip((block.sync, block.gpsimd, block.scalar, block.vector, block.tensor), project, scan):
            @on
            def _(e):
                for part in parts:
                    part(e)


def mamba_project(c, g, dram, dr, rev, hh, hl, w, xi, sz, dt, u, sc):
    sc.landed = [c.sem(f"{dr}_bb{i}") for i in range(2)]
    s_x, s_z, s_pad, s_cp, s_cv, s_xi, s_sz, s_xp, s_xe, s_bc, s_dm, s_ab, s_e1, s_l1, s_mx, s_dt, s_u, s_A, s_dd, s_sz3 = map(
        c.sem, [f"{dr}_{n}" for n in "x z pad cp cv xi sz xp xe bc dm ab e1 l1 mx dt u A dd sz3".split()])
    by_seq = lambda ap: ap.rearrange("p (b s) -> p b s", s=SEQ)
    raw, cv, dtr, bcr, ps = sc.raw, sc.cv, sc.dtr, sc.bcr, sc.ps
    BC, LR, DTB, ZB = 1, 2, [3, 1, 2, 0], [0, 3, 1, 2]
    def sync(e):
        c.wait(e, s_xe, 1)
        e.dma_start(dram["bc"], bcr[:, :]).then_inc(s_bc, 16)
        c.wait(e, s_bc, 16)
        for q in range(2):
            load_state(e, dram, sc, q, slice(q, q + 1), slice(DS + q, DS + q + 1))
        if w.after:
            c.wait(e, s_z, DB)
            c.wait(e, s_cv, PADC * DB)
            c.wait(e, s_mx, DB)
            mamba_weights(c, dram, "bm", w.after)

    def tensor(e):
        c.wait(e, w.ready, w.count)
        def in_proj(m, b, sem):
            for h in range(NH):
                terms = [(wp, x, k) for k in range(KC) for wp, x in ((sc.wh, hh), (sc.wh, hl), (sc.wl, hh))]
                for i, (wp, x, k) in enumerate(terms):
                    mm = e.matmul(ps[b][:, h * HALF:(h + 1) * HALF], wp[:, k, m * P:(m + 1) * P],
                                  x[:, k, h * HALF:(h + 1) * HALF], start=i == 0, stop=i == len(terms) - 1)
            mm.then_inc(sem, 1)
        for m in range(DB):
            in_proj(m, m, s_x)
        c.wait(e, s_cp, LR + 1)
        for k in range(DB):
            c.wait(e, s_xi, k + 1)
            for b, lo, hi in ((BC, DTR, DTR + 2 * DS), (LR, 0, DTR)):
                for h in range(NH):
                    mm = e.matmul(ps[b][0:hi - lo, h * HALF:(h + 1) * HALF], w.xp[:, k, lo:hi],
                                  xi[:, k, h * HALF:(h + 1) * HALF], start=k == 0, stop=k == DB - 1)
                if k == DB - 1:
                    mm.then_inc(s_xp, 1)
        in_proj(DB, ZB[0], s_z)
        c.wait(e, s_xe, 2)
        for d in range(DB):
            if DTB[d] == ZB[0]:
                c.wait(e, s_sz, 1)
            for h in range(NH):
                mm = e.matmul(ps[DTB[d]][:, h * HALF:(h + 1) * HALF], w.dt[:, d * P:(d + 1) * P],
                              dtr[:, h * HALF:(h + 1) * HALF], start=True, stop=True)
            mm.then_inc(s_dm, 1)
        for m in range(1, DB):
            c.wait(e, s_mx, DTB.index(ZB[m]) + 1)
            in_proj(DB + m, ZB[m], s_z)

    def gpsimd(e):
        def zero_column(ap):
            col = SEQ if rev else 0
            e.memset(ap.rearrange("p b (n s) -> p b n s", s=SEGS)[:, :, :, col:col + 1], 0.0).then_inc(s_pad, 1)

        pads = raw[:, :, :].rearrange("p b (n s) -> p b n s", s=SEGC)
        e.memset(pads[:, :, :, 0:PADC], 0.0).then_inc(s_pad, 1)
        e.memset(pads[:, :, :, PADC + SEQ:], 0.0).then_inc(s_pad, 1)
        zero_column(sc.uB[:, :, :])
        c.wait(e, w.ready, w.count)
        c.wait(e, s_A, 1)
        e.tensor_scalar(w.A[:, :, :], w.A[:, :, :], -1.0, None, ALU.mult).then_inc(s_A, 1)
        for d in range(DB):
            e.tensor_scalar(sc.dD[:, d, :], g.ident[:, :], w.Dv[:, d:d + 1], None, ALU.mult).then_inc(s_dd, 1)
        c.wait(e, s_z, DB)
        zero_column(sc.dA[:, :, :])

    def scalar(e):
        c.wait(e, w.ready, w.count)
        e.activation(w.A[:, :, :], w.A[:, :, :], ACT.Exp).then_inc(s_A, 1)
        c.wait(e, s_pad, 2)
        def copy_in(m):
            if m >= 2:
                c.wait(e, s_cv, PADC * (m - 1))
            c.wait(e, s_x, m + 1)
            e.activation(seq_view(raw[:, m % 2, :], SEGC, PADC), by_seq(ps[m][:, :]), ACT.Copy)
            if m >= 2:
                c.wait(e, s_xi, m - 1)
            e.activation(cv[:, m % 2, :], ps[m][:, :], ACT.Identity, bias=w.cvb[:, m:m + 1],
                         scale=w.cvw[:, m, PADC:DCONV]).then_inc(s_cp, 1)

        def silu_x(m):
            c.wait(e, s_cv, PADC * (m + 1))
            e.activation(xi[:, m, :], cv[:, m % 2, :], ACT.Silu).then_inc(s_xi, 1)

        copy_in(0)
        copy_in(1)
        silu_x(0)
        copy_in(2)
        silu_x(1)
        copy_in(3)
        silu_x(2)
        silu_x(3)
        for i, (b, dst) in enumerate([(BC, bcr[:, :]), (LR, dtr[:, :])]):
            c.wait(e, s_xp, i + 1)
            e.activation(dst, ps[b][0:dst.shape[0], :], ACT.Copy).then_inc(s_xe, 1)
        c.wait(e, s_z, 1)
        e.activation(sz[:, 0, :], ps[ZB[0]][:, :], ACT.Silu).then_inc(s_sz, 1)
        for d in range(DB):
            c.wait(e, s_dm, d + 1)
            e.activation(dt[:, d, :], ps[DTB[d]][:, :], ACT.Abs, bias=w.dtb[:, d:d + 1]).then_inc(s_ab, 1)
            c.wait(e, s_ab, d + 1)
            e.activation(dt[:, d, :], dt[:, d, :], ACT.Exp, scale=-1.0).then_inc(s_e1, 1)
        for d in range(DB):
            c.wait(e, s_e1, d + 1)
            e.activation(dt[:, d, :], dt[:, d, :], ACT.Ln, bias=1.0).then_inc(s_l1, 1)
        c.wait(e, s_z, DB)
        e.activation(sz[:, DB - 1, :], ps[ZB[DB - 1]][:, :], ACT.Copy).then_inc(s_sz3, 1)

    def vector(e):
        c.wait(e, w.ready, w.count)
        for m in range(DB):
            c.wait(e, s_cp, m + 1)
            out = by_seq(cv[:, m % 2, :])
            for t in range(PADC):
                src = seq_view(raw[:, m % 2, :], SEGC, 2 * PADC - t if rev else t)
                c.wait(e, s_cv, m * PADC + t)
                e.scalar_tensor_tensor(out, src, w.cvw[:, m, t:t + 1], out,
                                       ALU.mult, ALU.add).then_inc(s_cv, 1)
        for d in range(DB):
            c.wait(e, s_ab, d + 1)
            e.tensor_scalar(u[:, d, :], ps[DTB[d]][:, :], w.dtb[:, d:d + 1], 0.0,
                            ALU.add, ALU.max).then_inc(s_mx, 1)
        def z_out(m):
            c.wait(e, s_z, m + 1)
            e.tensor_copy(sz[:, m, :], ps[ZB[m]][:, :]).then_inc(s_sz, 1)

        z_out(1)
        z_out(2)
        for d in range(DB):
            c.wait(e, s_l1, d + 1)
            c.wait(e, s_mx, d + 1)
            e.tensor_tensor(dt[:, d, :], dt[:, d, :], u[:, d, :], ALU.add).then_inc(s_dt, 1)
            c.wait(e, s_dt, d + 1)
            e.tensor_tensor(u[:, d, :], dt[:, d, :], xi[:, d, :], ALU.mult).then_inc(s_u, 1)

    sc.pad, sc.dt_in, sc.u_in, sc.A_in, sc.dD_in = s_pad, s_dt, s_u, s_A, s_dd
    sc.z_out, sc.ZB = [(s_mx, DB), (s_sz, 2), (s_sz, 3), (s_sz3, 1)], ZB
    return sync, gpsimd, scalar, vector, tensor


def load_state(e, dram, sc, q, b_row, c_row):
    e.dma_start(sc.Bb[:, q, :], dram["bc"][b_row, :].broadcast_to([P, T])).then_inc(sc.landed[q], 16)
    e.dma_start(sc.Cb[:, q, :], dram["bc"][c_row, :].broadcast_to([P, T])).then_inc(sc.landed[q], 16)


def mamba_scan(c, g, dram, dr, rev, w, xi, sz, dt, u, acc, sc):
    nc = c.nc
    s_bb = sc.landed
    split_high, split_low = split_weights(c, dr + "s", sc)
    s_y, s_om, s_oa, s_si = map(c.sem, [f"{dr}s_{n}" for n in "y om oa si".split()])
    s_da, = c.counters(dr, "s_da", nc.scalar)
    s_ub, = c.counters(dr, "s_ub", nc.gpsimd)
    s_sc, s_hc = c.counters(dr, "s_sc s_hc", nc.vector)
    s_ac, = c.counters(dr, "s_ac", nc.tensor)
    lo = 0 if rev else 1
    U = 2 * DB
    Bb, Cb, dA, uB, hh, hC = sc.Bb, sc.Cb, sc.dA, sc.uB, sc.raw[:, :, 0:NSEQ * SEGS], sc.cv
    y = [sc.ps[b] for b in sc.ZB]

    def sync(e):
        with e.Fori(0, DS // 2 - 1) as j:
            for q in range(2):
                c.wait(e, s_hc, j * U + (q + 1) * DB)
                load_state(e, dram, sc, q, bass.ds(2 * j + (q + 2), 1), bass.ds(2 * j + (q + 2 + DS), 1))

    def gpsimd(e):
        c.wait(e, sc.pad, 4)
        with e.Fori(0, DS // 2) as j:
            for i in range(U):
                q, d = i // DB, i % DB
                if i < DB:
                    c.wait(e, sc.u_in, d + 1)
                if d == 0:
                    c.wait(e, s_bb[q], (j + 1) * 32)
                c.wait(e, s_sc, j * U + (i - 1))
                e.tensor_tensor(seq_view(uB[:, i % 2, :], SEGS, lo),
                                u[:, d, :].rearrange("p (b s) -> p b s", s=SEQ),
                                Bb[:, q, :].rearrange("p (b s) -> p b s", s=SEQ),
                                ALU.mult).then_inc(s_ub, 1)

    def scalar(e):
        c.wait(e, sc.pad, 4)
        c.wait(e, sc.A_in, 2)
        with e.Fori(0, DS // 2) as j:
            for i in range(U):
                q, d = i // DB, i % DB
                if i < DB:
                    c.wait(e, sc.dt_in, d + 1)
                c.wait(e, s_sc, j * U + (i - 1))
                e.activation(seq_view(dA[:, i % 2, :], SEGS, lo),
                             dt[:, d, :].rearrange("p (b s) -> p b s", s=SEQ), ACT.Exp,
                             scale=w.A[:, d, bass.ds(2 * j + q, 1)]).then_inc(s_da, 1)
        for d in range(1, DB):
            c.wait(e, *sc.z_out[d])
            e.activation(sz[:, d, :], sz[:, d, :], ACT.Silu).then_inc(s_si, 1)
        if w.after:
            c.wait(e, s_sc, DS * DB)
            split_high(e, w.after)

    def vector(e):
        with e.Fori(0, DS // 2) as j:
            for i in range(U):
                n, q, d, b = j * U + i, i // DB, i % DB, i % 2
                c.wait(e, s_da, n + 1)
                c.wait(e, s_ub, n + 1)
                c.wait(e, s_hc, j * U + (i - 1))
                way = slice(None, None, -1) if rev else slice(None)
                e.tensor_tensor_scan(hh[:, b, way], dA[:, b, way], uB[:, b, way], 0.0,
                                     ALU.mult, ALU.add).then_inc(s_sc, 1)
                if d == 0:
                    c.wait(e, s_bb[q], (j + 1) * 32)
                c.wait(e, s_sc, n + 1)
                c.wait(e, s_ac, j * U + (i - 1))
                e.tensor_tensor(hC[:, b, :].rearrange("p (b s) -> p b s", s=SEQ),
                                seq_view(hh[:, b, :], SEGS, lo),
                                Cb[:, q, :].rearrange("p (b s) -> p b s", s=SEQ),
                                ALU.mult).then_inc(s_hc, 1)
        for d in range(DB):
            c.wait(e, s_ac, (DS - 1) * DB + d + 1)
            c.wait(e, s_si, d)
            e.tensor_tensor(u[:, d, :], y[d][:, :], sz[:, d, :], ALU.mult).then_inc(s_y, 1)
        if w.after:
            split_low(e, w.after)
        for m in range(KC):
            c.wait(e, s_om, m + 1)
            e.tensor_tensor(acc[:, m, :], y[m][:, :], acc[:, m, :], ALU.add).then_inc(s_oa, 1)

    def tensor(e):
        for d in range(DB):
            c.wait(e, sc.dD_in, d + 1)
            c.wait(e, *sc.z_out[d])
            for h in range(NH):
                e.matmul(y[d][:, h * HALF:(h + 1) * HALF], sc.dD[:, d, :], xi[:, d, h * HALF:(h + 1) * HALF],
                         start=True, stop=False, skip_group_check=True)
        with e.Fori(0, DS // 2) as j:
            for i in range(U):
                n, d = j * U + i, i % DB
                c.wait(e, s_hc, n + 1)
                for h in range(NH):
                    mm = e.matmul(y[d][:, h * HALF:(h + 1) * HALF], g.ident[:, :],
                                  hC[:, i % 2, h * HALF:(h + 1) * HALF], start=False, stop=False,
                                  skip_group_check=True)
                mm.then_inc(s_ac, 1)
        for k in range(DB):
            c.wait(e, s_y, max(k + 1, KC))
            for m in range(KC):
                for h in range(NH):
                    mm = e.matmul(y[m][:, h * HALF:(h + 1) * HALF], w.out[:, k, m * P:(m + 1) * P],
                                  u[:, k, h * HALF:(h + 1) * HALF], start=k == 0, stop=k == DB - 1,
                                  skip_group_check=True)
                if k == DB - 1:
                    mm.then_inc(s_om, 1)

    return sync, gpsimd, scalar, vector, tensor


def to_tokens(c, g, name, feat, tok):
    nc = c.nc
    s_t, s_e = c.sem(name + "_t"), c.sem(name + "_e")
    with ExitStack() as ctx:
        ps = c.ps(ctx, name + "_ps", [P, NB, D])
        with nc.Block() as block:
            @block.tensor
            def _(e):
                for n in range(NB):
                    for k in range(KC):
                        mm = e.transpose(ps[:, n, k * P:(k + 1) * P], feat[:, k, n * P:(n + 1) * P], g.ident[:, :])
                    mm.then_inc(s_t, 1)

            @block.scalar
            def _(e):
                for q in range(2):
                    c.wait(e, s_t, 4 * (q + 1))
                    e.activation(tok[:, 4 * q:4 * q + 4, :], ps[:, 4 * q:4 * q + 4, :], ACT.Copy).then_inc(s_e, 1)


def mamba_output(c, g, wt, lh, ll):
    nc = c.nc
    s_mm, s_b, s_x, s_bn, s_lh, s_ll = map(c.sem, [f"mo_{n}" for n in "mm b x bn lh ll".split()])
    parts = [slice(q * LUTW // 4, (q + 1) * LUTW // 4) for q in range(4)]
    w, b = wt.w_out, wt.b_out
    with ExitStack() as ctx:
        ps = c.ps(ctx, "mo_ps", [P, NB, D])
        with nc.Block() as block:
            @block.tensor
            def _(e):
                for n in range(NB):
                    for k in range(KC):
                        mm = e.matmul(ps[:, n, :], g.feat[:, k, n * P:(n + 1) * P], w[:, k, :],
                                      start=k == 0, stop=k == KC - 1)
                    if n % 2:
                        mm.then_inc(s_mm, 1)

            @block.gpsimd
            def _(e):
                e.tensor_tensor(g.x[:, :, :], g.x[:, :, :], b[:, :].unsqueeze(1).broadcast_to([P, NB, D]),
                                ALU.add).then_inc(s_b, 1)

            @block.scalar
            def _(e):
                for p in parts:
                    e.activation(lh[:, p], g.lutw[:, p], ACT.Copy).then_inc(s_lh, 1)

            @block.vector
            def _(e):
                for i, p in enumerate(parts):
                    c.wait(e, s_lh, i + 1)
                    e.tensor_tensor(ll[:, p], g.lutw[:, p], lh[:, p].bitcast(F32), ALU.subtract).then_inc(s_ll, 1)
                c.wait(e, s_b, 1)
                for n in range(NB):
                    c.wait(e, s_mm, n // 2 + 1)
                    e.tensor_tensor(g.x[:, n, :], ps[:, n, :], g.x[:, n, :], ALU.add).then_inc(s_x, 1)
                    c.wait(e, s_x, n + 1)
                    e.bn_stats(g.stats[:, n, :], g.x[:, n, :]).then_inc(s_bn, 1)


def table_ffn(c, g, out, lh, ll, xh, xl):
    nc = c.nc
    s_g, s_u, s_si, s_a, s_ah, s_al, s_y, s_x, s_o = map(c.sem, [f"ff_{n}" for n in "g u si a ah al y x o".split()])
    M = len(FB)
    def views(w):
        return (w[:, 0:KC * FI].rearrange("p (k n) -> p k n", k=KC),
                w[:, KC * FI:2 * KC * FI].rearrange("p (k n) -> p k n", k=KC),
                w[:, 2 * KC * FI:LUTW].rearrange("p (m n) -> p m n", m=M))
    (gh, uh, dh), (gl, ul, dl) = views(lh), views(ll)
    with ExitStack() as ctx:
        si = c.sb(ctx, "ff_si", [P, 2, T])
        a = c.sb(ctx, "ff_a", [P, 2, T])
        ah = c.sb(ctx, "ff_ah", [P, M, T], F32R)
        al = c.sb(ctx, "ff_al", [P, M, T], F32R)
        ps = [c.ps(ctx, f"ff_p{i}", [P, T]) for i in range(4)]

        def low(e, m):
            r = FB[m][1]
            c.wait(e, s_ah, m + 1)
            e.tensor_tensor(al[0:r, m, :], a[0:r, m % 2, :], ah[0:r, m, :].bitcast(F32),
                            ALU.subtract).then_inc(s_al, 1)

        with nc.Block() as block:
            @block.tensor
            def _(e):
                for m, (o, r) in enumerate(FB):
                    for wh, wl, b, sem in ((gh, gl, 2 * (m % 2), s_g), (uh, ul, 2 * (m % 2) + 1, s_u)):
                        if m >= 2:
                            c.wait(e, s_a, m - 1)
                        for h in range(NH):
                            terms = [(w, x, k) for k in range(KC) for w, x in ((wh, xh), (wh, xl), (wl, xh))]
                            for i, (w, x, k) in enumerate(terms):
                                mm = e.matmul(ps[b][0:r, h * HALF:(h + 1) * HALF], w[:, k, o:o + r],
                                              x[:, k, h * HALF:(h + 1) * HALF], start=i == 0, stop=i == len(terms) - 1)
                        mm.then_inc(sem, 1)
                c.wait(e, s_a, M - 1)
                for odd in range(2):
                    for some in (range(M - 1), range(M - 1, M)):
                        for n in range(odd, NB, 2):
                            for m in some:
                                if n == 0:
                                    c.wait(e, s_al, m + 1)
                                r = FB[m][1]
                                for i, (x, w) in enumerate(((ah, dh), (ah, dl), (al, dh))):
                                    mm = e.matmul(ps[n // 4][:, (n % 4) * D:(n % 4 + 1) * D],
                                                  x[0:r, m, n * P:(n + 1) * P], w[0:r, m, :],
                                                  start=m + i == 0, stop=m == M - 1 and i == 2)
                            if odd and m == M - 1:
                                mm.then_inc(s_y, 1)

            @block.scalar
            def _(e):
                def high(m):
                    r = FB[m][1]
                    c.wait(e, s_a, m + 1)
                    e.activation(ah[0:r, m, :], a[0:r, m % 2, :], ACT.Copy).then_inc(s_ah, 1)

                for m, (o, r) in enumerate(FB):
                    c.wait(e, s_g, m + 1)
                    if m >= 2:
                        c.wait(e, s_a, m - 1)
                    e.activation(si[0:r, m % 2, :], ps[2 * (m % 2)][0:r, :], ACT.Silu).then_inc(s_si, 1)
                    if m:
                        high(m - 1)
                high(M - 1)

            @block.vector
            def _(e):
                for m, (o, r) in enumerate(FB):
                    c.wait(e, s_si, m + 1)
                    c.wait(e, s_u, m + 1)
                    if m >= 2:
                        c.wait(e, s_al, m - 1)
                    e.tensor_tensor(a[0:r, m % 2, :], ps[2 * (m % 2) + 1][0:r, :], si[0:r, m % 2, :],
                                    ALU.mult).then_inc(s_a, 1)
                    if m:
                        low(e, m - 1)
                low(e, M - 1)
                for n in range(NB):
                    c.wait(e, s_y, n // 2 + 1)
                    e.tensor_tensor(g.x[:, n, :], ps[n // 4][:, (n % 4) * D:(n % 4 + 1) * D], g.x[:, n, :],
                                    ALU.add).then_inc(s_x, 1)

            @block.sync
            def _(e):
                for n in range(NB):
                    c.wait(e, s_x, n + 1)
                    e.dma_start(out[n * P:(n + 1) * P, :], g.x[:, n, :]).then_inc(s_o, 16)
                c.wait(e, s_o, NB * 16)


class Shared:
    pass


def fetch(nc, s, pairs):
    for dst, src in pairs:
        nc.sync.dma_start(dst, src).then_inc(s, 16)
    return 16 * len(pairs)


def build(nc, dram, out):
    with ExitStack() as ctx:
        c = Core(nc, ctx)
        g = Shared()
        g.x = c.sb(ctx, "x", [P, NB, D])
        g.feat = c.sb(ctx, "feat", [P, KC, T])
        g.lutw = c.sb(ctx, "lutw", [P, MOE_K * LCH])
        g.ident = c.sb(ctx, "ident", [P, P])
        g.gmask = c.sb(ctx, "gmask", [P, 8])
        g.iota_e = c.sb(ctx, "iota_e", [P, NEXP])
        g.iota_l = c.sb(ctx, "iota_l", [P, LUT])
        g.lutb = c.sb(ctx, "lutb", [P, LUT])
        dram["cw"] = nc.dram_tensor("cw_rows", (NCW, T), F32, kind="Internal").ap()
        dram["bc"] = nc.dram_tensor("bc_rows", (2 * DS, T), F32, kind="Internal").ap()
        wt = Shared()
        chunks = lambda name: dram[name].rearrange("(k p) n -> p k n", p=P)
        wt.gate, wt.w_in, wt.w_out = (c.sb(ctx, n, [P, KC, w]) for n, w in
                                      (("gate", NEXP), ("w_in", D), ("w_out", D)))
        wt.b_in, wt.b_out = c.sb(ctx, "b_in", [P, KC]), c.sb(ctx, "b_out", [P, D])
        wt.ln = c.sb(ctx, "ln_gb", [P, 2, KC])
        s_x = [c.kept(f"x_in{q}") for q in range(NB // 2)]
        g.stats = c.sb(ctx, "x_stats", [P, NB, 6])
        wt.at_in, wt.late_in = c.kept("at_in"), c.kept("late_in")
        at = ctx.enter_context(ExitStack())
        wt.wq2, wt.wk2, wt.wv, wt.wout = (c.sb(at, n, [P, KC, w]) for n, w in (
            ("wq2", HJ * P), ("wk2", P), ("wv", KV), ("wout", D)))
        wt.bq2, wt.bk, wt.bv, wt.bout = (c.sb(at, n, [P, w]) for n, w in (
            ("bq2", HJ), ("bk", 1), ("bv", KV), ("bout", D)))
        for q in range(NB // 2):
            nc.sync.dma_start(g.x[:, 2 * q:2 * q + 2, :], dram["x"][2 * q * P:(2 * q + 2) * P, :]
                              .rearrange("(n p) d -> p n d", p=P)).then_inc(s_x[q], 16)

        def first_loads():
            wt.at_n = fetch(nc, wt.at_in, [
                (wt.wk2[:, :, :], chunks("wk2")), (wt.bk[:, :], dram["bk2"]), (wt.wq2[:, :, :], chunks("wq2")),
                (wt.bq2[:, :], dram["bq2"]), (wt.wv[:, :, :], chunks("wv")), (wt.wout[:, :, :], chunks("Wout")),
                (wt.bv[:, :], dram["bv"].broadcast_to([P, KV])), (wt.bout[:, :], dram["bout"].broadcast_to([P, D]))])

        def later_loads():
            wt.late_n = fetch(nc, wt.late_in, [
                (wt.gate[:, :, :], chunks("gate_wT")), (wt.w_in[:, :, :], chunks("w_inT")),
                (wt.b_in[:, :], dram["b_in"]), (wt.w_out[:, :, :], chunks("w_outT")),
                (wt.b_out[:, :], dram["b_out"].broadcast_to([P, D])), (wt.ln[:, 0, :], dram["ln_g"]),
                (wt.ln[:, 1, :], dram["ln_b"]), (g.lutb[:, :], dram["lut"].broadcast_to([P, LUT]))])

        constants(c, g)
        layernorm(c, g, "ln1", g.x, g.feat, loads=s_x, beside=first_loads)
        attention(c, g, wt, later_loads)
        at.close()
        with ExitStack() as moe:
            g.lut_f = c.sb(moe, "lut_f", [P, MOE_K * LCH])
            xh = c.sb(moe, "xh", [P, KC, T], F32R)
            xl = c.sb(moe, "xl", [P, KC, T], F32R)
            layernorm(c, g, "ln2", g.x, g.feat, hi=xh, lo=xl, stats=g.stats)
            with ExitStack() as idx:
                g.lut_i = c.sb(idx, "lut_i", [P, LUTW], I32)
                routing(c, g, dram, wt)
            experts(c, g, dram, xh, xl)
        c.recycle()
        with ExitStack() as mm:
            acc = c.sb(mm, "acc", [P, KC, T])
            wf, wb = Shared(), Shared()
            for w, dr in ((wf, "fm"), (wb, "bm")):
                w.A, w.Dv = c.sb(mm, dr + "_A", [P, DB, DS]), c.sb(mm, dr + "_Dv", [P, DB])
                w.out = c.sb(mm, dr + "_w_o", [P, DB, D])
                if w is wf:
                    w.win, wl_in = c.sb_twice(mm, "win", [P, KC, 2 * DI], "wl_in", [P, KC, 2 * DI])
                    w.xp = c.sb(mm, "wxp", [P, DB, DTR + 2 * DS])
                    w.dt, w.cvw = c.sb(mm, "wdt", [P, DI]), c.sb(mm, "cvw", [P, DB, DCONV])
                    w.cvb, w.dtb = c.sb(mm, "cvb", [P, DB]), c.sb(mm, "dtb", [P, DB])
                else:
                    w.win, w.xp, w.dt, w.cvw, w.cvb, w.dtb = wf.win, wf.xp, wf.dt, wf.cvw, wf.cvb, wf.dtb
            wf.after, wb.after = wb, None
            xi = c.sb(mm, "xi", [P, DB, T])
            sz = c.sb(mm, "sz", [P, DB, T])
            dt = c.sb(mm, "dt", [P, DB, T])
            u = c.sb(mm, "u", [P, DB, T])
            sc = Shared()
            sc.Bb, sc.Cb = (c.sb(mm, n, [P, 2, T]) for n in ("Bb", "Cb"))
            sc.uB = c.sb(mm, "uB", [P, 2, NSEQ * SEGS])
            sc.dA, sc.wh = c.sb_twice(mm, "dA", [P, 2, NSEQ * SEGS], "wh_in", [P, KC, 2 * DI])
            sc.wl = wl_in
            sc.raw, sc.cv = c.sb(mm, "raw", [P, 2, NSEQ * SEGC]), c.sb(mm, "cv", [P, 2, T])
            sc.dtr, sc.bcr = c.sb(mm, "dtr", [P, T]), c.sb(mm, "bcr", [2 * DS, T])
            sc.dD = c.sb(mm, "dD", [P, DB, P])
            layernorm(c, g, "ln3", g.x, g.feat, beside=lambda: mamba_weights(c, dram, "fm", wf))
            with ExitStack() as banks:
                hh, hl = (c.sb(banks, n, [P, KC, T], F32R) for n in ("hh", "hl"))
                mamba_input(c, g, wt, acc, hh, hl, wf, sc)
                sc.ps = [c.ps(banks, f"m_ps{i}", [P, T]) for i in range(4)]
                for dr, rev, w in (("fm", False, wf), ("bm", True, wb)):
                    mamba_direction(c, g, dram, dr, rev, hh, hl, w, xi, sz, dt, u, acc, sc)
                    c.recycle()
            rt = c.sb(mm, "r_tok", [P, NB, D])
            to_tokens(c, g, "rt_tok", acc, rt)
            layernorm(c, g, "lnm", rt, g.feat, gamma=wt.ln[:, 0, :], beta=wt.ln[:, 1, :])
        with ExitStack() as ffn:
            lh, ll = (c.sb(ffn, n, [P, LUTW], F32R) for n in ("lut_h", "lut_l"))
            xh, xl = (c.sb(ffn, n, [P, KC, T], F32R) for n in ("ff_xh", "ff_xl"))
            mamba_output(c, g, wt, lh, ll)
            layernorm(c, g, "ln4", g.x, hi=xh, lo=xl, stats=g.stats)
            table_ffn(c, g, out, lh, ll, xh, xl)


def kernel(**inputs):
    import numpy as np
    import concourse.bacc as bacc
    from concourse.bass_utils import run_bass_kernel_spmd

    f = {k: np.asarray(v) for k, v in inputs.items()}

    def columns(v):
        return v.reshape(-1, P).T

    def by_hidden(gate, up, down, count):
        rows = count * P
        flat = [w.transpose(1, 0, 2).reshape(KC, P, count, P).transpose(2, 1, 0, 3).reshape(count, P, KC * P)
                for w in (gate, up)]
        return np.concatenate(flat + [down.reshape(rows, D).reshape(count, P, D)], axis=2)

    large = by_hidden(f["L0_ffn_Wg"], f["L0_ffn_Wu"], f["L0_ffn_Wd"], EB).reshape(MOE_IT, 3, P, MOE_WN)
    small = by_hidden(f["L0_ffn_cWg"], f["L0_ffn_cWu"], f["L0_ffn_cWd"], NCH).reshape(MOE_IT, 2, P, MOE_WN)
    moe = np.concatenate([large, small], axis=1).reshape(MOE_IT * MOE_K, P, MOE_WN)
    moe = np.concatenate([moe, moe[:1]], axis=0)

    def twice(w):
        return np.repeat(w.reshape(len(w), -1, 1, KV), 2, axis=2).reshape(len(w), -1)

    wqkv, bqkv = f["L0_attn_Wqkv"], f["L0_attn_bqkv"].reshape(1, -1)

    def table_rows(idx):
        return idx.T.reshape(KC, P, FI).transpose(1, 0, 2).reshape(P, KC * FI)

    down = np.zeros((len(FB) * P, D), f["L1_ffn_down_idx"].dtype)
    down[:FI] = f["L1_ffn_down_idx"].T
    down = down.reshape(len(FB), P, D).transpose(1, 0, 2).reshape(P, len(FB) * D)
    arrays = {
        "x": f["L0_attn_x"].reshape(T, D), "wq2": twice(wqkv[:, :D]), "wk2": twice(wqkv[:, D:D + KV]),
        "wv": wqkv[:, D + KV:], "bq2": columns(twice(bqkv[:, :D]).ravel()), "bk2": columns(twice(bqkv[:, D:D + KV]).ravel()),
        "bv": bqkv[:, D + KV:],
        "Wout": f["L0_attn_Wout"], "bout": f["L0_attn_bout"].reshape(1, D), "gate_wT": f["L0_ffn_gate_w"].T,
        "moe_w": moe, "lut": f["L1_ffn_lut"].reshape(1, LUT),
        "lut_idx": np.concatenate([table_rows(f["L1_ffn_gate_idx"]), table_rows(f["L1_ffn_up_idx"]), down], axis=1),
        "w_inT": f["L1_attn_w_in"].T, "b_in": columns(f["L1_attn_b_in"]),
        "ln_g": columns(f["L1_attn_ln_g"]), "ln_b": columns(f["L1_attn_ln_b"]),
        "w_outT": f["L1_attn_w_out"].T, "b_out": f["L1_attn_b_out"].reshape(1, D),
    }
    for dr in ("fm", "bm"):
        n = f"L1_attn_{dr}_"
        arrays |= {
            dr + "_in_wT": f[n + "in_w"].T, dr + "_xproj_wT": f[n + "xproj_w"].T, dr + "_dt_wT": f[n + "dt_w"].T,
            dr + "_conv_w": f[n + "conv_w"], dr + "_conv_b": columns(f[n + "conv_b"]),
            dr + "_dt_b": columns(f[n + "dt_b"]), dr + "_A_log": f[n + "A_log"], dr + "_D": columns(f[n + "D"]),
            dr + "_out_wT": f[n + "out_w"].T,
        }
    nc = bacc.Bacc("TRN2", target_bir_lowering=False, num_devices=1)
    arrays = {f"in_{k}": np.ascontiguousarray(v) for k, v in arrays.items()}
    dram = {k[3:]: nc.dram_tensor(k, v.shape, mybir.dt.from_np(v.dtype), kind="ExternalInput").ap()
            for k, v in arrays.items()}
    out = nc.dram_tensor("out", (T, D), F32, kind="ExternalOutput").ap()
    build(nc, dram, out)
    r = run_bass_kernel_spmd(nc, [arrays], core_ids=[0])
    return r.results[0]["out"].reshape(NSEQ, SEQ, D)
```
